# Optimizing a Trainium2 kernel written in Bass

```python
import numpy as np
import jax
import jax.numpy as jnp

def _softmax(x, axis=-1):
    return jax.nn.softmax(x, axis=axis)

def _gelu(x):
    return jax.nn.gelu(x, approximate=True)

def _silu(x):
    return jax.nn.silu(x)

def _sigmoid(x):
    return jax.nn.sigmoid(x)

def _layernorm(x, axis=-1, eps=1e-05):
    m = jnp.mean(x, axis=axis, keepdims=True)
    v = jnp.var(x, axis=axis, keepdims=True)
    return (x - m) / jnp.sqrt(v + eps)

def _scatter_add(tgt, idx, src, axis=0):
    return tgt.at[idx].add(src)

def _segment_sum(src, seg, n):
    return jax.ops.segment_sum(src, seg, n)
kernel_name = 'mk_prb_d4_jaxref_r4_e621ed'

def setup_inputs(seed: int=0):
    np.random.seed(seed)
    _w = jnp.asarray

    def _L0_attn_setup():
        import jax, jax.numpy as jnp
        import numpy as np
        import math
        B, S, D = (4, 512, 256)
        H = 16
        HD = D // H
        DL = 64
        LAMBDA_DECAY = 0.01
        key = jax.random.key(seed)
        ks = jax.random.split(key, 8)
        sc = lambda fan_in: 1.0 / math.sqrt(fan_in)
        return {'x': jax.random.normal(ks[0], (B, S, D), dtype=jnp.float32), 'W_q': jax.random.normal(ks[1], (D, D), dtype=jnp.float32) * sc(D), 'W_k': jax.random.normal(ks[2], (D, D), dtype=jnp.float32) * sc(D), 'W_v': jax.random.normal(ks[3], (D, D), dtype=jnp.float32) * sc(D), 'W_o': jax.random.normal(ks[4], (D, D), dtype=jnp.float32) * sc(D), 'W_down_kv': jax.random.normal(ks[5], (D, DL), dtype=jnp.float32) * sc(D), 'W_up_k': jax.random.normal(ks[6], (DL, D), dtype=jnp.float32) * sc(DL), 'W_up_v': jax.random.normal(ks[7], (DL, D), dtype=jnp.float32) * sc(DL)}
    _L0_attn_in = _L0_attn_setup()

    def _L0_ffn_setup():
        import jax, jax.numpy as jnp
        import numpy as np
        B, T, C = (2, 512, 256)
        H, D = (16, 64)
        CR = 8
        R = C // CR
        ROPE = D // 2
        NOPE = D - ROPE
        E, K, I, S = (8, 2, 128, 1)
        THETA = 100000.0
        EPS = 1e-05

        def _rmsnorm(x, w):
            rms = jnp.sqrt(jnp.mean(x * x, axis=-1, keepdims=True) + EPS)
            return w * (x / rms)

        def _rope(xh):
            d = xh.shape[-1]
            t = jnp.arange(xh.shape[2], dtype=jnp.float32)
            freqs = 1.0 / THETA ** (jnp.arange(0, d, 2, dtype=jnp.float32) / d)
            ang = jnp.outer(t, freqs)
            cos, sin = (jnp.cos(ang), jnp.sin(ang))
            xr = xh.reshape(xh.shape[:-1] + (d // 2, 2))
            x0, x1 = (xr[..., 0], xr[..., 1])
            rot = jnp.stack([x0 * cos - x1 * sin, x0 * sin + x1 * cos], axis=-1)
            return rot.reshape(xh.shape)

        def _attention(x, Wq, Wkva, Wkvb, Wo):
            b, t, _ = x.shape
            q = (x @ Wq).reshape(b, t, H, D).transpose(0, 2, 1, 3)
            ckv = x @ Wkva
            kv_latent, k_rope = (ckv[:, :, :R], ckv[:, :, R:])
            kv = (kv_latent @ Wkvb).reshape(b, t, H, NOPE).transpose(0, 2, 1, 3)
            k_rope = jnp.broadcast_to(k_rope[:, None, :, :], (b, H, t, ROPE))
            q_nope, q_rope = (q[..., :NOPE], q[..., NOPE:])
            q = jnp.concatenate([q_nope, _rope(q_rope)], axis=-1)
            k = jnp.concatenate([kv, _rope(k_rope)], axis=-1)
            v = jnp.concatenate([kv, jnp.zeros_like(k_rope)], axis=-1)
            att = jnp.einsum('bhqd,bhkd->bhqk', q, k) / jnp.sqrt(jnp.float32(D))
            mask = jnp.tril(jnp.ones((t, t), dtype=bool))
            att = jnp.where(mask, att, jnp.float32(-jnp.inf))
            att = jax.nn.softmax(att, axis=-1)
            y = jnp.einsum('bhqk,bhkd->bhqd', att, v)
            y = y.transpose(0, 2, 1, 3).reshape(b, t, H * D)
            return y @ Wo

        def _experts(x_flat, Wg, Wu, Wd):
            g = jax.nn.silu(jnp.einsum('nc,eci->nei', x_flat, Wg))
            u = jnp.einsum('nc,eci->nei', x_flat, Wu)
            return jnp.einsum('nei,eic->nec', g * u, Wd)

        def _moe(x, Wgate, expert_bias, Wg, Wu, Wd, sWg, sWu, sWd):
            b, t, c = x.shape
            xf = x.reshape(-1, c)
            shared = jnp.mean(_experts(xf, sWg, sWu, sWd), axis=1)
            logits = xf @ Wgate + expert_bias
            probs = jax.nn.softmax(logits, axis=-1)
            topk_p, topk_i = jax.lax.top_k(probs, K)
            topk_p = topk_p / jnp.sum(topk_p, axis=-1, keepdims=True)
            comb = jnp.sum(jax.nn.one_hot(topk_i, E, dtype=xf.dtype) * topk_p[..., None], axis=1)
            routed = jnp.einsum('ne,nec->nc', comb, _experts(xf, Wg, Wu, Wd))
            return (shared + routed).reshape(b, t, c)
        key = jax.random.key(seed)
        ks = jax.random.split(key, 16)
        w = lambda k, shp: jax.random.normal(k, shp, dtype=jnp.float32) * 0.02
        return {'x': jax.random.normal(ks[0], (B, T, C), dtype=jnp.float32), 'w_ln1': jnp.ones((C,), jnp.float32), 'Wq': w(ks[1], (C, H * D)), 'Wkva': w(ks[2], (C, R + ROPE)), 'Wkvb': w(ks[3], (R, H * NOPE)), 'Wo': w(ks[4], (H * D, C)), 'w_ln2': jnp.ones((C,), jnp.float32), 'Wgate': w(ks[5], (C, E)), 'expert_bias': jnp.zeros((E,), jnp.float32), 'Wg': w(ks[6], (E, C, I)), 'Wu': w(ks[7], (E, C, I)), 'Wd': w(ks[8], (E, I, C)), 'sWg': w(ks[9], (S, C, I)), 'sWu': w(ks[10], (S, C, I)), 'sWd': w(ks[11], (S, I, C))}
    _L0_ffn_in = _L0_ffn_setup()

    def _L1_attn_setup():
        import jax, jax.numpy as jnp
        import numpy as np
        from jax import lax
        NL, D, ED, N, K, R = (2, 256, 512, 16, 4, 64)
        B, L = (2, 256)
        EPS = 1e-05

        def _rmsnorm(x, w):
            return x * jax.lax.rsqrt(jnp.mean(x * x, axis=-1, keepdims=True) + EPS) * w

        def _depthwise_causal_conv(x, w, b):
            y = lax.conv_general_dilated(x, w, window_strides=(1,), padding=[(K - 1, 0)], dimension_numbers=('NCH', 'OIH', 'NCH'), feature_group_count=ED)
            return y + b[None, :, None]

        def _selective_scan(deltaA, deltaBx, C):

            def step(h, inp):
                dA, dBx, c = inp
                h = dA * h + dBx
                y = jnp.einsum('ben,bn->be', h, c)
                return (h, y)
            h0 = jnp.zeros((deltaA.shape[0], ED, N), dtype=deltaA.dtype)
            _, ys = lax.scan(step, h0, (jnp.moveaxis(deltaA, 1, 0), jnp.moveaxis(deltaBx, 1, 0), jnp.moveaxis(C, 1, 0)))
            return jnp.moveaxis(ys, 0, 1)

        def _mamba_block(xn, p):
            in_w, cw, cb, xp_w, dtw, dtb, A_log, Dp, out_w = p
            xz = jnp.einsum('bld,ed->ble', xn, in_w)
            xi, z = jnp.split(xz, 2, axis=-1)
            xc = _depthwise_causal_conv(jnp.swapaxes(xi, 1, 2), cw, cb)
            u = jax.nn.silu(jnp.swapaxes(xc, 1, 2))
            dbc = jnp.einsum('ble,re->blr', u, xp_w)
            d_r, Bm, Cm = jnp.split(dbc, [R, R + N], axis=-1)
            delta = jax.nn.softplus(jnp.einsum('blr,er->ble', d_r, dtw) + dtb)
            A = -jnp.exp(A_log)
            deltaA = jnp.exp(delta[..., None] * A)
            deltaBx = delta[..., None] * Bm[:, :, None, :] * u[..., None]
            y = _selective_scan(deltaA, deltaBx, Cm)
            y = y + Dp * u
            y = y * jax.nn.silu(z)
            return jnp.einsum('ble,de->bld', y, out_w)
        key = jax.random.key(seed)
        ks = jax.random.split(key, 12)
        dt_init_std = R ** (-0.5)
        dt = jnp.exp(jax.random.uniform(ks[6], (NL, ED)) * (np.log(0.1) - np.log(0.001)) + np.log(0.001))
        dt = jnp.clip(dt, 0.0001, None)
        inv_dt = dt + jnp.log(-jnp.expm1(-dt))
        A = jnp.tile(jnp.arange(1, N + 1, dtype=jnp.float32), (NL, ED, 1))
        return {'x': jax.random.normal(ks[0], (B, L, D), dtype=jnp.float32), 'in_proj_w': jax.random.normal(ks[1], (NL, 2 * ED, D), dtype=jnp.float32) * 0.02, 'conv_w': jax.random.normal(ks[2], (NL, ED, 1, K), dtype=jnp.float32) * 0.2, 'conv_b': jax.random.normal(ks[3], (NL, ED), dtype=jnp.float32) * 0.02, 'x_proj_w': jax.random.normal(ks[4], (NL, R + 2 * N, ED), dtype=jnp.float32) * 0.02, 'dt_w': jax.random.uniform(ks[5], (NL, ED, R), minval=-dt_init_std, maxval=dt_init_std, dtype=jnp.float32), 'dt_b': inv_dt, 'A_log': jnp.log(A), 'D_p': jnp.ones((NL, ED), dtype=jnp.float32), 'out_proj_w': jax.random.normal(ks[7], (NL, D, ED), dtype=jnp.float32) * 0.02, 'norm_w': jnp.ones((NL, D), dtype=jnp.float32)}
    _L1_attn_in = _L1_attn_setup()

    def _L1_ffn_setup():
        import jax, jax.numpy as jnp
        import numpy as np
        B, T, D, E, H = (4, 512, 256, 4, 8)
        EPS = 1e-05

        def _uniform(k, shape, bound):
            return jax.random.uniform(k, shape, jnp.float32, -bound, bound)

        def _layernorm(x, w, b):
            mu = jnp.mean(x, axis=-1, keepdims=True)
            var = jnp.mean(jnp.square(x - mu), axis=-1, keepdims=True)
            return (x - mu) * jax.lax.rsqrt(var + EPS) * w + b
        key = jax.random.key(seed)
        ks = jax.random.split(key, 12)
        wb = np.sqrt(6.0 / D) / np.sqrt(6.0)
        wb = 1.0 / np.sqrt(D)
        return {'x': jax.random.normal(ks[0], (B, T, D), jnp.float32), 'router_prob': jax.random.uniform(ks[1], (B, T, E), jnp.float32), 'norm_w': jnp.ones((D,), jnp.float32), 'norm_b': jnp.zeros((D,), jnp.float32), 'q_w': _uniform(ks[2], (D, D), wb), 'q_b': _uniform(ks[3], (D,), wb), 'k_w': _uniform(ks[4], (D, D), wb), 'k_b': _uniform(ks[5], (D,), wb), 'v_w': _uniform(ks[6], (D, D), wb), 'v_b': _uniform(ks[7], (D,), wb), 'o_w': _uniform(ks[8], (D, D), wb), 'o_b': _uniform(ks[9], (D,), wb)}
    _L1_ffn_in = _L1_ffn_setup()

    def _L2_attn_setup():
        import math
        import jax, jax.numpy as jnp
        import numpy as np
        B, T, C, H = (1, 1024, 256, 16)
        HD = C // H

        def get_slopes(n):

            def pow2(n):
                start = 2 ** (-2 ** (-(math.log2(n) - 3)))
                return [start * start ** i for i in range(n)]
            if math.log2(n).is_integer():
                return pow2(n)
            cp2 = 2 ** math.floor(math.log2(n))
            return pow2(cp2) + get_slopes(2 * cp2)[0::2][:n - cp2]
        key = jax.random.key(seed)
        ks = jax.random.split(key, 5)
        x = jax.random.normal(ks[0], (B, T, C), dtype=jnp.float32)
        mk = lambda k: 0.02 * jax.random.normal(k, (C, C), dtype=jnp.float32)
        return {'x': x, 'Wq': mk(ks[1]), 'bq': jnp.zeros((C,), jnp.float32), 'Wk': mk(ks[2]), 'bk': jnp.zeros((C,), jnp.float32), 'Wv': mk(ks[3]), 'bv': jnp.zeros((C,), jnp.float32), 'Wo': 0.02 / math.sqrt(24) * jax.random.normal(ks[4], (C, C), dtype=jnp.float32), 'bo': jnp.zeros((C,), jnp.float32)}
    _L2_attn_in = _L2_attn_setup()

    def _L2_ffn_setup():
        import jax, jax.numpy as jnp
        import numpy as np
        E = 16
        G = 4
        EPG = E // G
        K = 4
        TOPK_GROUP = 2
        PER_GROUP_K = K // TOPK_GROUP

        def _route(xf, router_w, correction_bias):
            S = xf.shape[0]
            logits = xf @ router_w.T
            scores = jax.nn.sigmoid(logits)
            sb = scores + correction_bias
            grp_top = jax.lax.top_k(sb.reshape(S, G, EPG), PER_GROUP_K)[0]
            group_scores = grp_top.sum(axis=-1)
            _, group_idx = jax.lax.top_k(group_scores, TOPK_GROUP)
            group_mask = jnp.zeros((S, G), sb.dtype).at[jnp.arange(S)[:, None], group_idx].set(1.0)
            score_mask = jnp.broadcast_to(group_mask[:, :, None], (S, G, EPG)).reshape(S, E)
            masked = jnp.where(score_mask > 0, sb, -jnp.inf)
            _, topk_idx = jax.lax.top_k(masked, K)
            w = jnp.take_along_axis(scores, topk_idx, axis=1)
            w = w / (w.sum(axis=-1, keepdims=True) + 1e-20)
            return (topk_idx, w, scores)
        key = jax.random.key(seed)
        ks = jax.random.split(key, 9)
        B, T, C, H, HS = (2, 256, 256, 64, 512)
        std = 0.02
        return {'x': jax.random.normal(ks[0], (B, T, C), jnp.float32), 'router_w': jax.random.normal(ks[1], (E, C), jnp.float32) * std, 'correction_bias': jnp.zeros((E,), jnp.float32), 'gate_w': jax.random.normal(ks[2], (E, C, H), jnp.float32) * std, 'up_w': jax.random.normal(ks[3], (E, C, H), jnp.float32) * std, 'down_w': jax.random.normal(ks[4], (E, H, C), jnp.float32) * std, 'shared_gate_w': jax.random.normal(ks[5], (HS, C), jnp.float32) * std, 'shared_up_w': jax.random.normal(ks[6], (HS, C), jnp.float32) * std, 'shared_down_w': jax.random.normal(ks[7], (C, HS), jnp.float32) * std}
    _L2_ffn_in = _L2_ffn_setup()

    def _L3_attn_setup():
        import jax, jax.numpy as jnp
        import numpy as np
        B, N, D, NH, MAXLEN = (2, 512, 256, 16, 512)
        HD = D // NH

        def srel_skew(x):
            b, h, n, _ = x.shape
            v = jnp.pad(x, ((0, 0), (0, 0), (0, 0), (1, 0)))
            return v.reshape(b, h, n + 1, n)[:, :, :n, :]

        def split_head(x):
            b, n, _ = x.shape
            return x.reshape(b, n, NH, HD).transpose(0, 2, 1, 3)
        key = jax.random.key(seed)
        ks = jax.random.split(key, 7)
        scale = 0.02
        return {'x': jax.random.normal(ks[0], (B, N, D), dtype=jnp.float32), 'Wq': jax.random.normal(ks[1], (D, D), dtype=jnp.float32) * scale, 'Wk': jax.random.normal(ks[2], (D, D), dtype=jnp.float32) * scale, 'Wv': jax.random.normal(ks[3], (D, D), dtype=jnp.float32) * scale, 'Wp': jax.random.normal(ks[4], (D, D), dtype=jnp.float32) * scale, 'bp': jnp.zeros((D,), dtype=jnp.float32), 'rel_embed': jax.random.normal(ks[5], (MAXLEN, D), dtype=jnp.float32) * scale}
    _L3_attn_in = _L3_attn_setup()

    def _L3_ffn_setup():
        import jax, jax.numpy as jnp
        import numpy as np
        B, S, H, E = (8, 1024, 256, 8)
        TEMPERATURE = 1.0
        key = jax.random.key(seed)
        ks = jax.random.split(key, 7)
        s_h = 1.0 / np.sqrt(H).astype(np.float32)
        s_h2 = 1.0 / np.sqrt(H // 2).astype(np.float32)
        return {'hidden_states': jax.random.normal(ks[0], (B, S, H), jnp.float32), 'W1': jax.random.normal(ks[1], (H, H // 2), jnp.float32) * s_h, 'b1': jnp.zeros((H // 2,), jnp.float32), 'W2': jax.random.normal(ks[2], (H // 2, E), jnp.float32) * s_h2, 'b2': jnp.zeros((E,), jnp.float32), 'expert_W': jax.random.normal(ks[3], (E, H, H), jnp.float32) * s_h, 'expert_b': jax.random.normal(ks[4], (E, H), jnp.float32)}
    _L3_ffn_in = _L3_ffn_setup()
    _d = {'L0_attn_x': _L0_attn_in['x'], 'L0_attn_W_q': _L0_attn_in['W_q'], 'L0_attn_W_k': _L0_attn_in['W_k'], 'L0_attn_W_v': _L0_attn_in['W_v'], 'L0_attn_W_o': _L0_attn_in['W_o'], 'L0_attn_W_down_kv': _L0_attn_in['W_down_kv'], 'L0_attn_W_up_k': _L0_attn_in['W_up_k'], 'L0_attn_W_up_v': _L0_attn_in['W_up_v'], 'L0_ffn_w_ln1': _L0_ffn_in['w_ln1'], 'L0_ffn_Wq': _L0_ffn_in['Wq'], 'L0_ffn_Wkva': _L0_ffn_in['Wkva'], 'L0_ffn_Wkvb': _L0_ffn_in['Wkvb'], 'L0_ffn_Wo': _L0_ffn_in['Wo'], 'L0_ffn_w_ln2': _L0_ffn_in['w_ln2'], 'L0_ffn_Wgate': _L0_ffn_in['Wgate'], 'L0_ffn_expert_bias': _L0_ffn_in['expert_bias'], 'L0_ffn_Wg': _L0_ffn_in['Wg'], 'L0_ffn_Wu': _L0_ffn_in['Wu'], 'L0_ffn_Wd': _L0_ffn_in['Wd'], 'L0_ffn_sWg': _L0_ffn_in['sWg'], 'L0_ffn_sWu': _L0_ffn_in['sWu'], 'L0_ffn_sWd': _L0_ffn_in['sWd'], 'L1_attn_in_proj_w': _L1_attn_in['in_proj_w'], 'L1_attn_conv_w': _L1_attn_in['conv_w'], 'L1_attn_conv_b': _L1_attn_in['conv_b'], 'L1_attn_x_proj_w': _L1_attn_in['x_proj_w'], 'L1_attn_dt_w': _L1_attn_in['dt_w'], 'L1_attn_dt_b': _L1_attn_in['dt_b'], 'L1_attn_A_log': _L1_attn_in['A_log'], 'L1_attn_D_p': _L1_attn_in['D_p'], 'L1_attn_out_proj_w': _L1_attn_in['out_proj_w'], 'L1_attn_norm_w': _L1_attn_in['norm_w'], 'L1_ffn_router_prob': _L1_ffn_in['router_prob'], 'L1_ffn_norm_w': _L1_ffn_in['norm_w'], 'L1_ffn_norm_b': _L1_ffn_in['norm_b'], 'L1_ffn_q_w': _L1_ffn_in['q_w'], 'L1_ffn_q_b': _L1_ffn_in['q_b'], 'L1_ffn_k_w': _L1_ffn_in['k_w'], 'L1_ffn_k_b': _L1_ffn_in['k_b'], 'L1_ffn_v_w': _L1_ffn_in['v_w'], 'L1_ffn_v_b': _L1_ffn_in['v_b'], 'L1_ffn_o_w': _L1_ffn_in['o_w'], 'L1_ffn_o_b': _L1_ffn_in['o_b'], 'L2_attn_Wq': _L2_attn_in['Wq'], 'L2_attn_bq': _L2_attn_in['bq'], 'L2_attn_Wk': _L2_attn_in['Wk'], 'L2_attn_bk': _L2_attn_in['bk'], 'L2_attn_Wv': _L2_attn_in['Wv'], 'L2_attn_bv': _L2_attn_in['bv'], 'L2_attn_Wo': _L2_attn_in['Wo'], 'L2_attn_bo': _L2_attn_in['bo'], 'L2_ffn_router_w': _L2_ffn_in['router_w'], 'L2_ffn_correction_bias': _L2_ffn_in['correction_bias'], 'L2_ffn_gate_w': _L2_ffn_in['gate_w'], 'L2_ffn_up_w': _L2_ffn_in['up_w'], 'L2_ffn_down_w': _L2_ffn_in['down_w'], 'L2_ffn_shared_gate_w': _L2_ffn_in['shared_gate_w'], 'L2_ffn_shared_up_w': _L2_ffn_in['shared_up_w'], 'L2_ffn_shared_down_w': _L2_ffn_in['shared_down_w'], 'L3_attn_Wq': _L3_attn_in['Wq'], 'L3_attn_Wk': _L3_attn_in['Wk'], 'L3_attn_Wv': _L3_attn_in['Wv'], 'L3_attn_Wp': _L3_attn_in['Wp'], 'L3_attn_bp': _L3_attn_in['bp'], 'L3_attn_rel_embed': _L3_attn_in['rel_embed'], 'L3_ffn_W1': _L3_ffn_in['W1'], 'L3_ffn_b1': _L3_ffn_in['b1'], 'L3_ffn_W2': _L3_ffn_in['W2'], 'L3_ffn_b2': _L3_ffn_in['b2'], 'L3_ffn_expert_W': _L3_ffn_in['expert_W'], 'L3_ffn_expert_b': _L3_ffn_in['expert_b']}
    _x0 = _d['L0_attn_x']
    _d['L0_attn_x'] = jax.random.normal(jax.random.fold_in(jax.random.key(seed), 1), (8, 512, 256), dtype=_x0.dtype)
    del _x0
    return _d

def reference(L0_attn_x, L0_attn_W_q, L0_attn_W_k, L0_attn_W_v, L0_attn_W_o, L0_attn_W_down_kv, L0_attn_W_up_k, L0_attn_W_up_v, L0_ffn_w_ln1, L0_ffn_Wq, L0_ffn_Wkva, L0_ffn_Wkvb, L0_ffn_Wo, L0_ffn_w_ln2, L0_ffn_Wgate, L0_ffn_expert_bias, L0_ffn_Wg, L0_ffn_Wu, L0_ffn_Wd, L0_ffn_sWg, L0_ffn_sWu, L0_ffn_sWd, L1_attn_in_proj_w, L1_attn_conv_w, L1_attn_conv_b, L1_attn_x_proj_w, L1_attn_dt_w, L1_attn_dt_b, L1_attn_A_log, L1_attn_D_p, L1_attn_out_proj_w, L1_attn_norm_w, L1_ffn_router_prob, L1_ffn_norm_w, L1_ffn_norm_b, L1_ffn_q_w, L1_ffn_q_b, L1_ffn_k_w, L1_ffn_k_b, L1_ffn_v_w, L1_ffn_v_b, L1_ffn_o_w, L1_ffn_o_b, L2_attn_Wq, L2_attn_bq, L2_attn_Wk, L2_attn_bk, L2_attn_Wv, L2_attn_bv, L2_attn_Wo, L2_attn_bo, L2_ffn_router_w, L2_ffn_correction_bias, L2_ffn_gate_w, L2_ffn_up_w, L2_ffn_down_w, L2_ffn_shared_gate_w, L2_ffn_shared_up_w, L2_ffn_shared_down_w, L3_attn_Wq, L3_attn_Wk, L3_attn_Wv, L3_attn_Wp, L3_attn_bp, L3_attn_rel_embed, L3_ffn_W1, L3_ffn_b1, L3_ffn_W2, L3_ffn_b2, L3_ffn_expert_W, L3_ffn_expert_b):

    def _L0_attn_ref(x, W_q, W_k, W_v, W_o, W_down_kv, W_up_k, W_up_v):
        import jax, jax.numpy as jnp
        import numpy as np
        import math
        B, S, D = (4, 512, 256)
        H = 16
        HD = D // H
        DL = 64
        LAMBDA_DECAY = 0.01
        b, s, d = x.shape
        q = x @ W_q
        k = x @ W_k
        v = x @ W_v
        latent_kv = (k + v) @ W_down_kv
        k_rec = (latent_kv @ W_up_k).reshape(b, s, H, HD).transpose(0, 2, 1, 3)
        v_rec = (latent_kv @ W_up_v).reshape(b, s, H, HD).transpose(0, 2, 1, 3)
        qh = q.reshape(b, s, H, HD).transpose(0, 2, 1, 3)
        scores = jnp.einsum('bhqd,bhkd->bhqk', qh, k_rec) / math.sqrt(d)
        t = jnp.arange(s, dtype=jnp.float32)
        decay = jnp.exp(-LAMBDA_DECAY * jnp.abs(t[:, None] - t[None, :]))
        scores = scores * decay[None, None, :, :]
        attn = jax.nn.softmax(scores, axis=-1)
        out = jnp.einsum('bhqk,bhkd->bhqd', attn, v_rec)
        out = out.transpose(0, 2, 1, 3).reshape(b, s, d)
        return out @ W_o

    def _L0_ffn_ref(x, w_ln1, Wq, Wkva, Wkvb, Wo, w_ln2, Wgate, expert_bias, Wg, Wu, Wd, sWg, sWu, sWd):
        import jax, jax.numpy as jnp
        import numpy as np
        B, T, C = (2, 512, 256)
        H, D = (16, 64)
        CR = 8
        R = C // CR
        ROPE = D // 2
        NOPE = D - ROPE
        E, K, I, S = (8, 2, 128, 1)
        THETA = 100000.0
        EPS = 1e-05

        def _rmsnorm(x, w):
            rms = jnp.sqrt(jnp.mean(x * x, axis=-1, keepdims=True) + EPS)
            return w * (x / rms)

        def _rope(xh):
            d = xh.shape[-1]
            t = jnp.arange(xh.shape[2], dtype=jnp.float32)
            freqs = 1.0 / THETA ** (jnp.arange(0, d, 2, dtype=jnp.float32) / d)
            ang = jnp.outer(t, freqs)
            cos, sin = (jnp.cos(ang), jnp.sin(ang))
            xr = xh.reshape(xh.shape[:-1] + (d // 2, 2))
            x0, x1 = (xr[..., 0], xr[..., 1])
            rot = jnp.stack([x0 * cos - x1 * sin, x0 * sin + x1 * cos], axis=-1)
            return rot.reshape(xh.shape)

        def _attention(x, Wq, Wkva, Wkvb, Wo):
            b, t, _ = x.shape
            q = (x @ Wq).reshape(b, t, H, D).transpose(0, 2, 1, 3)
            ckv = x @ Wkva
            kv_latent, k_rope = (ckv[:, :, :R], ckv[:, :, R:])
            kv = (kv_latent @ Wkvb).reshape(b, t, H, NOPE).transpose(0, 2, 1, 3)
            k_rope = jnp.broadcast_to(k_rope[:, None, :, :], (b, H, t, ROPE))
            q_nope, q_rope = (q[..., :NOPE], q[..., NOPE:])
            q = jnp.concatenate([q_nope, _rope(q_rope)], axis=-1)
            k = jnp.concatenate([kv, _rope(k_rope)], axis=-1)
            v = jnp.concatenate([kv, jnp.zeros_like(k_rope)], axis=-1)
            att = jnp.einsum('bhqd,bhkd->bhqk', q, k) / jnp.sqrt(jnp.float32(D))
            mask = jnp.tril(jnp.ones((t, t), dtype=bool))
            att = jnp.where(mask, att, jnp.float32(-jnp.inf))
            att = jax.nn.softmax(att, axis=-1)
            y = jnp.einsum('bhqk,bhkd->bhqd', att, v)
            y = y.transpose(0, 2, 1, 3).reshape(b, t, H * D)
            return y @ Wo

        def _experts(x_flat, Wg, Wu, Wd):
            g = jax.nn.silu(jnp.einsum('nc,eci->nei', x_flat, Wg))
            u = jnp.einsum('nc,eci->nei', x_flat, Wu)
            return jnp.einsum('nei,eic->nec', g * u, Wd)

        def _moe(x, Wgate, expert_bias, Wg, Wu, Wd, sWg, sWu, sWd):
            b, t, c = x.shape
            xf = x.reshape(-1, c)
            shared = jnp.mean(_experts(xf, sWg, sWu, sWd), axis=1)
            logits = xf @ Wgate + expert_bias
            probs = jax.nn.softmax(logits, axis=-1)
            topk_p, topk_i = jax.lax.top_k(probs, K)
            topk_p = topk_p / jnp.sum(topk_p, axis=-1, keepdims=True)
            comb = jnp.sum(jax.nn.one_hot(topk_i, E, dtype=xf.dtype) * topk_p[..., None], axis=1)
            routed = jnp.einsum('ne,nec->nc', comb, _experts(xf, Wg, Wu, Wd))
            return (shared + routed).reshape(b, t, c)
        x = x + _attention(_rmsnorm(x, w_ln1), Wq, Wkva, Wkvb, Wo)
        residual = x
        xn = _rmsnorm(x, w_ln2)
        x_out = _moe(xn, Wgate, expert_bias, Wg, Wu, Wd, sWg, sWu, sWd)
        return residual + x_out

    def _L1_attn_ref(x, in_proj_w, conv_w, conv_b, x_proj_w, dt_w, dt_b, A_log, D_p, out_proj_w, norm_w):
        import jax, jax.numpy as jnp
        import numpy as np
        from jax import lax
        NL, D, ED, N, K, R = (2, 256, 512, 16, 4, 64)
        B, L = (2, 256)
        EPS = 1e-05

        def _rmsnorm(x, w):
            return x * jax.lax.rsqrt(jnp.mean(x * x, axis=-1, keepdims=True) + EPS) * w

        def _depthwise_causal_conv(x, w, b):
            y = lax.conv_general_dilated(x, w, window_strides=(1,), padding=[(K - 1, 0)], dimension_numbers=('NCH', 'OIH', 'NCH'), feature_group_count=ED)
            return y + b[None, :, None]

        def _selective_scan(deltaA, deltaBx, C):

            def step(h, inp):
                dA, dBx, c = inp
                h = dA * h + dBx
                y = jnp.einsum('ben,bn->be', h, c)
                return (h, y)
            h0 = jnp.zeros((deltaA.shape[0], ED, N), dtype=deltaA.dtype)
            _, ys = lax.scan(step, h0, (jnp.moveaxis(deltaA, 1, 0), jnp.moveaxis(deltaBx, 1, 0), jnp.moveaxis(C, 1, 0)))
            return jnp.moveaxis(ys, 0, 1)

        def _mamba_block(xn, p):
            in_w, cw, cb, xp_w, dtw, dtb, A_log, Dp, out_w = p
            xz = jnp.einsum('bld,ed->ble', xn, in_w)
            xi, z = jnp.split(xz, 2, axis=-1)
            xc = _depthwise_causal_conv(jnp.swapaxes(xi, 1, 2), cw, cb)
            u = jax.nn.silu(jnp.swapaxes(xc, 1, 2))
            dbc = jnp.einsum('ble,re->blr', u, xp_w)
            d_r, Bm, Cm = jnp.split(dbc, [R, R + N], axis=-1)
            delta = jax.nn.softplus(jnp.einsum('blr,er->ble', d_r, dtw) + dtb)
            A = -jnp.exp(A_log)
            deltaA = jnp.exp(delta[..., None] * A)
            deltaBx = delta[..., None] * Bm[:, :, None, :] * u[..., None]
            y = _selective_scan(deltaA, deltaBx, Cm)
            y = y + Dp * u
            y = y * jax.nn.silu(z)
            return jnp.einsum('ble,de->bld', y, out_w)
        h = x
        for i in range(NL):
            p = (in_proj_w[i], conv_w[i], conv_b[i], x_proj_w[i], dt_w[i], dt_b[i], A_log[i], D_p[i], out_proj_w[i])
            h = _mamba_block(_rmsnorm(h, norm_w[i]), p) + h
        return h

    def _L1_ffn_ref(x, router_prob, norm_w, norm_b, q_w, q_b, k_w, k_b, v_w, v_b, o_w, o_b):
        import jax, jax.numpy as jnp
        import numpy as np
        B, T, D, E, H = (4, 512, 256, 4, 8)
        EPS = 1e-05

        def _uniform(k, shape, bound):
            return jax.random.uniform(k, shape, jnp.float32, -bound, bound)

        def _layernorm(x, w, b):
            mu = jnp.mean(x, axis=-1, keepdims=True)
            var = jnp.mean(jnp.square(x - mu), axis=-1, keepdims=True)
            return (x - mu) * jax.lax.rsqrt(var + EPS) * w + b
        e_cnt = router_prob.shape[2]
        b, t, d = x.shape
        n = t // e_cnt
        h = H
        scale = d ** (-0.5)
        qs, ks_, vs = ([], [], [])
        for e in range(e_cnt):
            xe = x[:, e * n:(e + 1) * n, :]
            xn = _layernorm(xe, norm_w, norm_b)
            m = d // 2 ** e
            xm = xn[..., :m]
            qs.append(jnp.einsum('bnm,dm->bnd', xm, q_w[:, :m]) + q_b)
            ks_.append(jnp.einsum('bnm,dm->bnd', xm, k_w[:, :m]) + k_b)
            vs.append(jnp.einsum('bnm,dm->bnd', xm, v_w[:, :m]) + v_b)
        q = jnp.concatenate(qs, axis=1)
        k = jnp.concatenate(ks_, axis=1)
        v = jnp.concatenate(vs, axis=1)
        dh = d // h
        q = q.reshape(b, t, h, dh).transpose(0, 2, 1, 3)
        k = k.reshape(b, t, h, dh).transpose(0, 2, 1, 3)
        v = v.reshape(b, t, h, dh).transpose(0, 2, 1, 3)
        attn = jnp.einsum('bhqd,bhkd->bhqk', q, k) * scale
        attn = jax.nn.softmax(attn, axis=-1)
        attn_out = jnp.einsum('bhqk,bhkd->bhqd', attn, v)
        attn_out = attn_out.transpose(0, 2, 1, 3).reshape(b, t, d)
        outs = []
        for e in range(e_cnt):
            sl = slice(e * n, (e + 1) * n)
            m = d // 2 ** e
            xm = attn_out[:, sl, :m]
            out = jnp.einsum('bnm,om->bno', xm, o_w[:m, :m]) + o_b[:m]
            pad = d - m
            if pad:
                out = jnp.pad(out, ((0, 0), (0, 0), (0, pad)))
            outs.append(out + x[:, sl, :])
        return jnp.concatenate(outs, axis=1)

    def _L2_attn_ref(x, Wq, bq, Wk, bk, Wv, bv, Wo, bo):
        import math
        import jax, jax.numpy as jnp
        import numpy as np
        B, T, C, H = (1, 1024, 256, 16)
        HD = C // H

        def get_slopes(n):

            def pow2(n):
                start = 2 ** (-2 ** (-(math.log2(n) - 3)))
                return [start * start ** i for i in range(n)]
            if math.log2(n).is_integer():
                return pow2(n)
            cp2 = 2 ** math.floor(math.log2(n))
            return pow2(cp2) + get_slopes(2 * cp2)[0::2][:n - cp2]
        b, t, c = x.shape
        proj = lambda W, bias: (x @ W + bias).reshape(b, t, H, HD).transpose(0, 2, 1, 3)
        q, k, v = (proj(Wq, bq), proj(Wk, bk), proj(Wv, bv))
        scale = 1.0 / jnp.sqrt(jnp.asarray(HD, x.dtype))
        attn = jnp.einsum('bhqd,bhkd->bhqk', q, k) * scale
        slopes = jnp.asarray(get_slopes(H), dtype=x.dtype)
        alibi = -slopes[:, None, None] * (t - 1 - jnp.arange(t, dtype=x.dtype))[None, None, :]
        attn = attn + alibi
        causal = jnp.tril(jnp.ones((t, t), dtype=bool))[None, None]
        attn = jnp.where(causal, attn, jnp.finfo(x.dtype).min)
        p = jax.nn.softmax(attn, axis=-1)
        out = jnp.einsum('bhqk,bhkd->bhqd', p, v).transpose(0, 2, 1, 3).reshape(b, t, c)
        return out @ Wo + bo

    def _L2_ffn_ref(x, router_w, correction_bias, gate_w, up_w, down_w, shared_gate_w, shared_up_w, shared_down_w):
        import jax, jax.numpy as jnp
        import numpy as np
        E = 16
        G = 4
        EPG = E // G
        K = 4
        TOPK_GROUP = 2
        PER_GROUP_K = K // TOPK_GROUP

        def _route(xf, router_w, correction_bias):
            S = xf.shape[0]
            logits = xf @ router_w.T
            scores = jax.nn.sigmoid(logits)
            sb = scores + correction_bias
            grp_top = jax.lax.top_k(sb.reshape(S, G, EPG), PER_GROUP_K)[0]
            group_scores = grp_top.sum(axis=-1)
            _, group_idx = jax.lax.top_k(group_scores, TOPK_GROUP)
            group_mask = jnp.zeros((S, G), sb.dtype).at[jnp.arange(S)[:, None], group_idx].set(1.0)
            score_mask = jnp.broadcast_to(group_mask[:, :, None], (S, G, EPG)).reshape(S, E)
            masked = jnp.where(score_mask > 0, sb, -jnp.inf)
            _, topk_idx = jax.lax.top_k(masked, K)
            w = jnp.take_along_axis(scores, topk_idx, axis=1)
            w = w / (w.sum(axis=-1, keepdims=True) + 1e-20)
            return (topk_idx, w, scores)
        B, T, C = x.shape
        S = B * T
        xf = x.reshape(S, C)
        sg = xf @ shared_gate_w.T
        su = xf @ shared_up_w.T
        shared_out = jax.nn.silu(sg) * su @ shared_down_w.T
        topk_idx, w, _scores = _route(xf, router_w, correction_bias)
        combine = jnp.zeros((S, E), xf.dtype).at[jnp.arange(S)[:, None], topk_idx].add(w)
        g = jnp.einsum('sc,ech->esh', xf, gate_w)
        u = jnp.einsum('sc,ech->esh', xf, up_w)
        h = jax.nn.silu(g) * u
        hw = h * combine.T[:, :, None]
        routed = jnp.einsum('esh,ehc->sc', hw, down_w)
        return (shared_out + routed).reshape(B, T, C)

    def _L3_attn_ref(x, Wq, Wk, Wv, Wp, bp, rel_embed):
        import jax, jax.numpy as jnp
        import numpy as np
        B, N, D, NH, MAXLEN = (2, 512, 256, 16, 512)
        HD = D // NH

        def srel_skew(x):
            b, h, n, _ = x.shape
            v = jnp.pad(x, ((0, 0), (0, 0), (0, 0), (1, 0)))
            return v.reshape(b, h, n + 1, n)[:, :, :n, :]

        def split_head(x):
            b, n, _ = x.shape
            return x.reshape(b, n, NH, HD).transpose(0, 2, 1, 3)
        b, n, d = x.shape
        qx = split_head(x @ Wq.T)
        kx = split_head(x @ Wk.T)
        vx = split_head(x @ Wv.T)
        ns = jnp.arange(n) + (MAXLEN - n)
        ex = rel_embed[ns].reshape(n, NH, HD).transpose(1, 0, 2)
        srel = srel_skew(jnp.einsum('bhnd,hmd->bhnm', qx, ex))
        inv_dim = 1.0 / np.sqrt(d / NH)
        qk = (jnp.einsum('bhnd,bhmd->bhnm', qx, kx) + srel) * inv_dim
        mask = 1000000000.0 * jnp.triu(jnp.ones((n, n), dtype=x.dtype), 1)
        atten = jax.nn.softmax(qk - mask, axis=-1)
        out = jnp.einsum('bhnm,bhmd->bhnd', atten, vx).transpose(0, 2, 1, 3).reshape(b, n, d)
        return out @ Wp.T + bp

    def _L3_ffn_ref(hidden_states, W1, b1, W2, b2, expert_W, expert_b):
        import jax, jax.numpy as jnp
        import numpy as np
        B, S, H, E = (8, 1024, 256, 8)
        TEMPERATURE = 1.0
        h = jax.nn.relu(jnp.einsum('bsh,hf->bsf', hidden_states, W1) + b1)
        logits = jnp.einsum('bsf,fe->bse', h, W2) + b2
        probs = jax.nn.softmax(logits / TEMPERATURE, axis=-1)
        sel = jnp.argmax(probs, axis=-1)
        out = jnp.zeros_like(hidden_states)
        for e in range(E):
            mask = (sel == e)[..., None].astype(hidden_states.dtype)
            xe = hidden_states * mask
            ye = jnp.einsum('bsh,hd->bsd', xe, expert_W[e]) + expert_b[e]
            out = out + ye * mask
        return out
    x = L0_attn_x
    xn = _layernorm(x, axis=-1)
    x = x + _L0_attn_ref(xn, L0_attn_W_q, L0_attn_W_k, L0_attn_W_v, L0_attn_W_o, L0_attn_W_down_kv, L0_attn_W_up_k, L0_attn_W_up_v) + _L0_ffn_ref(xn, L0_ffn_w_ln1, L0_ffn_Wq, L0_ffn_Wkva, L0_ffn_Wkvb, L0_ffn_Wo, L0_ffn_w_ln2, L0_ffn_Wgate, L0_ffn_expert_bias, L0_ffn_Wg, L0_ffn_Wu, L0_ffn_Wd, L0_ffn_sWg, L0_ffn_sWu, L0_ffn_sWd)
    xn = _layernorm(x, axis=-1)
    x = x + _L1_attn_ref(xn, L1_attn_in_proj_w, L1_attn_conv_w, L1_attn_conv_b, L1_attn_x_proj_w, L1_attn_dt_w, L1_attn_dt_b, L1_attn_A_log, L1_attn_D_p, L1_attn_out_proj_w, L1_attn_norm_w) + _L1_ffn_ref(xn, L1_ffn_router_prob, L1_ffn_norm_w, L1_ffn_norm_b, L1_ffn_q_w, L1_ffn_q_b, L1_ffn_k_w, L1_ffn_k_b, L1_ffn_v_w, L1_ffn_v_b, L1_ffn_o_w, L1_ffn_o_b)
    xn = _layernorm(x, axis=-1)
    x = x + _L2_attn_ref(xn, L2_attn_Wq, L2_attn_bq, L2_attn_Wk, L2_attn_bk, L2_attn_Wv, L2_attn_bv, L2_attn_Wo, L2_attn_bo) + _L2_ffn_ref(xn, L2_ffn_router_w, L2_ffn_correction_bias, L2_ffn_gate_w, L2_ffn_up_w, L2_ffn_down_w, L2_ffn_shared_gate_w, L2_ffn_shared_up_w, L2_ffn_shared_down_w)
    xn = _layernorm(x, axis=-1)
    x = x + _L3_attn_ref(xn, L3_attn_Wq, L3_attn_Wk, L3_attn_Wv, L3_attn_Wp, L3_attn_bp, L3_attn_rel_embed) + _L3_ffn_ref(xn, L3_ffn_W1, L3_ffn_b1, L3_ffn_W2, L3_ffn_b2, L3_ffn_expert_W, L3_ffn_expert_b)
    return x

_drawn_inputs = setup_inputs


def setup_inputs(seed=0):
    import zlib

    import numpy as np

    out = dict(_drawn_inputs(seed))
    spreads = {'L0_ffn_w_ln1': (1.0, 0.2),
     'L0_ffn_w_ln2': (1.0, 0.2),
     'L0_ffn_expert_bias': (0.0, 0.1),
     'L1_attn_D_p': (1.0, 0.2),
     'L1_attn_norm_w': (1.0, 0.2),
     'L1_ffn_norm_w': (1.0, 0.2),
     'L1_ffn_norm_b': (0.0, 0.1),
     'L2_attn_bq': (0.0, 0.1),
     'L2_attn_bk': (0.0, 0.1),
     'L2_attn_bv': (0.0, 0.1),
     'L2_attn_bo': (0.0, 0.1),
     'L2_ffn_correction_bias': (0.0, 0.1),
     'L3_attn_bp': (0.0, 0.1),
     'L3_ffn_b1': (0.0, 0.1),
     'L3_ffn_b2': (0.0, 0.1)}
    factors = {}
    for name, (base, spread) in spreads.items():
        noise = np.random.default_rng([zlib.crc32(name.encode()), seed]).standard_normal(out[name].shape)
        drawn = base * np.exp(spread * noise) if base else spread * noise
        out[name] = jnp.asarray(drawn.astype(out[name].dtype))
    for name, factor in factors.items():
        out[name] = (out[name] * factor).astype(out[name].dtype)
    return out
```

```python
from contextlib import ExitStack

import numpy as np

import concourse.bass as bass
from concourse import mybir

F32 = mybir.dt.float32
BF16 = mybir.dt.bfloat16
ALU = mybir.AluOpType
ACT = mybir.ActivationFunctionType
AX = mybir.AxisListType.X

P = 128
S = 512
D = 256
NI = S // P
NC = D // P
BIG = 1.0e30
LOWEST = 3.0e38
EPS = 1e-5
ED, NS, DTR, KC, NL = 512, 16, 64, 4, 2
NT = ED // P
REL = 4 * P * (S + 1) + 16
NCONST = 2 * P + 32 + 8 + 4 + 2
ARENA = 47800


def _rows(w):
    w = np.asarray(w)
    k, n = w.shape
    c = -(-k // P)
    out = np.zeros((c * P, n), np.float32)
    out[:k] = w
    return out.reshape(c, P, n).transpose(1, 0, 2).reshape(P, c * n)


def _spread(w, heads, slot):
    w = np.asarray(w)
    out = np.zeros((w.shape[0], heads, slot), np.float32)
    out[:, :, : w.shape[1] // heads] = w.reshape(w.shape[0], heads, -1)
    return out.reshape(w.shape[0], heads * slot)


def _col(v):
    return np.asarray(v, np.float32).reshape(-1, P).T


def _row(v):
    out = np.zeros((P, np.asarray(v).size), np.float32)
    out[0] = np.asarray(v).reshape(-1)
    return out


def _tri(n):
    t = np.tril(np.ones((n, n), np.float32), -1)
    return np.broadcast_to(t.reshape(1, -1), (P, n * n))


def _select(e, tiles):
    per = e // tiles
    out = np.zeros((P, tiles * P), np.float32)
    for r in range(e):
        for part in range(3):
            out[32 * part + r, r * P // per:(r + 1) * P // per] = 1
    return out


def pack_block(block, a):
    g = lambda name: np.asarray(a[name])
    t = np.arange(S, dtype=np.float32)
    out = []
    add = lambda name, w: out.append((name, np.asarray(w, np.float32)))
    if block == 0:
        decay = np.exp(np.float32(-0.01) * np.abs(t[:, None] - t[None, :])).astype(np.float32)
        add("a_q", _rows(g("L0_attn_W_q")))
        add("a_k", _rows(g("L0_attn_W_k")))
        add("a_v", _rows(g("L0_attn_W_v")))
        add("a_down", _rows(g("L0_attn_W_down_kv")))
        add("a_upk", _rows(g("L0_attn_W_up_k")))
        add("a_upv", _rows(g("L0_attn_W_up_v")))
        add("a_o", _rows(g("L0_attn_W_o")))
        add("decay", _rows(decay))
        freqs = (1.0 / np.float32(100000.0) ** (np.arange(0, 32, 2, dtype=np.float32) / 32)).astype(np.float32)
        ang = np.outer(t, freqs).astype(np.float32)
        cos, sin = np.ones((64, S), np.float32), np.zeros((64, S), np.float32)
        cos[32::2] = cos[33::2] = np.cos(ang).T
        sin[32::2], sin[33::2] = -np.sin(ang).T, np.sin(ang).T
        swap = np.zeros((P, P), np.float32)
        swap[np.arange(P), np.arange(P) ^ 1] = 1
        add("cos", np.tile(cos, (2, 1)))
        add("sin", np.tile(sin, (2, 1)))
        add("swap", swap)
        add("f_q", _rows(g("L0_ffn_Wq")))
        add("f_kva", _rows(g("L0_ffn_Wkva")))
        k2 = np.zeros((64, 16, 64), np.float32)
        k2[:32, :, :32] = g("L0_ffn_Wkvb").reshape(32, 16, 32)
        k2[32 + np.arange(32), :, 32 + np.arange(32)] = 1
        add("f_k2", _rows(k2.reshape(64, 1024)))
        add("f_kvb", _rows(g("L0_ffn_Wkvb")))
        add("f_o", _rows(g("L0_ffn_Wo").reshape(16, 64, D)[:, :32].reshape(512, D)))
        add("ln1", _col(g("L0_ffn_w_ln1")))
        add("ln2", _col(g("L0_ffn_w_ln2")))
        add("gate", _rows(g("L0_ffn_Wgate")))
        add("gate_b", _row(g("L0_ffn_expert_bias")))
        add("tri", _tri(8))
        add("select", _select(8, 8))
        for name, own, shared in (("e_g", "Wg", "sWg"), ("e_u", "Wu", "sWu"), ("e_d", "Wd", "sWd")):
            add(name, np.concatenate([_rows(w) for w in (*g("L0_ffn_" + shared), *g("L0_ffn_" + own))], 1))
    if block == 1:
        for i in range(NL):
            n = f"m{i}_"
            add(n + "in", _rows(g("L1_attn_in_proj_w")[i].T))
            add(n + "cw", g("L1_attn_conv_w")[i].reshape(NT, P, KC).transpose(1, 0, 2).reshape(P, -1))
            add(n + "cb", _col(g("L1_attn_conv_b")[i]))
            add(n + "x", _rows(g("L1_attn_x_proj_w")[i].T))
            add(n + "dt", _rows(g("L1_attn_dt_w")[i].T))
            add(n + "dtb", _col(g("L1_attn_dt_b")[i]))
            add(n + "A", g("L1_attn_A_log")[i].reshape(NT, P, NS).transpose(1, 0, 2).reshape(P, -1))
            add(n + "D", _col(g("L1_attn_D_p")[i]))
            add(n + "out", _rows(g("L1_attn_out_proj_w")[i].T))
            add(n + "norm", _col(g("L1_attn_norm_w")[i]))
        for n in "qkvo":
            add("f_" + n, _rows(g(f"L1_ffn_{n}_w").T))
        for n in "qk":
            add(f"f_{n}b", _col(g(f"L1_ffn_{n}_b")))
        for n in "vo":
            add(f"f_{n}b", _row(g(f"L1_ffn_{n}_b")))
        add("norm_w", _col(g("L1_ffn_norm_w")))
        add("norm_b", _col(g("L1_ffn_norm_b")))
    if block == 2:
        for n in "qk":
            add("a_" + n, _rows(_spread(g("L2_attn_W" + n), 16, 32)))
        for n in "vo":
            add("a_" + n, _rows(g("L2_attn_W" + n)))
            add(f"a_{n}b", _row(g("L2_attn_b" + n)))
        qb = _spread(g("L2_attn_bq").reshape(1, D), 16, 32).reshape(16, 32)
        qb[:, 16] = 4
        add("a_qb", _col(qb.reshape(-1)))
        add("a_kb", _col(_spread(g("L2_attn_bk").reshape(1, D), 16, 32).reshape(-1)))
        slopes = np.float32([2.0 ** (-0.5 * (h + 1)) for h in range(16)])
        alibi = np.zeros((16, 32, S), np.float32)
        alibi[:, 16] = -slopes[:, None] * (np.float32(S - 1) - t)[None, :]
        add("alibi", _rows(alibi.reshape(512, S)))
        add("gate", _rows(g("L2_ffn_router_w").T))
        add("bias", np.broadcast_to(g("L2_ffn_correction_bias").reshape(1, 16), (P, 16)))
        add("tri4", _tri(4))
        add("tri16", _tri(16))
        add("select", _select(16, 8))
        for name, own, shared in (("e_g", "gate_w", "shared_gate_w"), ("e_u", "up_w", "shared_up_w")):
            two = g("L2_ffn_" + own).reshape(8, 2, D, 64).transpose(0, 2, 1, 3).reshape(8, D, P)
            four = g("L2_ffn_" + shared).T.reshape(D, 4, P).transpose(1, 0, 2)
            add(name, np.concatenate([_rows(w) for w in (*four, *two)], 1))
        down = (*g("L2_ffn_shared_down_w").T.reshape(4, P, D), *g("L2_ffn_down_w").reshape(8, P, D))
        add("e_d", np.concatenate([_rows(w) for w in down], 1))
    if block == 3:
        for n in "qk":
            add("a_" + n, _rows(g("L3_attn_W" + n).T))
        add("a_v", _rows(g("L3_attn_Wv").T))
        add("a_o", _rows(g("L3_attn_Wp").T))
        add("a_ob", _row(g("L3_attn_bp")))
        e = np.zeros((P, 16, S), np.float32)
        for h in range(16):
            e[16 * (h % 8):16 * (h % 8) + 16, h] = g("L3_attn_rel_embed")[:, 16 * h:16 * h + 16].T
        add("a_e", e.reshape(P, 16 * S))
        add("w1", _rows(g("L3_ffn_W1")))
        add("b1", _col(g("L3_ffn_b1")))
        add("w2", _rows(g("L3_ffn_W2")))
        add("b2", _row(g("L3_ffn_b2")))
        add("tri", _tri(8))
        add("select", _select(8, 8))
        add("e_w", np.concatenate([_rows(w) for w in g("L3_ffn_expert_W")], 1))
        add("e_b", _rows(g("L3_ffn_expert_b")))
    return out


def pack_constants():
    upper = np.triu(np.full((P, P), BIG, np.float32), 1)
    three = np.zeros((P, 32), np.float32)
    three[:96] = np.tile(np.eye(32, dtype=np.float32), (3, 1))
    slots = [np.repeat(np.eye(P // n, dtype=np.float32), n, 0) for n in (16, 32, 64)]
    return np.concatenate([np.eye(P, dtype=np.float32), upper, three, *slots], 1)


def build(nc, x_in, consts, packs, sizes, out, blocks, batches):
    ctx = ExitStack()
    with ctx:
        sb = lambda name, n, dt=F32: ctx.enter_context(nc.sbuf_tensor(name, [P, n], dt))
        arena = sb("arena", ARENA)
        X3, XN3, XT3, ACC3 = (sb(n, NI * D) for n in ("x_sb", "xn_sb", "xt_sb", "acc_sb"))
        X, XN, ACC = (w[:, :].rearrange("p (i d) -> p i d", i=NI) for w in (X3, XN3, ACC3))
        XT = XT3[:, :].rearrange("p (c s) -> p c s", c=NC)
        const = sb("const", NCONST)
        ident, upper = const[:, 0:P], const[:, P:2 * P]
        constb = sb("constb", NCONST, BF16)
        identb, upperb, three = constb[:, 0:P], constb[:, P:2 * P], constb[0:96, 2 * P:2 * P + 32]
        slots = {16: const[:, 288:296], 32: const[:, 296:300], 64: const[:, 300:302]}
        ones = sb("ones", P)
        zero = sb("zero", 16)
        small = sb("small", 512)
        psum = ctx.enter_context(nc.psum_tensor("psum", [P, 8 * 512], F32))
        bank = lambda i, n=1: psum[:, i * 512:(i + n) * 512]
        x_mid = nc.dram_tensor("x_mid", [batches * S, D], F32).ap()
        rel_mid = nc.dram_tensor("rel_mid", [16, REL], F32).ap()

        sem = lambda name: ctx.enter_context(nc.semaphore(name))
        constants_loaded = sem("constants_loaded")
        weights_loaded = sem("weights_loaded")
        constants_made = sem("constants_made")
        zeros_stored = sem("zeros_stored")
        select_made = sem("select_made")
        go_even = sem("go_even")
        x_loaded = sem("x_loaded")
        x_stored = sem("x_stored")
        dve_step = sem("dve_step")
        act_step = sem("act_step")
        stats_ready = sem("stats_ready")
        rstd_ready = sem("rstd_ready")
        normed = sem("normed")
        turned = sem("turned")
        turned_dve = sem("turned_dve")
        turned_act = sem("turned_act")
        proj_ready = sem("proj_ready")
        proj_dve = sem("proj_dve")
        proj_act = sem("proj_act")
        swapped = sem("swapped")
        cos_done = sem("cos_done")
        sin_done = sem("sin_done")
        roped = sem("roped")
        keys_ready = sem("keys_ready")
        scores_ready = sem("scores_ready")
        max_ready = sem("max_ready")
        exp_ready = sem("exp_ready")
        pt_ready = sem("pt_ready")
        pt_dve = sem("pt_dve")
        pt_act = sem("pt_act")
        o_ready = sem("o_ready")
        on_ready = sem("on_ready")
        rel_ready = sem("rel_ready")
        rel_dve = sem("rel_dve")
        rel_act = sem("rel_act")
        rel_stored = sem("rel_stored")
        rel_loaded = [sem(f"rel_loaded{i}") for i in range(4)]
        conv_ready = sem("conv_ready")
        u_ready = sem("u_ready")
        soft_in = sem("soft_in")
        soft_abs = sem("soft_abs")
        soft_log = sem("soft_log")
        delta_ready = sem("delta_ready")
        split_ready = sem("split_ready")
        b_ready = sem("b_ready")
        c_ready = sem("c_ready")
        da_ready = sem("da_ready")
        dbx_done = sem("dbx_done")
        scan_done = sem("scan_done")
        hc_done = sem("hc_done")
        y_added = sem("y_added")
        y_ready = sem("y_ready")
        logits_ready = sem("logits_ready")
        router_in = sem("router_in")
        router_exp = sem("router_exp")
        comb_ready = sem("comb_ready")
        comb_turned = sem("comb_turned")
        combt_ready = sem("combt_ready")
        gate_ready = sem("gate_ready")
        silu_ready = sem("silu_ready")
        hidden_ready = sem("hidden_ready")
        down_ready = sem("down_ready")
        down_done = sem("down_done")
        arrived = sem("arrived")
        go_odd = sem("go_odd")

        def meet(e, odd):
            if e is nc.sync:
                e.wait_ge(arrived, 4)
                e.sem_clear(range(go_even.num + 1 - odd, go_odd.num + 1 - odd))
                e.drain().then_inc(go_odd if odd else go_even, 1)
            else:
                e.drain().then_inc(arrived, 1)
                e.wait_ge(go_odd if odd else go_even, 1)
                e.drain()
            v.count = a.count = 0

        class Steps:

            def __init__(self, engine, semaphore):
                self.engine, self.semaphore, self.count = engine, semaphore, 0

            def step(self, instruction):
                instruction.then_inc(self.semaphore, 1)
                self.count += 1

            def settle(self):
                self.engine.wait_ge(self.semaphore, self.count)

        v = Steps(nc.vector, dve_step)
        a = Steps(nc.scalar, act_step)

        class Place:
            pass

        def views(block):
            w, at = {}, 0
            for name, n in sizes[block]:
                w[name] = arena[:, at:at + n]
                at += n
            if "select" in w:
                n = w["select"].shape[1] // 2
                w["select_b"] = arena[:, at:at + n].bitcast(BF16)
                at += n
            return w, at

        def chunks(ap, c):
            return ap.rearrange("p (c n) -> p c n", c=c)

        class Taker:
            def __init__(self, at):
                self.at = at

            def __call__(self, n):
                assert self.at + n <= ARENA, (self.at, n)
                self.at += n
                return arena[:, self.at - n:self.at]

        st = small[:, 0:24].rearrange("p (i s) -> p i s", i=NI)
        mv = small[:, 24:32].rearrange("p (i s) -> p i s", i=NI)
        msq, var, lnv, rstd = (small[:, 32 + 4 * i:36 + 4 * i] for i in range(4))

        def norm_vector(k, src, rms, dst, dst_t, w=None, b=None):
            for i in range(NI):
                last = nc.vector.bn_stats(st[:, i], src[:, i])
            v.step(last)
            v.settle()
            for i in range(NI):
                last = nc.vector.bn_aggr(mv[:, i], st[:, i])
            v.step(last)
            v.settle()
            if rms:
                v.step(nc.vector.tensor_tensor(msq, mv[:, :, 0], mv[:, :, 0], ALU.mult))
                v.settle()
                nc.vector.scalar_tensor_tensor(out=var, in0=msq, scalar=EPS, in1=mv[:, :, 1],
                                               op0=ALU.add, op1=ALU.add).then_inc(stats_ready, 1)
            else:
                nc.vector.tensor_scalar(var, mv[:, :, 1], EPS, None, ALU.add).then_inc(stats_ready, 1)
            nc.vector.wait_ge(rstd_ready, k + 1)
            for i in range(NI):
                if rms:
                    last = nc.vector.tensor_scalar(dst[:, i], src[:, i], rstd[:, i:i + 1], None, ALU.mult)
                else:
                    last = nc.vector.tensor_scalar(dst[:, i], src[:, i], mv[:, i, 0:1], rstd[:, i:i + 1],
                                                   ALU.subtract, ALU.mult)
            last.then_inc(normed, 1)
            nc.vector.wait_ge(turned, 2 * k + 1)
            if w is None:
                nc.vector.tensor_copy(dst_t[:, 0], bank(6)).then_inc(turned_dve, 1)
            elif b is None:
                nc.vector.tensor_scalar(dst_t[:, 0], bank(6), w[:, 0:1], None, ALU.mult).then_inc(turned_dve, 1)
            else:
                nc.vector.tensor_scalar(dst_t[:, 0], bank(6), w[:, 0:1], b[:, 0:1],
                                        ALU.mult, ALU.add).then_inc(turned_dve, 1)

        def norm_scalar(k, dst_t, w=None, b=None):
            nc.scalar.wait_ge(stats_ready, k + 1)
            a.step(nc.scalar.activation(lnv, var, ACT.Ln))
            a.settle()
            nc.scalar.activation(rstd, lnv, ACT.Exp, scale=-0.5).then_inc(rstd_ready, 1)
            nc.scalar.wait_ge(turned, 2 * k + 2)
            if w is None:
                last = nc.scalar.activation(dst_t[:, 1], bank(7), ACT.Copy)
            elif b is None:
                last = nc.scalar.activation(dst_t[:, 1], bank(7), ACT.Copy, scale=w[:, 1:2])
            else:
                last = nc.scalar.activation(dst_t[:, 1], bank(7), ACT.Identity, scale=w[:, 1:2], bias=b[:, 1:2])
            last.then_inc(turned_act, 1)

        def norm_tensor(k, dst):
            nc.tensor.wait_ge(normed, k + 1)
            for c in range(NC):
                for i in range(NI):
                    last = nc.tensor.transpose(bank(6 + c)[:, i * P:(i + 1) * P], dst[:, i, c * P:(c + 1) * P], ident)
                last.then_inc(turned, 1)

        def turned_there(e, k):
            e.wait_ge(turned_dve, k + 1)
            e.wait_ge(turned_act, k + 1)

        class Tiles:

            def __init__(self, tiles, before=None):
                self.tiles, self.before = tiles, before
                self.first = before.end if before else (0, 0, 0)
                self.through = []
                self.on_act = []
                d, s = self.first[1], self.first[2]
                for n, (_, _, way, _) in enumerate(tiles):
                    on_act = bool({"relu", "silu"} & set(way)) or (n % 2 == 1 and not {"col", "plus"} & set(way))
                    self.on_act.append(on_act)
                    d, s = d + (not on_act), s + on_act
                    self.through.append((d, s))
                self.end = (self.first[0] + len(tiles), d, s)

        def tiles_there(e, t, n=-1):
            d, s = t.through[n]
            if d and e is not nc.vector or d and n != -1:
                e.wait_ge(proj_dve, d)
            elif d:
                e.wait_ge(proj_dve, d)
            if s:
                e.wait_ge(proj_act, s)

        def tiles_tensor(t):
            if t.before:
                tiles_there(nc.tensor, t.before)
            for n, (pairs, dst, way, need) in enumerate(t.tiles):
                if need is not None:
                    tiles_there(nc.tensor, t, need)
                elif n >= 4:
                    tiles_there(nc.tensor, t, n - 4)
                o = bank(n % 4)[0:dst.shape[0], 0:dst.shape[-1]]
                for j, (lhs, rhs) in enumerate(pairs):
                    last = nc.tensor.matmul(o, lhs, rhs, start=j == 0, stop=j == len(pairs) - 1)
                last.then_inc(proj_ready, 1)

        def tiles_vector(t):
            for n, (pairs, dst, way, need) in enumerate(t.tiles):
                if t.on_act[n]:
                    continue
                nc.vector.wait_ge(proj_ready, t.first[0] + n + 1)
                o = bank(n % 4)[0:dst.shape[0], 0:dst.shape[-1]]
                if "plus" in way:
                    last = nc.vector.scalar_tensor_tensor(out=dst, in0=o, scalar=way["col"], in1=way["plus"],
                                                          op0=ALU.add, op1=ALU.add)
                elif "col" in way:
                    last = nc.vector.tensor_scalar(dst, o, way["col"], way.get("mul", 1.0), ALU.add, ALU.mult)
                elif "spread" in way:
                    for h in range(dst.shape[1]):
                        last = nc.vector.tensor_scalar(dst[:, h], o, way["spread"][:, h:h + 1], None, ALU.mult)
                elif "mul" in way:
                    last = nc.vector.tensor_scalar(dst, o, way["mul"], None, ALU.mult)
                else:
                    last = nc.vector.tensor_copy(dst, o)
                last.then_inc(proj_dve, 1)

        def tiles_scalar(t):
            for n, (pairs, dst, way, need) in enumerate(t.tiles):
                if not t.on_act[n]:
                    continue
                nc.scalar.wait_ge(proj_ready, t.first[0] + n + 1)
                o = bank(n % 4)[0:dst.shape[0], 0:dst.shape[-1]]
                if "silu" in way:
                    last = nc.scalar.activation(dst, o, ACT.Silu)
                elif "relu" in way:
                    last = nc.scalar.activation(dst, o, ACT.Relu, bias=way["col"])
                elif "spread" in way:
                    for h in range(dst.shape[1]):
                        last = nc.scalar.activation(dst[:, h], o, ACT.Copy, scale=way["spread"][:, h:h + 1])
                else:
                    last = nc.scalar.activation(dst, o, ACT.Copy, scale=way.get("mul", 1.0))
                last.then_inc(proj_act, 1)

        def feature_tile(w, src, cols):
            return [(w[:, c, cols], src[:, c]) for c in range(w.shape[1])]

        def token_tile(src, w, i, cols):
            return [(src[:, c, i * P:(i + 1) * P], w[:, c, cols]) for c in range(w.shape[1])]

        def bias_row(row):
            return [(ones[:, :], row)]

        class Attention:
            def __init__(self, take, heads, slot, vwidth, causal, mode, decay=None, two_steps=False):
                self.heads, self.slot, self.vwidth = heads, slot, vwidth
                self.causal, self.mode, self.decay = causal, mode, decay
                start = take.at
                self.nt = heads * slot // P
                self.nch = heads * vwidth // P
                self.qz = chunks(take(self.nt * (S + 1)), self.nt)
                self.q = self.qz[:, :, 1:]
                self.per_tile = P // slot
                self.k = chunks(take(heads * S), heads)
                self.mask = slots[slot]
                self.ktile = chunks(take(self.nt * S), self.nt) if two_steps else None
                self.v = chunks(take(NI * heads * vwidth), NI)
                self.p = take(4 * S).rearrange("p (g e s) -> p g e s", g=2, e=2)
                self.t = take(4 * S).rearrange("p (g e s) -> p g e s", g=2, e=2) if mode != "plain" else None
                self.pts = chunks(take(4 * S), 4)
                self.on = chunks(take(2 * heads * vwidth), 2)
                self.ot = chunks(take(self.nch * S), self.nch)
                self.sums = take(NI * heads)
                self.rsum = take(2 * heads)
                self.mx = take(4)
                self.nmx = take(4)
                self.rel = take(4 * 4 * S).rearrange("p (r h s) -> p r h s", r=4, h=4) if mode == "rel" else None
                self.size = take.at - start
                self.groups = [(i, h) for i in range(NI) for h in range(0, heads, 2)]
                self.per = heads // 2
                self.slots = []
                self.steps = max(len(self.groups) + 5, 0)
                for n in range(self.steps):
                    if 1 <= n <= len(self.groups):
                        self.slots += [("p", n - 1, 0), ("p", n - 1, 1)]
                    i = self.finishing(n, 3)
                    if i is not None:
                        self.slots.append(("o", i, 0))
                    i = self.finishing(n, 4)
                    if i is not None:
                        self.slots.append(("y", i, 0))
                self.reads = []
                d = s = 0
                for kind, _, e in self.slots:
                    on_act = kind == "p" and e == 1
                    d, s = d + (not on_act), s + on_act
                    self.reads.append((d, s, on_act))

            def keys(self, i):
                return (i + 1) * P if self.causal else S

            def keys_of(self, t):
                return self.k[:, t * self.per_tile:(t + 1) * self.per_tile]

            def finishing(self, n, lag):
                g = n - lag
                if 0 <= g < len(self.groups) + 0 and (g + 1) % self.per == 0:
                    return g // self.per
                return None

        def slot_read(at, s):
            d, c, on_act = at.reads[s]
            if on_act:
                nc.tensor.wait_ge(pt_act, c)
            else:
                nc.tensor.wait_ge(pt_dve, d)

        def attention_tensor(at, wo, width_of, bias):
            s = 0
            base = {}
            for n in range(at.steps):
                if n < len(at.groups):
                    i, h = at.groups[n]
                    kw = at.keys(i)
                    if n >= 2:
                        if at.mode == "plain":
                            nc.tensor.wait_ge(exp_ready, 2 * (n - 1))
                        else:
                            nc.tensor.wait_ge(max_ready, n - 1)
                    for e in range(2):
                        o = bank(2 * (n % 2) + e)
                        if at.ktile is not None and i == 0:
                            nc.tensor.wait_ge(keys_ready, h + e + 1)
                        last = nc.tensor.matmul(o[:, 0:kw], at.q[:, (h + e) // at.per_tile, i * P:(i + 1) * P],
                                                at.k[:, h + e, 0:kw], start=True, stop=not at.causal)
                        if at.causal:
                            last = nc.tensor.matmul(o[:, kw - P:kw], identb, upperb, start=False, stop=True)
                    last.then_inc(scores_ready, 1)
                if 1 <= n <= len(at.groups):
                    i, h = at.groups[n - 1]
                    for e in range(2):
                        nc.tensor.wait_ge(exp_ready, 2 * (n - 1) + e + 1)
                        if s >= 2:
                            slot_read(at, s - 2)
                        for kb in range(at.keys(i) // P):
                            last = nc.tensor.transpose(bank(4 + s % 2)[:, kb * P:(kb + 1) * P],
                                                       at.p[:, (n - 1) % 2, e, kb * P:(kb + 1) * P], ident)
                        last.then_inc(pt_ready, 1)
                        base[n - 1, e] = s
                        s += 1
                if 2 <= n <= len(at.groups) + 1:
                    i, h = at.groups[n - 2]
                    if h == 0 and i >= 2:
                        nc.tensor.wait_ge(on_ready, i - 1)
                    for e in range(2):
                        slot_read(at, base[n - 2, e])
                        vs = slice((h + e) * at.vwidth, (h + e + 1) * at.vwidth)
                        nk = at.keys(i) // P
                        for kb in range(nk):
                            last = nc.tensor.matmul(bank(6 + i % 2)[:, vs],
                                                    at.pts[:, (2 * (n - 2) + e) % 4, kb * P:(kb + 1) * P],
                                                    at.v[:, kb, vs], start=kb == 0, stop=kb == nk - 1)
                    if h + 2 == at.heads:
                        last.then_inc(o_ready, 1)
                i = at.finishing(n, 3)
                if i is not None:
                    nc.tensor.wait_ge(on_ready, i + 1)
                    slot_read(at, s - 2)
                    for c in range(at.nch):
                        last = nc.tensor.transpose(bank(4 + s % 2)[:, c * P:(c + 1) * P],
                                                   at.on[:, i % 2, c * P:(c + 1) * P], ident)
                    last.then_inc(pt_ready, 1)
                    base["o", i] = s
                    s += 1
                i = at.finishing(n, 4)
                if i is not None:
                    slot_read(at, base["o", i])
                    if s - 2 != base["o", i]:
                        slot_read(at, s - 2)
                    m = width_of(i)
                    o = bank(4 + s % 2)[:, 0:m]
                    if bias is not None:
                        nc.tensor.matmul(o, ones[:, :], bias[:, 0:m], start=True, stop=False)
                    full = m if m < D else at.nch * P
                    for c in range(-(-full // P)):
                        rows = min(P, full - c * P)
                        last = nc.tensor.matmul(o, at.ot[0:rows, c, i * P:(i + 1) * P], wo[0:rows, c, 0:m],
                                                start=bias is None and c == 0, stop=(c + 1) * P >= full)
                    last.then_inc(pt_ready, 1)
                    s += 1

        def keys_vector(at):
            nc.vector.wait_ge(proj_dve, at.tiles_done)
            for h in range(at.heads):
                nc.vector.tensor_scalar(at.k[:, h], at.ktile[:, h // at.per_tile],
                                        at.mask[:, h % at.per_tile:h % at.per_tile + 1], None, ALU.mult
                                        ).then_inc(keys_ready, 1)

        def attention_vector(at, width_of, add_to, base_of):
            s = 0
            later = []
            for n in range(at.steps):
                if n < len(at.groups):
                    i, h = at.groups[n]
                    kw = at.keys(i)
                    g = n % 2
                    nc.vector.wait_ge(scores_ready, n + 1)
                    if n >= 2:
                        nc.vector.wait_ge(exp_ready, 2 * (n - 1))
                    if at.mode == "plain":
                        o = bank(2 * g, 2).rearrange("p (e s) -> p e s", e=2)[:, :, 0:kw]
                        nc.vector.tensor_reduce(at.nmx[:, 2 * g:2 * g + 2], o, AX, ALU.min).then_inc(max_ready, 1)
                    elif at.mode == "decay":
                        for e in range(2):
                            last = nc.vector.tensor_tensor_reduce(
                                at.t[:, g, e, 0:kw], bank(2 * g + e)[:, 0:kw], at.decay[:, i, 0:kw], 1.0, -LOWEST,
                                ALU.mult, ALU.max, at.mx[:, 2 * g + e:2 * g + e + 1])
                        v.step(last)
                        v.settle()
                        nc.vector.tensor_scalar(at.nmx[:, 2 * g:2 * g + 2], at.mx[:, 2 * g:2 * g + 2], -1.0, None,
                                                ALU.mult).then_inc(max_ready, 1)
                    else:
                        if h % 4 == 0:
                            r = i * 4 + h // 4
                            nc.vector.wait_ge(rel_loaded[r % 4], 16 * (r // 4 + 1))
                        for e in range(2):
                            last = nc.vector.tensor_tensor_reduce(
                                at.t[:, g, e, 0:kw], bank(2 * g + e)[:, 0:kw],
                                at.rel[:, (i * 4 + h // 4) % 4, h % 4 + e, 0:kw], 1.0, LOWEST,
                                ALU.add, ALU.min, at.nmx[:, 2 * g + e:2 * g + e + 1])
                        last.then_inc(max_ready, 1)
                while s < len(at.slots) and (later or True):
                    kind, j, e = at.slots[s]
                    at_step = j + 1 if kind == "p" else (j + 1) * at.per - 1 + (3 if kind == "o" else 4)
                    if at_step > n:
                        break
                    if kind == "p" and e == 0:
                        kw = at.keys(at.groups[j][0])
                        nc.vector.wait_ge(pt_ready, s + 1)
                        nc.vector.tensor_copy(at.pts[:, (2 * j) % 4, 0:kw], bank(4 + s % 2)[:, 0:kw]).then_inc(pt_dve, 1)
                    elif kind == "o":
                        nc.vector.wait_ge(pt_ready, s + 1)
                        nc.vector.tensor_copy(at.ot[:, :, j * P:(j + 1) * P],
                                              bank(4 + s % 2)[:, 0:at.nch * P].rearrange("p (c q) -> p c q", q=P)
                                              ).then_inc(pt_dve, 1)
                    elif kind == "y":
                        m = width_of(j)
                        nc.vector.wait_ge(pt_ready, s + 1)
                        nc.vector.tensor_tensor(add_to[:, j, 0:m], bank(4 + s % 2)[:, 0:m], base_of[:, j, 0:m],
                                                ALU.add).then_inc(pt_dve, 1)
                    s += 1
                i = at.finishing(n, 2)
                if i is not None:
                    nc.vector.wait_ge(exp_ready, 2 * (i + 1) * at.per)
                    rs = at.rsum[:, (i % 2) * at.heads:(i % 2 + 1) * at.heads]
                    v.step(nc.vector.reciprocal(rs, at.sums[:, i * at.heads:(i + 1) * at.heads]))
                    nc.vector.wait_ge(o_ready, i + 1)
                    v.settle()
                    nc.vector.tensor_tensor(
                        at.on[:, i % 2].rearrange("p (h d) -> p h d", h=at.heads),
                        bank(6 + i % 2)[:, 0:at.heads * at.vwidth].rearrange("p (h d) -> p h d", h=at.heads),
                        rs.rearrange("p (h o) -> p h o", o=1).to_broadcast([P, at.heads, at.vwidth]),
                        ALU.mult).then_inc(on_ready, 1)

        def attention_scalar(at):
            s = 0
            for n in range(at.steps):
                if n < len(at.groups):
                    i, h = at.groups[n]
                    kw = at.keys(i)
                    g = n % 2
                    nc.scalar.wait_ge(max_ready, n + 1)
                    if n >= 2:
                        k = [q for q, (kind, j, e) in enumerate(at.slots) if kind == "p" and j == n - 2][-1]
                        nc.scalar.wait_ge(pt_ready, k + 1)
                    for e in range(2):
                        src = bank(2 * g + e)[:, 0:kw] if at.mode == "plain" else at.t[:, g, e, 0:kw]
                        nc.scalar.activation(at.p[:, g, e, 0:kw], src, ACT.Exp,
                                             bias=at.nmx[:, 2 * g + e:2 * g + e + 1],
                                             scale=1.0 if at.mode == "decay" else -1.0,
                                             accum_out=at.sums[:, i * at.heads + h + e:i * at.heads + h + e + 1]
                                             ).then_inc(exp_ready, 1)
                for q, (kind, j, e) in enumerate(at.slots):
                    if kind == "p" and e == 1 and j == n - 1:
                        kw = at.keys(at.groups[j][0])
                        nc.scalar.wait_ge(pt_ready, q + 1)
                        nc.scalar.activation(at.pts[:, (2 * j + 1) % 4, 0:kw], bank(4 + q % 2)[:, 0:kw],
                                             ACT.Copy).then_inc(pt_act, 1)

        def rank_vector(score, rank, groups, n, tri, work):
            gt, eq = (w[:, 0:groups * n * n].rearrange("p (g e r) -> p g e r", g=groups, e=n) for w in work)
            rival = score.rearrange("p g (o r) -> p g o r", o=1).to_broadcast([P, groups, n, n])
            own = score.rearrange("p g (e o) -> p g e o", o=1).to_broadcast([P, groups, n, n])
            low = tri.rearrange("p (o e r) -> p o e r", o=1, e=n).to_broadcast([P, groups, n, n])
            nc.vector.tensor_tensor(gt, rival, own, ALU.is_gt)
            v.step(nc.vector.tensor_tensor(eq, rival, own, ALU.is_equal))
            v.settle()
            v.step(nc.vector.tensor_tensor(eq, eq, low, ALU.mult))
            v.settle()
            v.step(nc.vector.tensor_tensor(gt, gt, eq, ALU.add))
            v.settle()
            v.step(nc.vector.tensor_reduce(rank, gt, AX, ALU.add))
            v.settle()

        def over(ap, shape):
            return ap.rearrange("p (g o) -> p g o", o=1).to_broadcast(shape)

        def softmax_router_vector(r, experts, keep, weigh, tri):
            e3 = [P, NI, experts]
            lg = bank(7)[:, 0:NI * experts].rearrange("p (i e) -> p i e", i=NI)
            nc.vector.wait_ge(logits_ready, 1)
            v.step(nc.vector.tensor_reduce(r.a4, lg, AX, ALU.max))
            v.settle()
            nc.vector.tensor_tensor(r.e, lg, over(r.a4, e3), ALU.subtract).then_inc(router_in, 1)
            nc.vector.wait_ge(router_exp, 1)
            v.step(nc.vector.tensor_reduce(r.a4, r.e, AX, ALU.add))
            v.settle()
            v.step(nc.vector.reciprocal(r.b4, r.a4))
            v.settle()
            v.step(nc.vector.tensor_tensor(r.e, r.e, over(r.b4, e3), ALU.mult))
            v.settle()
            rank_vector(r.e, r.rank, NI, experts, tri, r.work)
            if weigh:
                v.step(nc.vector.scalar_tensor_tensor(out=r.e, in0=r.rank, scalar=float(keep), in1=r.e,
                                                      op0=ALU.is_lt, op1=ALU.mult))
                v.settle()
                v.step(nc.vector.tensor_reduce(r.a4, r.e, AX, ALU.add))
                v.settle()
                v.step(nc.vector.reciprocal(r.b4, r.a4))
                v.settle()
                nc.vector.tensor_tensor(r.comb, r.e, over(r.b4, e3), ALU.mult).then_inc(comb_ready, 1)
            else:
                nc.vector.tensor_scalar(r.comb, r.rank, float(keep), None, ALU.is_lt).then_inc(comb_ready, 1)
            combt_vector(r, experts)

        def combt_vector(r, experts):
            nc.vector.memset(r.parts[0:96], 0.0)
            nc.vector.wait_ge(comb_turned, 1)
            v.step(nc.vector.tensor_copy(r.combt[0:experts], bank(6)[0:experts, 0:S]))
            v.settle()
            split_vector(r.combt[0:experts], experts, r.parts, (0, 32, 64), r.rest[0:experts],
                         r.second[0:experts]).then_inc(combt_ready, 1)

        def router_scalar(r, scale):
            nc.scalar.wait_ge(router_in, 1)
            nc.scalar.activation(r.e, r.e, ACT.Exp, scale=scale).then_inc(router_exp, 1)

        def router_tensor(r, src, gate, bias, experts):
            for i in range(NI):
                o = bank(7)[:, i * experts:(i + 1) * experts]
                if bias is not None:
                    nc.tensor.matmul(o, ones[:, :], bias[:, 0:experts], start=True, stop=False)
                nch = gate.shape[1]
                for c in range(nch):
                    last = nc.tensor.matmul(o, src[:, c, i * P:(i + 1) * P], gate[:, c, 0:experts],
                                            start=bias is None and c == 0, stop=c == nch - 1)
            last.then_inc(logits_ready, 1)

        def comb_tensor(r, experts):
            nc.tensor.wait_ge(comb_ready, 1)
            for i in range(NI):
                last = nc.tensor.transpose(bank(6)[0:experts, i * P:(i + 1) * P], r.comb[:, i], ident)
            last.then_inc(comb_turned, 1)
            nc.tensor.wait_ge(combt_ready, 1)

        class Router:
            def __init__(self, take, experts):
                t3 = lambda: chunks(take(NI * experts), NI)
                self.e, self.rank, self.comb, self.f, self.g = t3(), t3(), t3(), t3(), t3()
                self.work = [take(NI * experts * experts) for _ in range(2)]
                self.a4, self.b4 = take(4), take(4)
                self.gs, self.gr = take(16), take(16)
                self.combt, self.rest, self.second = take(S), take(S), take(S // 2).bitcast(BF16)
                self.parts = take(S // 2).bitcast(BF16)

        class Experts:
            def __init__(self, take, r, w, routed, shared, experts):
                self.r, self.shared, self.n, self.experts = r, shared, routed + shared, experts
                self.wg, self.wu = (w[k].rearrange("p (t c n) -> p t c n", t=self.n, c=NC) for k in ("e_g", "e_u"))
                self.wd = chunks(w["e_d"], self.n)
                self.select = w["select_b"].rearrange("p (t n) -> p t n", n=P)
                self.s = chunks(take(2 * S), 2)
                self.h = chunks(take(2 * S), 2)
                self.hw = chunks(take(self.n * S), self.n)

        def experts_tensor(x, src):
            for j in range(x.n):
                b = 3 * (j % 2)
                if j == min(x.shared, 2):
                    comb_tensor(x.r, x.experts)
                if j >= 2:
                    nc.tensor.wait_ge(hidden_ready, j - 1)
                for k, w in enumerate((x.wg, x.wu)):
                    for c in range(NC):
                        last = nc.tensor.matmul(bank(b + k), w[:, j, c], src[:, c], start=c == 0, stop=c == NC - 1)
                if j >= x.shared:
                    last = nc.tensor.matmul(bank(b + 2), x.select[0:96, j - x.shared], x.r.parts[0:96], start=True, stop=True)
                last.then_inc(gate_ready, 1)
            nc.tensor.wait_ge(hidden_ready, x.n)
            for i in range(NI):
                if i >= 2:
                    nc.tensor.wait_ge(down_done, i - 1)
                for j in range(x.n):
                    last = nc.tensor.matmul(bank(6 + i % 2)[:, 0:D], x.hw[:, j, i * P:(i + 1) * P], x.wd[:, j],
                                            start=j == 0, stop=j == x.n - 1)
                last.then_inc(down_ready, 1)

        def experts_scalar(x):
            for j in range(x.n):
                nc.scalar.wait_ge(gate_ready, j + 1)
                if j >= 2:
                    nc.scalar.wait_ge(hidden_ready, j - 1)
                nc.scalar.activation(x.s[:, j % 2], bank(3 * (j % 2)), ACT.Silu).then_inc(silu_ready, 1)

        def experts_vector(x):
            for j in range(x.n):
                b = 3 * (j % 2)
                nc.vector.wait_ge(silu_ready, j + 1)
                if j >= x.shared:
                    v.step(nc.vector.tensor_tensor(x.h[:, j % 2], x.s[:, j % 2], bank(b + 1), ALU.mult))
                    v.settle()
                    last = nc.vector.tensor_tensor(x.hw[:, j], x.h[:, j % 2], bank(b + 2), ALU.mult)
                else:
                    last = nc.vector.tensor_tensor(x.hw[:, j], x.s[:, j % 2], bank(b + 1), ALU.mult)
                last.then_inc(hidden_ready, 1)

        def down_vector(base):
            for i in range(NI):
                nc.vector.wait_ge(down_ready, i + 1)
                nc.vector.tensor_tensor(X[:, i], bank(6 + i % 2)[:, 0:D], base[:, i], ALU.add).then_inc(down_done, 1)

        def tokens(dram, b):
            return dram[bass.ds(b * S, S), :].rearrange("(i p) d -> p i d", p=P)

        def load_x(b, src):
            nc.sync.dma_start(X, tokens(src, b)).then_inc(x_loaded, 16)
            nc.sync.wait_ge(x_loaded, 16)

        def store_x(b, dst, ready, count, buffer):
            nc.sync.wait_ge(ready, count)
            nc.sync.dma_start(tokens(dst, b), buffer).then_inc(x_stored, 16)
            nc.sync.wait_ge(x_stored, 16)

        whole = lambda i: D

        def plan0():
            w, end = views(0)
            A = Place()
            take = Taker(end)
            A.at = Attention(take, 16, 16, 16, False, "decay", chunks(w["decay"], NI))
            kv, lat = chunks(take(2 * S), 2), take(S)
            wq, wk, wv = chunks(w["a_q"], 2), chunks(w["a_k"], 2), chunks(w["a_v"], 2)
            down, upk, upv = chunks(w["a_down"], 2), w["a_upk"], w["a_upv"]
            col = lambda t: slice(t * P, (t + 1) * P)
            tiles = [(feature_tile(wk, XT, col(t)) + feature_tile(wv, XT, col(t)), kv[:, t], {}, None) for t in range(2)]
            tiles += [(feature_tile(wq, XT, col(t)), A.at.q[:, t], {"mul": 1 / 16}, None) for t in range(2)]
            tiles += [(feature_tile(down, kv, slice(0, 64)), lat[0:64], {}, 1)]
            A.lat = lat
            tiles += [([(upk[:, col(t)], lat)], A.at.keys_of(t), {"spread": A.at.mask}, 4) for t in range(2)]
            tiles += [([(lat[:, col(i)], upv)], A.at.v[:, i], {}, None) for i in range(NI)]
            A.tiles = Tiles([(p, d, y, n if n is None or k - 4 <= n else k - 4) for k, (p, d, y, n) in enumerate(tiles)])
            A.wo = chunks(w["a_o"], 2)

            B = Place()
            take = Taker(end)
            B.at = Attention(take, 16, 64, 32, True, "plain")
            B.r1 = chunks(take(NI * D), NI)
            B.r1t = chunks(take(NC * S), NC)
            B.lkr = take(S)
            B.sin = chunks(take(2 * S), 2)
            B.x2 = chunks(take(NI * D), NI)
            fq, kva, k2, kvb = chunks(w["f_q"], 2), chunks(w["f_kva"], 2), w["f_k2"], w["f_kvb"]
            tiles = [(feature_tile(kva, B.r1t, slice(0, 64)), B.lkr[0:64], {}, None)]
            tiles += [(feature_tile(fq, B.r1t, col(t)), B.at.q[:, t], {"mul": -1 / 8}, None) for t in range(8)]
            B.first = Tiles(tiles)
            B.rope = [B.lkr[0:64]] + [B.at.q[:, t] for t in range(8)]
            tiles = [([(k2[:, col(t)], B.lkr)], B.at.keys_of(t), {"spread": B.at.mask}, None) for t in range(8)]
            tiles += [([(B.lkr[:, col(i)], kvb)], B.at.v[:, i], {}, None) for i in range(NI)]
            B.second = Tiles(tiles, B.first)
            B.wo = chunks(w["f_o"], 4)
            take = Taker(end)
            B.router = Router(take, 8)
            B.experts = Experts(take, B.router, w, 8, 1, 8)
            assert take.at <= end + B.at.size
            B.w = w
            return A, B

        def rope_tensor(B):
            for n, t in enumerate(B.rope):
                tiles_there(nc.tensor, B.first, n)
                if n == 0:
                    tiles_there(nc.tensor, B.first)
                if n >= 2:
                    nc.tensor.wait_ge(sin_done, n - 1)
                rows = t.shape[0]
                nc.tensor.matmul(bank(4 + n % 2)[0:rows], B.w["swap"][0:rows, 0:rows], t, start=True, stop=True
                                 ).then_inc(swapped, 1)

        def rope_gpsimd(B):
            for n, t in enumerate(B.rope):
                nc.gpsimd.wait_ge(swapped, n + 1)
                nc.gpsimd.tensor_tensor(t, t, B.w["cos"][0:t.shape[0]], ALU.mult).then_inc(cos_done, 1)

        def rope_vector(B):
            for n in range(len(B.rope) + 1):
                if n < len(B.rope):
                    rows = B.rope[n].shape[0]
                    nc.vector.wait_ge(swapped, n + 1)
                    if n >= 2:
                        nc.vector.wait_ge(roped, n - 1)
                    nc.vector.tensor_tensor(B.sin[0:rows, n % 2], bank(4 + n % 2)[0:rows], B.w["sin"][0:rows],
                                            ALU.mult).then_inc(sin_done, 1)
                if n >= 1:
                    t = B.rope[n - 1]
                    nc.vector.wait_ge(cos_done, n)
                    nc.vector.wait_ge(sin_done, n)
                    nc.vector.tensor_tensor(t, t, B.sin[0:t.shape[0], (n - 1) % 2], ALU.add).then_inc(roped, 1)

        def block0(e, b, A, B, src, dst):
            w = B.w
            if e is nc.sync:
                load_x(b, src)
                meet(e, 0)
                store_x(b, dst, down_done, NI, X)
                meet(e, 1)
            if e is nc.gpsimd:
                meet(e, 0)
                rope_gpsimd(B)
                meet(e, 1)
            if e is nc.tensor:
                norm_tensor(0, XN)
                turned_there(e, 0)
                tiles_tensor(A.tiles)
                tiles_there(e, A.tiles)
                attention_tensor(A.at, A.wo, whole, None)
                meet(e, 0)
                norm_tensor(0, B.r1)
                turned_there(e, 0)
                tiles_tensor(B.first)
                rope_tensor(B)
                e.wait_ge(roped, 1)
                tiles_tensor(B.second)
                tiles_there(e, B.second)
                e.wait_ge(roped, 9)
                attention_tensor(B.at, B.wo, whole, None)
                norm_tensor(1, B.r1)
                turned_there(e, 1)
                router_tensor(B.router, B.r1t, chunks(w["gate"], 2), w["gate_b"], 8)
                experts_tensor(B.experts, B.r1t)
                meet(e, 1)
            if e is nc.scalar:
                norm_scalar(0, XT)
                tiles_scalar(A.tiles)
                attention_scalar(A.at)
                meet(e, 0)
                norm_scalar(0, B.r1t, w["ln1"])
                tiles_scalar(B.first)
                tiles_scalar(B.second)
                attention_scalar(B.at)
                norm_scalar(1, B.r1t, w["ln2"])
                router_scalar(B.router, 1.0)
                experts_scalar(B.experts)
                meet(e, 1)
            if e is nc.vector:
                nc.vector.memset(A.lat[64:128], 0.0)
                e.wait_ge(x_loaded, 16)
                norm_vector(0, X, False, XN, XT)
                tiles_vector(A.tiles)
                attention_vector(A.at, whole, ACC, X)
                meet(e, 0)
                nc.vector.memset(B.lkr[64:128], 0.0)
                norm_vector(0, XN, True, B.r1, B.r1t, w["ln1"])
                tiles_vector(B.first)
                rope_vector(B)
                tiles_vector(B.second)
                attention_vector(B.at, whole, B.x2, XN)
                nc.vector.wait_ge(pt_dve, B.at.reads[-1][0])
                v.step(nc.vector.tensor_tensor(ACC, ACC, B.x2, ALU.add))
                norm_vector(1, B.x2, True, B.r1, B.r1t, w["ln2"])
                softmax_router_vector(B.router, 8, 2, True, w["tri"])
                experts_vector(B.experts)
                down_vector(ACC)
                meet(e, 1)

        class Scan:

            def __init__(self, take):
                four = lambda: chunks(take(NT * S), NT)
                two = lambda: take(2 * NT * S).rearrange("p (g t s) -> p g t s", g=2, t=NT)
                self.h, self.r = chunks(take(NI * D), NI), chunks(take(NI * D), NI)
                self.rt = chunks(take(NC * S), NC)
                self.xi = chunks(take(NT * (S + 4)), NT)
                self.c, self.u, self.z, self.delta, self.du, self.soft = (four() for _ in range(6))
                self.dbc, self.rest, self.second = take(S), take(S), take(S // 2).bitcast(BF16)
                self.bc = take(S // 2).bitcast(BF16)
                self.da, self.dbx, self.hs, self.hc = (two() for _ in range(4))
                self.ae, self.aneg = take(NT * NS), take(NT * NS)

        def plan_scan(sc, w, i, before):
            L = Place()
            n = f"m{i}_"
            L.cw, L.cb, L.a_log, L.d, L.norm = (w[n + k] for k in ("cw", "cb", "A", "D", "norm"))
            L.out = chunks(w[n + "out"], NT)
            w_in, wx, wdt = chunks(w[n + "in"], NC), chunks(w[n + "x"], NT), w[n + "dt"]
            col = lambda t: slice(t * P, (t + 1) * P)
            tiles = []
            for t in range(NT):
                tiles.append((feature_tile(w_in, sc.rt, col(t)), sc.xi[:, t, KC - 1:KC - 1 + S], {}, None))
                tiles.append((feature_tile(w_in, sc.rt, col(NT + t)), sc.z[:, t], {"silu": 1}, None))
            L.first = Tiles(tiles, before)
            tiles = [(feature_tile(wx, sc.u, slice(0, DTR + 2 * NS)), sc.dbc[0:DTR + 2 * NS], {}, None)]
            rows = slice(0, DTR + 2 * NS)
            tiles += [([(wdt[rows, col(t)], sc.dbc[rows])], sc.c[:, t], {"col": w[n + "dtb"][:, t:t + 1]}, 0)
                      for t in range(NT)]
            L.second = Tiles(tiles, L.first)
            return L

        def one_hot(row):
            return three[:, row:row + 1].to_broadcast([96, P])

        def split_vector(x, rows, parts, at_rows, rest, second):
            first = parts[at_rows[0]:at_rows[0] + rows]
            v.step(nc.vector.tensor_copy(first, x))
            v.settle()
            v.step(nc.vector.tensor_tensor(rest, x, first, ALU.subtract))
            v.settle()
            v.step(nc.vector.tensor_copy(second, rest))
            v.settle()
            nc.vector.tensor_copy(parts[at_rows[1]:at_rows[1] + rows], second)
            return nc.vector.tensor_tensor(parts[at_rows[2]:at_rows[2] + rows], rest, second, ALU.subtract)

        def scan_tensor(sc, L, i):
            norm_tensor(i + 1, sc.r)
            turned_there(nc.tensor, i + 1)
            tiles_tensor(L.first)
            nc.tensor.wait_ge(u_ready, NT * (i + 1))
            tiles_tensor(L.second)
            tiles_there(nc.tensor, L.second)
            at = NS * i
            for n in range(NS + 1):
                if n < NS:
                    if at + n >= 2:
                        nc.tensor.wait_ge(dbx_done, at + n - 1)
                    if n == 0:
                        nc.tensor.wait_ge(split_ready, i + 1)
                    nc.tensor.matmul(bank(4 + n % 2), one_hot(n), sc.bc[0:96],
                                     start=True, stop=True).then_inc(b_ready, 1)
                    if at + n >= 2:
                        nc.tensor.wait_ge(hc_done, at + n - 1)
                    nc.tensor.matmul(bank(6 + n % 2), one_hot(NS + n), sc.bc[0:96],
                                     start=True, stop=True).then_inc(c_ready, 1)
                if n >= 1:
                    nc.tensor.wait_ge(hc_done, at + n)
                    for t in range(NT):
                        last = nc.tensor.matmul(bank(t), ident, sc.hc[:, (n - 1) % 2, t],
                                                start=n == 1, stop=n == NS)
                    last.then_inc(y_added, 1)
            nc.tensor.wait_ge(y_ready, i + 1)
            for j in range(NI):
                if NI * i + j >= 2:
                    nc.tensor.wait_ge(down_done, NI * i + j - 1)
                for t in range(NT):
                    last = nc.tensor.matmul(bank(4 + j % 2)[:, 0:D], sc.c[:, t, j * P:(j + 1) * P], L.out[:, t],
                                            start=t == 0, stop=t == NT - 1)
                last.then_inc(down_ready, 1)

        def scan_scalar(sc, L, i):
            norm_scalar(i + 1, sc.rt, L.norm)
            tiles_scalar(L.first)
            for t in range(NT):
                nc.scalar.wait_ge(conv_ready, NT * i + t + 1)
                nc.scalar.activation(sc.u[:, t], sc.c[:, t], ACT.Silu).then_inc(u_ready, 1)
            a.step(nc.scalar.activation(sc.ae, L.a_log, ACT.Exp))
            a.settle()
            a.step(nc.scalar.activation(sc.aneg, sc.ae, ACT.Copy, scale=-1.0))
            tiles_there(nc.scalar, L.second)
            a.step(nc.scalar.activation(sc.soft, sc.c, ACT.Abs))
            a.settle()
            a.step(nc.scalar.activation(sc.soft, sc.soft, ACT.Exp, scale=-1.0))
            a.settle()
            nc.scalar.activation(sc.soft, sc.soft, ACT.Ln, bias=1.0).then_inc(soft_log, 1)
            nc.scalar.wait_ge(delta_ready, i + 1)
            at = NS * i
            for n in range(NS):
                if at + n >= 2:
                    nc.scalar.wait_ge(scan_done, at + n - 1)
                for t in range(NT):
                    last = nc.scalar.activation(sc.da[:, n % 2, t, 1:S], sc.delta[:, t, 1:S], ACT.Exp,
                                                scale=sc.aneg[:, t * NS + n:t * NS + n + 1])
                last.then_inc(da_ready, 1)

        def scan_vector(sc, L, i, h_in):
            norm_vector(i + 1, h_in, True, sc.r, sc.rt, L.norm)
            tiles_vector(L.first)
            nc.vector.wait_ge(proj_dve, L.first.end[1])
            for k in range(KC):
                for t in range(NT):
                    src, tap = sc.xi[:, t, k:k + S], L.cw[:, t * KC + k:t * KC + k + 1]
                    if k == 0:
                        last = nc.vector.tensor_scalar(sc.c[:, t], src, tap, L.cb[:, t:t + 1], ALU.mult, ALU.add)
                    else:
                        last = nc.vector.scalar_tensor_tensor(out=sc.c[:, t], in0=src, scalar=tap, in1=sc.c[:, t],
                                                              op0=ALU.mult, op1=ALU.add)
                    if k == KC - 1:
                        last.then_inc(conv_ready, 1)
                if k < KC - 1:
                    v.step(last)
                    v.settle()
            nc.vector.wait_ge(u_ready, NT * (i + 1))
            tiles_vector(L.second)
            nc.vector.wait_ge(proj_dve, L.second.through[0][0])
            if i:
                nc.vector.wait_ge(y_added, NS * i)
            bc = slice(DTR, DTR + 2 * NS)
            split_vector(sc.dbc[bc], 2 * NS, sc.bc, (64, 32, 0), sc.rest[bc], sc.second[bc]).then_inc(split_ready, 1)
            nc.vector.wait_ge(soft_log, i + 1)
            nc.vector.scalar_tensor_tensor(out=sc.delta, in0=sc.c, scalar=0.0, in1=sc.soft,
                                           op0=ALU.max, op1=ALU.add).then_inc(delta_ready, 1)
            nc.vector.wait_ge(delta_ready, i + 1)
            v.step(nc.vector.tensor_tensor(sc.du, sc.delta, sc.u, ALU.mult))
            v.settle()
            at = NS * i
            flat = lambda w: w.rearrange("p t s -> p (t s)")
            for n in range(NS + 1):
                if n < NS:
                    nc.vector.wait_ge(b_ready, at + n + 1)
                    if at + n >= 2:
                        nc.vector.wait_ge(scan_done, at + n - 1)
                    nc.vector.tensor_tensor(sc.dbx[:, n % 2], sc.du,
                                            bank(4 + n % 2).rearrange("p (o s) -> p o s", o=1).to_broadcast([P, NT, S]),
                                            ALU.mult).then_inc(dbx_done, 1)
                if n >= 1:
                    m = n - 1
                    nc.vector.wait_ge(scan_done, at + n)
                    nc.vector.wait_ge(c_ready, at + n)
                    if at + m >= 2:
                        nc.vector.wait_ge(y_added, at + m - 1)
                    nc.vector.tensor_tensor(sc.hc[:, m % 2], sc.hs[:, m % 2],
                                            bank(6 + m % 2).rearrange("p (o s) -> p o s", o=1).to_broadcast([P, NT, S]),
                                            ALU.mult).then_inc(hc_done, 1)
                if n < NS:
                    nc.vector.wait_ge(da_ready, at + n + 1)
                    nc.vector.wait_ge(dbx_done, at + n + 1)
                    if at + n >= 2:
                        nc.vector.wait_ge(hc_done, at + n - 1)
                    nc.vector.tensor_tensor_scan(flat(sc.hs[:, n % 2]), flat(sc.da[:, n % 2]), flat(sc.dbx[:, n % 2]),
                                                 0.0, ALU.mult, ALU.add).then_inc(scan_done, 1)
            nc.vector.wait_ge(y_added, at + NS)
            for t in range(NT):
                last = nc.vector.scalar_tensor_tensor(out=sc.c[:, t], in0=sc.u[:, t], scalar=L.d[:, t:t + 1],
                                                      in1=bank(t), op0=ALU.mult, op1=ALU.add)
            v.step(last)
            v.settle()
            nc.vector.tensor_tensor(sc.c, sc.c, sc.z, ALU.mult).then_inc(y_ready, 1)
            for j in range(NI):
                nc.vector.wait_ge(down_ready, NI * i + j + 1)
                nc.vector.tensor_tensor(sc.h[:, j], bank(4 + j % 2)[:, 0:D], h_in[:, j], ALU.add).then_inc(down_done, 1)
            nc.vector.wait_ge(down_done, NI * (i + 1))

        def plan1():
            w, end = views(1)
            A = Place()
            A.scan = Scan(Taker(end))
            A.layers = []
            for i in range(NL):
                A.layers.append(plan_scan(A.scan, w, i, A.layers[-1].second if A.layers else None))
            B = Place()
            take = Taker(end)
            B.at = Attention(take, 8, 32, 32, False, "plain", two_steps=True)
            B.l, B.lt = chunks(take(NI * D), NI), chunks(take(NC * S), NC)
            fq, fk, fv = (chunks(w["f_" + n], 2) for n in "qkv")
            def rows(i):
                return [(c, min(P, (D >> i) - c * P)) for c in range(-(-(D >> i) // P))]
            tiles = []
            for wt, dst, bias, mul in ((fk, B.at.ktile, w["f_kb"], 1.0), (fq, B.at.q, w["f_qb"], -1 / 16)):
                for t in range(2):
                    for i in range(NI):
                        blk = slice(i * P, (i + 1) * P)
                        tiles.append(([(wt[0:m, c, t * P:(t + 1) * P], B.lt[0:m, c, blk]) for c, m in rows(i)],
                                      dst[:, t, blk], {"col": bias[:, t:t + 1], "mul": mul}, None))
            for i in range(NI):
                blk = slice(i * P, (i + 1) * P)
                tiles.append((bias_row(w["f_vb"]) + [(B.lt[0:m, c, blk], fv[0:m, c, :]) for c, m in rows(i)],
                              B.at.v[:, i], {}, None))
            B.tiles = Tiles(tiles)
            B.at.tiles_done = B.tiles.end[1]
            B.wo = chunks(w["f_o"], 2)
            B.w = w
            return A, B

        def block1(e, b, A, B, src, dst):
            w = B.w
            narrow = lambda i: D >> i
            if e is nc.sync:
                load_x(b, src)
                meet(e, 0)
                store_x(b, dst, pt_dve, B.at.reads[-1][0], ACC)
                meet(e, 1)
            if e is nc.gpsimd:
                meet(e, 0)
                meet(e, 1)
            if e is nc.tensor:
                norm_tensor(0, XN)
                turned_there(e, 0)
                for i in range(NL):
                    scan_tensor(A.scan, A.layers[i], i)
                meet(e, 0)
                norm_tensor(0, B.l)
                turned_there(e, 0)
                tiles_tensor(B.tiles)
                tiles_there(e, B.tiles)
                attention_tensor(B.at, B.wo, narrow, w["f_ob"])
                meet(e, 1)
            if e is nc.scalar:
                norm_scalar(0, XT)
                for i in range(NL):
                    scan_scalar(A.scan, A.layers[i], i)
                meet(e, 0)
                norm_scalar(0, B.lt, w["norm_w"], w["norm_b"])
                tiles_scalar(B.tiles)
                attention_scalar(B.at)
                meet(e, 1)
            if e is nc.vector:
                e.wait_ge(x_loaded, 16)
                norm_vector(0, X, False, XN, XT)
                nc.vector.memset(A.scan.xi[:, :, 0:KC - 1], 0.0)
                v.step(nc.vector.memset(A.scan.da[:, :, :, 0:1], 0.0))
                v.settle()
                for i in range(NL):
                    scan_vector(A.scan, A.layers[i], i, XN if i == 0 else A.scan.h)
                v.step(nc.vector.tensor_tensor(ACC, X, A.scan.h, ALU.add))
                v.settle()
                v.step(nc.vector.tensor_tensor(ACC, ACC, XN, ALU.add))
                meet(e, 0)
                norm_vector(0, XN, False, B.l, B.lt, w["norm_w"], w["norm_b"])
                tiles_vector(B.tiles)
                keys_vector(B.at)
                attention_vector(B.at, narrow, ACC, ACC)
                meet(e, 1)

        def plan2():
            w, end = views(2)
            A = Place()
            take = Taker(end)
            A.at = Attention(take, 16, 32, 16, True, "plain", two_steps=True)
            wq, wk, wv = chunks(w["a_q"], 2), chunks(w["a_k"], 2), chunks(w["a_v"], 2)
            alibi = chunks(w["alibi"], 4)
            col = lambda t: slice(t * P, (t + 1) * P)
            tiles = []
            for t in range(4):
                tiles.append((feature_tile(wk, XT, col(t)), A.at.ktile[:, t],
                              {"col": w["a_kb"][:, t:t + 1], "plus": alibi[:, t]}, None))
            for t in range(4):
                tiles.append((feature_tile(wq, XT, col(t)), A.at.q[:, t],
                              {"col": w["a_qb"][:, t:t + 1], "mul": -1 / 4}, None))
                tiles.append((bias_row(w["a_vb"]) + token_tile(XT, wv, t, slice(0, D)), A.at.v[:, t], {}, None))
            A.tiles = Tiles(tiles)
            A.at.tiles_done = A.tiles.end[1]
            A.wo = chunks(w["a_o"], 2)
            B = Place()
            take = Taker(end)
            B.router = Router(take, 16)
            B.experts = Experts(take, B.router, w, 8, 4, 16)
            B.w = w
            return A, B

        def group_router_vector(r, w):
            e3, g3 = [P, NI, 16], [P, 16, 4]
            by_group = lambda ap: ap.rearrange("p i (g e) -> p (i g) e", g=4)
            lg = bank(7)[:, 0:NI * 16].rearrange("p (i e) -> p i e", i=NI)
            nc.vector.wait_ge(logits_ready, 1)
            nc.vector.tensor_copy(r.e, lg).then_inc(router_in, 1)
            nc.vector.wait_ge(router_exp, 1)
            v.step(nc.vector.tensor_scalar(r.e, r.e, 1.0, None, ALU.add))
            v.settle()
            v.step(nc.vector.reciprocal(r.f, r.e))
            v.settle()
            bias = w["bias"].rearrange("p (o e) -> p o e", o=1).to_broadcast(e3)
            v.step(nc.vector.tensor_tensor(r.g, r.f, bias, ALU.add))
            v.settle()
            rank_vector(by_group(r.g), by_group(r.rank), 16, 4, w["tri4"], r.work)
            v.step(nc.vector.scalar_tensor_tensor(out=r.e, in0=r.rank, scalar=2.0, in1=r.g, op0=ALU.is_lt, op1=ALU.mult))
            v.settle()
            v.step(nc.vector.tensor_reduce(r.gs, by_group(r.e), AX, ALU.add))
            v.settle()
            rank_vector(chunks(r.gs, NI), chunks(r.gr, NI), NI, 4, w["tri4"], r.work)
            v.step(nc.vector.tensor_scalar(r.gr, r.gr, 2.0, None, ALU.is_lt))
            v.settle()
            v.step(nc.vector.tensor_scalar(r.gs, r.gr, -1.0, LOWEST, ALU.add, ALU.mult))
            v.step(nc.vector.tensor_tensor(by_group(r.e), by_group(r.g), over(r.gr, g3), ALU.mult))
            v.settle()
            v.step(nc.vector.tensor_tensor(by_group(r.e), by_group(r.e), over(r.gs, g3), ALU.add))
            v.settle()
            rank_vector(r.e, r.rank, NI, 16, w["tri16"], r.work)
            v.step(nc.vector.scalar_tensor_tensor(out=r.e, in0=r.rank, scalar=4.0, in1=r.f, op0=ALU.is_lt, op1=ALU.mult))
            v.settle()
            v.step(nc.vector.tensor_reduce(r.a4, r.e, AX, ALU.add))
            v.settle()
            v.step(nc.vector.tensor_scalar(r.a4, r.a4, 1e-20, None, ALU.add))
            v.settle()
            v.step(nc.vector.reciprocal(r.b4, r.a4))
            v.settle()
            nc.vector.tensor_tensor(r.comb, r.e, over(r.b4, e3), ALU.mult).then_inc(comb_ready, 1)
            combt_vector(r, 16)

        def block2(e, b, A, B, src, dst):
            w = B.w
            if e is nc.sync:
                load_x(b, src)
                meet(e, 0)
                store_x(b, dst, down_done, NI, X)
                meet(e, 1)
            if e is nc.gpsimd:
                meet(e, 0)
                meet(e, 1)
            if e is nc.tensor:
                norm_tensor(0, XN)
                turned_there(e, 0)
                tiles_tensor(A.tiles)
                tiles_there(e, A.tiles)
                attention_tensor(A.at, A.wo, whole, w["a_ob"])
                meet(e, 0)
                router_tensor(B.router, XT, chunks(w["gate"], 2), None, 16)
                experts_tensor(B.experts, XT)
                meet(e, 1)
            if e is nc.scalar:
                norm_scalar(0, XT)
                tiles_scalar(A.tiles)
                attention_scalar(A.at)
                meet(e, 0)
                router_scalar(B.router, -1.0)
                experts_scalar(B.experts)
                meet(e, 1)
            if e is nc.vector:
                e.wait_ge(x_loaded, 16)
                norm_vector(0, X, False, XN, XT)
                tiles_vector(A.tiles)
                keys_vector(A.at)
                attention_vector(A.at, whole, ACC, X)
                meet(e, 0)
                group_router_vector(B.router, w)
                experts_vector(B.experts)
                down_vector(ACC)
                meet(e, 1)

        def plan3():
            w, end = views(3)
            A = Place()
            take = Taker(end)
            A.at = Attention(take, 16, 16, 16, True, "rel")
            A.stage = take(2 * 4 * (S + 1)).rearrange("p (g h s) -> p g h s", g=2, h=4)
            A.e = chunks(w["a_e"], 16)
            wq, wk, wv = chunks(w["a_q"], 2), chunks(w["a_k"], 2), chunks(w["a_v"], 2)
            col = lambda t: slice(t * P, (t + 1) * P)
            tiles = [(feature_tile(wq, XT, col(t)), A.at.q[:, t], {"mul": -1 / 4}, None) for t in range(2)]
            tiles += [(feature_tile(wk, XT, col(t)), A.at.keys_of(t), {"spread": A.at.mask}, None) for t in range(2)]
            tiles += [(token_tile(XT, wv, i, slice(0, D)), A.at.v[:, i], {}, None) for i in range(NI)]
            A.tiles = Tiles(tiles)
            A.wo = chunks(w["a_o"], 2)
            B = Place()
            take = Taker(end)
            B.router = Router(take, 8)
            B.h1 = take(S)
            B.tiles = Tiles([(feature_tile(chunks(w["w1"], 2), XT, slice(0, P)), B.h1, {"relu": 1, "col": w["b1"][:, 0:1]}, None)])
            B.xe = take(8 * NC * S).rearrange("p (e c s) -> p e c s", e=8, c=NC)
            B.select = chunks(w["select_b"], 8)
            B.ew = w["e_w"].rearrange("p (e c n) -> p e c n", e=8, c=NC)
            B.w = w
            return A, B

        def rel_tensor(A):
            at = A.at
            for r in range(16):
                i, h0 = r // 4, 4 * (r % 4)
                kw = at.keys(i)
                if r >= 1:
                    nc.tensor.wait_ge(rel_dve, 2 * r)
                    nc.tensor.wait_ge(rel_act, 2 * r)
                for h in range(4):
                    last = nc.tensor.matmul(bank(h)[:, 0:kw], at.qz[:, (h0 + h) // 8, i * P:(i + 1) * P],
                                            A.e[:, h0 + h, S - kw:S], start=True, stop=True)
                    last.then_inc(rel_ready, 1)

        def rel_vector(A):
            for r in range(16):
                kw = A.at.keys(r // 4)
                if r >= 2:
                    nc.vector.wait_ge(rel_stored, 16 * (r - 1))
                for h in (0, 2):
                    nc.vector.wait_ge(rel_ready, 4 * r + h + 1)
                    nc.vector.tensor_copy(A.stage[:, r % 2, h, 1:kw + 1], bank(h)[:, 0:kw]).then_inc(rel_dve, 1)

        def rel_scalar(A):
            for r in range(16):
                kw = A.at.keys(r // 4)
                if r >= 2:
                    nc.scalar.wait_ge(rel_stored, 16 * (r - 1))
                for h in (1, 3):
                    nc.scalar.wait_ge(rel_ready, 4 * r + h + 1)
                    nc.scalar.activation(A.stage[:, r % 2, h, 1:kw + 1], bank(h)[:, 0:kw], ACT.Copy).then_inc(rel_act, 1)

        def rel_sync(A):
            def load(r):
                kw = A.at.keys(r // 4)
                skewed = bass.AP(tensor=rel_mid.tensor, offset=r * REL + P + 1,
                                 ap=[[kw, P], [P * (kw + 1), 4], [1, kw]])
                nc.sync.dma_start(A.at.rel[:, r % 4, :, 0:kw], skewed).then_inc(rel_loaded[r % 4], 16)

            for r in range(16):
                kw = A.at.keys(r // 4)
                nc.sync.wait_ge(rel_dve, 2 * (r + 1))
                nc.sync.wait_ge(rel_act, 2 * (r + 1))
                nc.sync.dma_start(rel_mid[r, 0:4 * P * (kw + 1)].rearrange("(h p s) -> p h s", h=4, p=P),
                                  A.stage[:, r % 2, :, 0:kw + 1]).then_inc(rel_stored, 16)
                nc.sync.wait_ge(rel_stored, 16 * (r + 1))
                if r < 4:
                    load(r)
            for r in range(4, 16):
                nc.sync.wait_ge(max_ready, 2 * (r - 4) + 2)
                load(r)
            for k in range(4):
                nc.sync.wait_ge(rel_loaded[k], 64)

        def pick_tensor(B):
            for j in range(8):
                if j == 0:
                    comb_tensor(B.router, 8)
                if j >= 2:
                    nc.tensor.wait_ge(hidden_ready, j - 1)
                nc.tensor.matmul(bank(4 + j % 2), B.select[0:96, j], B.router.parts[0:96], start=True, stop=True
                                 ).then_inc(gate_ready, 1)
            nc.tensor.wait_ge(hidden_ready, 8)
            for i in range(NI):
                blk = slice(i * P, (i + 1) * P)
                if i >= 2:
                    nc.tensor.wait_ge(down_done, i - 1)
                o = bank(6 + i % 2)[:, 0:D]
                nc.tensor.matmul(o, B.router.combt[0:8, blk], B.w["e_b"][0:8, :], start=True, stop=False)
                for j in range(8):
                    for c in range(NC):
                        last = nc.tensor.matmul(o, B.xe[:, j, c, blk], B.ew[:, j, c], start=False,
                                                stop=j == 7 and c == NC - 1)
                last.then_inc(down_ready, 1)

        def pick_vector(B):
            for j in range(8):
                nc.vector.wait_ge(gate_ready, j + 1)
                nc.vector.tensor_tensor(B.xe[:, j], XT, bank(4 + j % 2).rearrange("p (o s) -> p o s", o=1)
                                        .to_broadcast([P, NC, S]), ALU.mult).then_inc(hidden_ready, 1)

        def block3(e, b, A, B, src, dst):
            w = B.w
            if e is nc.sync:
                load_x(b, src)
                rel_sync(A)
                meet(e, 0)
                store_x(b, dst, down_done, NI, X)
                meet(e, 1)
            if e is nc.gpsimd:
                meet(e, 0)
                meet(e, 1)
            if e is nc.tensor:
                norm_tensor(0, XN)
                turned_there(e, 0)
                tiles_tensor(A.tiles)
                tiles_there(e, A.tiles)
                rel_tensor(A)
                e.wait_ge(rel_dve, 32)
                e.wait_ge(rel_act, 32)
                attention_tensor(A.at, A.wo, whole, w["a_ob"])
                meet(e, 0)
                tiles_tensor(B.tiles)
                tiles_there(e, B.tiles)
                router_tensor(B.router, chunks(B.h1, 1), chunks(w["w2"], 1), w["b2"], 8)
                pick_tensor(B)
                meet(e, 1)
            if e is nc.scalar:
                norm_scalar(0, XT)
                tiles_scalar(A.tiles)
                rel_scalar(A)
                attention_scalar(A.at)
                meet(e, 0)
                tiles_scalar(B.tiles)
                router_scalar(B.router, 1.0)
                meet(e, 1)
            if e is nc.vector:
                e.wait_ge(x_loaded, 16)
                nc.vector.memset(A.at.qz[:, :, 0:1], 0.0)
                nc.vector.memset(A.stage[:, :, :, 0:1], 0.0)
                norm_vector(0, X, False, XN, XT)
                tiles_vector(A.tiles)
                rel_vector(A)
                attention_vector(A.at, whole, ACC, X)
                meet(e, 0)
                tiles_vector(B.tiles)
                softmax_router_vector(B.router, 8, 1, False, w["tri"])
                pick_vector(B)
                down_vector(ACC)
                meet(e, 1)

        plans = {n: (plan0, plan1, plan2, plan3)[n]() for n in blocks}
        bodies = {0: block0, 1: block1, 2: block2, 3: block3}

        block = ctx.enter_context(nc.Block())

        def run(e):
            for n, which in enumerate(blocks):
                e.wait_ge(weights_loaded, 64 * (n + 1))
                if e is nc.vector:
                    w = views(which)[0]
                    last = nc.vector.memset(zero[:, :], 0.0)
                    if "select" in w:
                        last = nc.vector.tensor_copy(w["select_b"], w["select"])
                    last.then_inc(select_made, 1)
                elif e is nc.tensor:
                    e.wait_ge(select_made, n + 1)
                src = x_in if n == 0 else x_mid
                dst = out if n == len(blocks) - 1 else x_mid
                with e.Fori(0, batches) as b:
                    bodies[which](e, b, *plans[which], src, dst)

        @block.sync
        def _(sp):
            sp.dma_start(const[:, :], consts).then_inc(constants_loaded, 16)
            sp.wait_ge(constants_made, 1)
            for i in range(NI):
                end = 4 * P * ((i + 1) * P + 1)
                sp.dma_start(rel_mid[4 * i:4 * i + 4, end:end + 16], zero[0:4, :]).then_inc(zeros_stored, 16)
            sp.wait_ge(zeros_stored, 16 * NI)
            for n, which in enumerate(blocks):
                total = sum(s for _, s in sizes[which])
                cut = [total * k // 4 for k in range(5)]
                for k in range(4):
                    sp.dma_start(arena[:, cut[k]:cut[k + 1]], packs[which][:, cut[k]:cut[k + 1]]).then_inc(weights_loaded, 16)
                sp.wait_ge(weights_loaded, 64 * (n + 1))
                src = x_in if n == 0 else x_mid
                dst = out if n == len(blocks) - 1 else x_mid
                with sp.Fori(0, batches) as b:
                    bodies[which](sp, b, *plans[which], src, dst)

        @block.tensor
        def _(pe):
            pe.wait_ge(constants_loaded, 16)
            pe.wait_ge(constants_made, 1)
            run(pe)

        @block.vector
        def _(dve):
            dve.wait_ge(constants_loaded, 16)
            nc.vector.memset(ones[:, :], 1.0)
            nc.vector.memset(zero[:, :], 0.0)
            nc.vector.tensor_copy(constb[:, :], const[:, :]).then_inc(constants_made, 1)
            run(dve)

        @block.scalar
        def _(act):
            run(act)

        @block.gpsimd
        def _(pool):
            run(pool)


def kernel(**inputs):
    import concourse.bacc as bacc
    from concourse.bass_utils import run_bass_kernel_spmd

    blocks = (0, 1, 2, 3)
    x = np.ascontiguousarray(inputs["L0_attn_x"])
    batches = x.shape[0]
    arrays = {"x_in": x.reshape(batches * S, D), "consts": pack_constants()}
    sizes = {}
    for n in blocks:
        parts = pack_block(n, inputs)
        sizes[n] = [(name, w.shape[1]) for name, w in parts]
        arrays[f"pack{n}"] = np.ascontiguousarray(np.concatenate([w for _, w in parts], 1))
    nc = bacc.Bacc("TRN2", target_bir_lowering=False, num_devices=1)
    aps = {k: nc.dram_tensor(k, list(w.shape), F32, kind="ExternalInput").ap() for k, w in arrays.items()}
    out = nc.dram_tensor("out", [batches * S, D], F32, kind="ExternalOutput").ap()
    build(nc, aps["x_in"], aps["consts"], {n: aps[f"pack{n}"] for n in blocks}, sizes, out, blocks, batches)
    got = run_bass_kernel_spmd(nc, [arrays], core_ids=[0]).results[0]["out"]
    return got.reshape(batches, S, D)
```

```python
from contextlib import ExitStack

import numpy as np

import concourse.bass as bass
from concourse import mybir

F32 = mybir.dt.float32
BF16 = mybir.dt.bfloat16
ALU = mybir.AluOpType
ACT = mybir.ActivationFunctionType
AX = mybir.AxisListType.X

P = 128
S = 512
D = 256
NI = S // P
NC = D // P
BIG = 1.0e30
LOWEST = 3.0e38
EPS = 1e-5
ED, NS, DTR, KC, NL = 512, 16, 64, 4, 2
NT = ED // P
NH = NT // 2
STEPS = 2 * NS
REL = 4 * P * (S + 1) + 16
NCONST = 2 * P + 32 + 8 + 4 + 2
LATE = ("cos", "f_q", "e_g", "e_w")
ARENA = 48000


def _rows(w):
    w = np.asarray(w)
    k, n = w.shape
    c = -(-k // P)
    out = np.zeros((c * P, n), np.float32)
    out[:k] = w
    return out.reshape(c, P, n).transpose(1, 0, 2).reshape(P, c * n)


def _wide(w):
    return np.pad(np.asarray(w, np.float32), ((0, 0), (0, P - w.shape[1])))


def _spread(w, heads, slot):
    w = np.asarray(w)
    out = np.zeros((w.shape[0], heads, slot), np.float32)
    out[:, :, : w.shape[1] // heads] = w.reshape(w.shape[0], heads, -1)
    return out.reshape(w.shape[0], heads * slot)


def _col(v):
    return np.asarray(v, np.float32).reshape(-1, P).T


def _row(v):
    out = np.zeros((P, np.asarray(v).size), np.float32)
    out[0] = np.asarray(v).reshape(-1)
    return out


def _tri(n):
    t = np.tril(np.ones((n, n), np.float32), -1)
    return np.broadcast_to(t.reshape(1, -1), (P, n * n))


def _select(e, tiles):
    per = e // tiles
    out = np.zeros((P, tiles * P), np.float32)
    for r in range(e):
        for part in range(3):
            out[32 * part + r, r * P // per:(r + 1) * P // per] = 1
    return out


def pack_block(block, a):
    g = lambda name: np.asarray(a[name])
    t = np.arange(S, dtype=np.float32)
    out = []
    add = lambda name, w: out.append((name, np.asarray(w, np.float32)))
    if block == 0:
        decay = np.exp(np.float32(-0.01) * np.abs(t[:, None] - t[None, :])).astype(np.float32)
        add("a_q", _rows(g("L0_attn_W_q")))
        add("a_k", _rows(g("L0_attn_W_k")))
        add("a_v", _rows(g("L0_attn_W_v")))
        add("a_down", _rows(_wide(g("L0_attn_W_down_kv"))))
        add("a_upk", _rows(g("L0_attn_W_up_k")))
        add("a_upv", _rows(g("L0_attn_W_up_v")))
        add("a_o", _rows(g("L0_attn_W_o")))
        add("decay", _rows(decay))
        add("ln1", _col(g("L0_ffn_w_ln1")))
        add("select", _select(8, 8))
        freqs = (1.0 / np.float32(100000.0) ** (np.arange(0, 32, 2, dtype=np.float32) / 32)).astype(np.float32)
        ang = np.outer(t, freqs).astype(np.float32)
        cos, sin = np.ones((64, S), np.float32), np.zeros((64, S), np.float32)
        cos[32::2] = cos[33::2] = np.cos(ang).T
        sin[32::2], sin[33::2] = -np.sin(ang).T, np.sin(ang).T
        swap = np.zeros((P, P), np.float32)
        swap[np.arange(P), np.arange(P) ^ 1] = 1
        add("cos", np.tile(cos, (2, 1)))
        add("sin", np.tile(sin, (2, 1)))
        add("swap", swap)
        add("f_q", _rows(g("L0_ffn_Wq")))
        add("f_kva", _rows(_wide(g("L0_ffn_Wkva"))))
        k2 = np.zeros((64, 16, 64), np.float32)
        k2[:32, :, :32] = g("L0_ffn_Wkvb").reshape(32, 16, 32)
        k2[32 + np.arange(32), :, 32 + np.arange(32)] = 1
        add("f_k2", _rows(k2.reshape(64, 1024)))
        add("f_kvb", _rows(g("L0_ffn_Wkvb")))
        add("f_o", _rows(g("L0_ffn_Wo").reshape(16, 64, D)[:, :32].reshape(512, D)))
        add("ln2", _col(g("L0_ffn_w_ln2")))
        add("gate", _rows(g("L0_ffn_Wgate")))
        add("gate_b", _row(g("L0_ffn_expert_bias")))
        add("tri", _tri(8))
        for name, own, shared in (("e_g", "Wg", "sWg"), ("e_u", "Wu", "sWu"), ("e_d", "Wd", "sWd")):
            add(name, np.concatenate([_rows(w) for w in (*g("L0_ffn_" + shared), *g("L0_ffn_" + own))], 1))
    if block == 1:
        for i in range(NL):
            n = f"m{i}_"
            add(n + "in", _rows(g("L1_attn_in_proj_w")[i].T))
            add(n + "cw", g("L1_attn_conv_w")[i].reshape(NT, P, KC).transpose(1, 0, 2).reshape(P, -1))
            add(n + "cb", _col(g("L1_attn_conv_b")[i]))
            add(n + "x", _rows(_wide(g("L1_attn_x_proj_w")[i].T)))
            add(n + "dt", _rows(g("L1_attn_dt_w")[i].T))
            add(n + "dtb", _col(g("L1_attn_dt_b")[i]))
            add(n + "A", g("L1_attn_A_log")[i].reshape(NT, P, NS).transpose(1, 0, 2).reshape(P, -1))
            add(n + "D", _col(g("L1_attn_D_p")[i]))
            add(n + "out", _rows(g("L1_attn_out_proj_w")[i].T))
            add(n + "norm", _col(g("L1_attn_norm_w")[i]))
        for n in "qkvo":
            add("f_" + n, _rows(g(f"L1_ffn_{n}_w").T))
        for n in "qk":
            add(f"f_{n}b", _col(g(f"L1_ffn_{n}_b")))
        for n in "vo":
            add(f"f_{n}b", _row(g(f"L1_ffn_{n}_b")))
        add("norm_w", _col(g("L1_ffn_norm_w")))
        add("norm_b", _col(g("L1_ffn_norm_b")))
    if block == 2:
        for n in "qk":
            add("a_" + n, _rows(_spread(g("L2_attn_W" + n), 16, 32)))
        for n in "vo":
            add("a_" + n, _rows(g("L2_attn_W" + n)))
            add(f"a_{n}b", _row(g("L2_attn_b" + n)))
        qb = _spread(g("L2_attn_bq").reshape(1, D), 16, 32).reshape(16, 32)
        qb[:, 16] = 4
        add("a_qb", _col(qb.reshape(-1)))
        add("a_kb", _col(_spread(g("L2_attn_bk").reshape(1, D), 16, 32).reshape(-1)))
        slopes = np.float32([2.0 ** (-0.5 * (h + 1)) for h in range(16)])
        alibi = np.zeros((16, 32, S), np.float32)
        alibi[:, 16] = -slopes[:, None] * (np.float32(S - 1) - t)[None, :]
        add("alibi", _rows(alibi.reshape(512, S)))
        add("gate", _rows(g("L2_ffn_router_w").T))
        add("bias", np.broadcast_to(g("L2_ffn_correction_bias").reshape(1, 16), (P, 16)))
        add("tri4", _tri(4))
        add("tri16", _tri(16))
        add("select", _select(16, 8))
        for name, own, shared in (("e_g", "gate_w", "shared_gate_w"), ("e_u", "up_w", "shared_up_w")):
            two = g("L2_ffn_" + own).reshape(8, 2, D, 64).transpose(0, 2, 1, 3).reshape(8, D, P)
            four = g("L2_ffn_" + shared).T.reshape(D, 4, P).transpose(1, 0, 2)
            add(name, np.concatenate([_rows(w) for w in (*four, *two)], 1))
        down = (*g("L2_ffn_shared_down_w").T.reshape(4, P, D), *g("L2_ffn_down_w").reshape(8, P, D))
        add("e_d", np.concatenate([_rows(w) for w in down], 1))
    if block == 3:
        for n in "qk":
            add("a_" + n, _rows(g("L3_attn_W" + n).T))
        add("a_v", _rows(g("L3_attn_Wv").T))
        add("a_o", _rows(g("L3_attn_Wp").T))
        add("a_ob", _row(g("L3_attn_bp")))
        e = np.zeros((P, 16, S), np.float32)
        for h in range(16):
            e[16 * (h % 8):16 * (h % 8) + 16, h] = g("L3_attn_rel_embed")[:, 16 * h:16 * h + 16].T
        add("a_e", e.reshape(P, 16 * S))
        add("w1", _rows(g("L3_ffn_W1")))
        add("b1", _col(g("L3_ffn_b1")))
        add("w2", _rows(g("L3_ffn_W2")))
        add("b2", _row(g("L3_ffn_b2")))
        add("tri", _tri(8))
        add("select", _select(8, 8))
        add("e_w", np.concatenate([_rows(w) for w in g("L3_ffn_expert_W")], 1))
        add("e_b", _rows(g("L3_ffn_expert_b")))
    return out


def pack_constants():
    upper = np.triu(np.full((P, P), BIG, np.float32), 1)
    three = np.zeros((P, 32), np.float32)
    three[:96] = np.tile(np.eye(32, dtype=np.float32), (3, 1))
    slots = [np.repeat(np.eye(P // n, dtype=np.float32), n, 0) for n in (16, 32, 64)]
    return np.concatenate([np.eye(P, dtype=np.float32), upper, three, *slots], 1)


def build(nc, x_in, consts, packs, sizes, out, blocks, batches):
    ctx = ExitStack()
    with ctx:
        sb = lambda name, n, dt=F32: ctx.enter_context(nc.sbuf_tensor(name, [P, n], dt))
        arena = sb("arena", ARENA)
        X3, XN3, XT3, ACC3 = (sb(n, NI * D) for n in ("x_sb", "xn_sb", "xt_sb", "acc_sb"))
        X, XN, ACC = (w[:, :].rearrange("p (i d) -> p i d", i=NI) for w in (X3, XN3, ACC3))
        XT = XT3[:, :].rearrange("p (c s) -> p c s", c=NC)
        const = sb("const", NCONST)
        ident, upper = const[:, 0:P], const[:, P:2 * P]
        constb = sb("constb", NCONST, BF16)
        identb, upperb, three = constb[:, 0:P], constb[:, P:2 * P], constb[0:96, 2 * P:2 * P + 32]
        slots = {16: const[:, 288:296], 32: const[:, 296:300], 64: const[:, 300:302]}
        ones = sb("ones", P)
        zero = sb("zero", 16)
        small = sb("small", 64)
        psum = ctx.enter_context(nc.psum_tensor("psum", [P, 8 * 512], F32))
        bank = lambda i, n=1: psum[:, i * 512:(i + n) * 512]
        x_mid = nc.dram_tensor("x_mid", [(batches + 1) * S, D], F32).ap()
        rel_mid = nc.dram_tensor("rel_mid", [16, REL], F32).ap()

        sem = lambda name: ctx.enter_context(nc.semaphore(name))
        constants_loaded = sem("constants_loaded")
        weights_loaded = sem("weights_loaded")
        late_loaded = sem("late_loaded")
        constants_made = sem("constants_made")
        zeros_stored = sem("zeros_stored")
        select_made = sem("select_made")
        go_even = sem("go_even")
        dve_step = sem("dve_step")
        act_step = sem("act_step")
        stats_ready = sem("stats_ready")
        rstd_ready = sem("rstd_ready")
        normed = sem("normed")
        turned = sem("turned")
        turned_dve = sem("turned_dve")
        turned_act = sem("turned_act")
        proj_ready = sem("proj_ready")
        proj_dve = sem("proj_dve")
        proj_act = sem("proj_act")
        swapped = sem("swapped")
        cos_done = sem("cos_done")
        sin_done = sem("sin_done")
        roped = sem("roped")
        keys_ready = sem("keys_ready")
        scores_ready = sem("scores_ready")
        max_ready = sem("max_ready")
        exp_ready = sem("exp_ready")
        pt_ready = sem("pt_ready")
        pt_dve = sem("pt_dve")
        pt_act = sem("pt_act")
        o_ready = sem("o_ready")
        on_ready = sem("on_ready")
        rel_ready = sem("rel_ready")
        rel_dve = sem("rel_dve")
        rel_act = sem("rel_act")
        rel_stored = [sem(f"rel_stored{i}") for i in range(2)]
        rel_loaded = [sem(f"rel_loaded{i}") for i in range(4)]
        conv_ready = sem("conv_ready")
        u_ready = sem("u_ready")
        soft_log = sem("soft_log")
        delta_ready = sem("delta_ready")
        split_ready = sem("split_ready")
        b_ready = sem("b_ready")
        c_ready = sem("c_ready")
        c_copied = sem("c_copied")
        da_ready = sem("da_ready")
        dbx_done = sem("dbx_done")
        scan_done = sem("scan_done")
        hc_done = sem("hc_done")
        y_added = sem("y_added")
        y_taken = sem("y_taken")
        y_ready = sem("y_ready")
        logits_ready = sem("logits_ready")
        router_in = sem("router_in")
        router_exp = sem("router_exp")
        comb_ready = sem("comb_ready")
        comb_turned = sem("comb_turned")
        combt_ready = sem("combt_ready")
        gate_ready = sem("gate_ready")
        silu_ready = sem("silu_ready")
        hidden_ready = sem("hidden_ready")
        down_ready = sem("down_ready")
        down_done = sem("down_done")
        arrived = sem("arrived")
        go_odd = sem("go_odd")
        x_loaded = sem("x_loaded")
        x_stored = sem("x_stored")

        def meet(e, odd):
            if e is nc.sync:
                e.wait_ge(arrived, 4)
                e.sem_clear(range(go_even.num, go_odd.num) if odd else range(go_even.num + 1, x_stored.num + 1))
                e.drain().then_inc(go_odd if odd else go_even, 1)
            else:
                e.drain().then_inc(arrived, 1)
                e.wait_ge(go_odd if odd else go_even, 1)
                e.drain()
                if not odd:
                    e.wait_ge(late_loaded, 32 * late.blocks)
            v.count = a.count = 0

        class Late:
            blocks = 0

        late = Late()

        class Steps:

            def __init__(self, engine, semaphore):
                self.engine, self.semaphore, self.count = engine, semaphore, 0

            def step(self, instruction):
                instruction.then_inc(self.semaphore, 1)
                self.count += 1

            def settle(self):
                self.engine.wait_ge(self.semaphore, self.count)

        v = Steps(nc.vector, dve_step)
        a = Steps(nc.scalar, act_step)

        class Place:
            pass

        def views(block):
            w, at = {}, 0
            for name, n in sizes[block]:
                w[name] = arena[:, at:at + n]
                at += n
            if "select" in w:
                n = w["select"].shape[1] // 2
                w["select_b"] = arena[:, at:at + n].bitcast(BF16)
                at += n
            return w, at

        def chunks(ap, c):
            return ap.rearrange("p (c n) -> p c n", c=c)

        class Taker:
            def __init__(self, at):
                self.at = at

            def __call__(self, n):
                assert self.at + n <= ARENA, (self.at, n)
                self.at += n
                return arena[:, self.at - n:self.at]

        st = small[:, 0:24].rearrange("p (i s) -> p i s", i=NI)
        mv = small[:, 24:32].rearrange("p (i s) -> p i s", i=NI)
        msq, var, inv, rstd = (small[:, 32 + 4 * i:36 + 4 * i] for i in range(4))
        warm = small[:, 48:49]

        def norm_vector(k, src, rms, dst, dst_t, w=None, b=None):
            for i in range(NI):
                last = nc.vector.bn_stats(st[:, i], src[:, i])
            v.step(last)
            v.settle()
            for i in range(NI):
                last = nc.vector.bn_aggr(mv[:, i], st[:, i])
            v.step(last)
            v.settle()
            if rms:
                v.step(nc.vector.tensor_tensor(msq, mv[:, :, 0], mv[:, :, 0], ALU.mult))
                v.settle()
                v.step(nc.vector.scalar_tensor_tensor(out=var, in0=msq, scalar=EPS, in1=mv[:, :, 1],
                                                      op0=ALU.add, op1=ALU.add))
            else:
                v.step(nc.vector.tensor_scalar(var, mv[:, :, 1], EPS, None, ALU.add))
            v.settle()
            nc.vector.reciprocal(inv, var).then_inc(stats_ready, 1)
            nc.vector.wait_ge(rstd_ready, k + 1)
            for i in range(NI):
                if rms:
                    last = nc.vector.tensor_scalar(dst[:, i], src[:, i], rstd[:, i:i + 1], None, ALU.mult)
                else:
                    last = nc.vector.tensor_scalar(dst[:, i], src[:, i], mv[:, i, 0:1], rstd[:, i:i + 1],
                                                   ALU.subtract, ALU.mult)
            last.then_inc(normed, 1)
            nc.vector.wait_ge(turned, 2 * k + 1)
            if w is None:
                nc.vector.tensor_copy(dst_t[:, 0], bank(6)).then_inc(turned_dve, 1)
            elif b is None:
                nc.vector.tensor_scalar(dst_t[:, 0], bank(6), w[:, 0:1], None, ALU.mult).then_inc(turned_dve, 1)
            else:
                nc.vector.tensor_scalar(dst_t[:, 0], bank(6), w[:, 0:1], b[:, 0:1],
                                        ALU.mult, ALU.add).then_inc(turned_dve, 1)

        def norm_scalar(k, dst_t, w=None, b=None):
            a.step(nc.scalar.activation(warm, ident[:, 0:1], ACT.Sqrt))
            nc.scalar.wait_ge(stats_ready, k + 1)
            nc.scalar.activation(rstd, inv, ACT.Sqrt).then_inc(rstd_ready, 1)
            nc.scalar.wait_ge(turned, 2 * k + 2)
            if w is None:
                last = nc.scalar.activation(dst_t[:, 1], bank(7), ACT.Copy)
            elif b is None:
                last = nc.scalar.activation(dst_t[:, 1], bank(7), ACT.Copy, scale=w[:, 1:2])
            else:
                last = nc.scalar.activation(dst_t[:, 1], bank(7), ACT.Identity, scale=w[:, 1:2], bias=b[:, 1:2])
            last.then_inc(turned_act, 1)

        def norm_tensor(k, dst):
            nc.tensor.wait_ge(normed, k + 1)
            for c in range(NC):
                for i in range(NI):
                    last = nc.tensor.transpose(bank(6 + c)[:, i * P:(i + 1) * P], dst[:, i, c * P:(c + 1) * P], ident)
                last.then_inc(turned, 1)

        def turned_there(e, k):
            e.wait_ge(turned_dve, k + 1)
            e.wait_ge(turned_act, k + 1)

        class Tiles:

            def __init__(self, tiles, before=None):
                self.tiles, self.before = tiles, before
                self.first = before.end if before else (0, 0, 0)
                self.through = []
                self.on_act = []
                d, s = self.first[1], self.first[2]
                for n, (_, _, way, _) in enumerate(tiles):
                    on_act = bool({"relu", "silu", "tap"} & set(way)) or (n % 2 == 1 and not {"col", "plus"} & set(way))
                    self.on_act.append(on_act)
                    d, s = d + (not on_act), s + on_act
                    self.through.append((d, s))
                self.end = (self.first[0] + len(tiles), d, s)

        def tiles_there(e, t, n=-1):
            d, s = t.through[n]
            if d:
                e.wait_ge(proj_dve, d)
            if s:
                e.wait_ge(proj_act, s)

        def tiles_tensor(t, part=slice(None)):
            if t.before:
                tiles_there(nc.tensor, t.before)
            for n in range(len(t.tiles))[part]:
                pairs, dst, way, need = t.tiles[n]
                if need is not None:
                    tiles_there(nc.tensor, t, need)
                elif n >= 4:
                    tiles_there(nc.tensor, t, n - 4)
                o = bank(n % 4)[0:dst.shape[0], 0:dst.shape[-1]]
                for j, (lhs, rhs) in enumerate(pairs):
                    last = nc.tensor.matmul(o, lhs, rhs, start=j == 0, stop=j == len(pairs) - 1)
                last.then_inc(proj_ready, 1)

        def tiles_vector(t, part=slice(None)):
            for n in range(len(t.tiles))[part]:
                pairs, dst, way, need = t.tiles[n]
                if t.on_act[n]:
                    continue
                nc.vector.wait_ge(proj_ready, t.first[0] + n + 1)
                o = bank(n % 4)[0:dst.shape[0], 0:dst.shape[-1]]
                if "plus" in way:
                    last = nc.vector.scalar_tensor_tensor(out=dst, in0=o, scalar=way["col"], in1=way["plus"],
                                                          op0=ALU.add, op1=ALU.add)
                elif "col" in way:
                    last = nc.vector.tensor_scalar(dst, o, way["col"], way.get("mul", 1.0), ALU.add, ALU.mult)
                elif "spread" in way:
                    for h in range(dst.shape[1]):
                        last = nc.vector.tensor_scalar(dst[:, h], o, way["spread"][:, h:h + 1], None, ALU.mult)
                elif "mul" in way:
                    last = nc.vector.tensor_scalar(dst, o, way["mul"], None, ALU.mult)
                else:
                    last = nc.vector.tensor_copy(dst, o)
                last.then_inc(proj_dve, 1)

        def tiles_scalar(t, part=slice(None)):
            for n in range(len(t.tiles))[part]:
                pairs, dst, way, need = t.tiles[n]
                if not t.on_act[n]:
                    continue
                nc.scalar.wait_ge(proj_ready, t.first[0] + n + 1)
                o = bank(n % 4)[0:dst.shape[0], 0:dst.shape[-1]]
                if "silu" in way:
                    last = nc.scalar.activation(dst, o, ACT.Silu)
                elif "tap" in way:
                    nc.scalar.activation(dst, o, ACT.Copy)
                    second, factor, addend = way["tap"]
                    last = nc.scalar.activation(second, o, ACT.Identity, scale=factor, bias=addend)
                elif "relu" in way:
                    last = nc.scalar.activation(dst, o, ACT.Relu, bias=way["col"])
                elif "spread" in way:
                    for h in range(dst.shape[1]):
                        last = nc.scalar.activation(dst[:, h], o, ACT.Copy, scale=way["spread"][:, h:h + 1])
                else:
                    last = nc.scalar.activation(dst, o, ACT.Copy, scale=way.get("mul", 1.0))
                last.then_inc(proj_act, 1)

        def feature_tile(w, src, cols):
            return [(w[:, c, cols], src[:, c]) for c in range(w.shape[1])]

        def token_tile(src, w, i, cols):
            return [(src[:, c, i * P:(i + 1) * P], w[:, c, cols]) for c in range(w.shape[1])]

        def bias_row(row):
            return [(ones[:, :], row)]

        class Attention:
            def __init__(self, take, heads, slot, vwidth, causal, mode, decay=None, two_steps=False):
                self.heads, self.slot, self.vwidth = heads, slot, vwidth
                self.causal, self.mode, self.decay = causal, mode, decay
                start = take.at
                self.nt = heads * slot // P
                self.nch = heads * vwidth // P
                self.qz = chunks(take(self.nt * (S + 1)), self.nt)
                self.q = self.qz[:, :, 1:]
                self.per_tile = P // slot
                self.k = chunks(take(heads * S), heads)
                self.mask = slots[slot]
                self.ktile = chunks(take(self.nt * S), self.nt) if two_steps else None
                self.v = chunks(take(NI * heads * vwidth), NI)
                self.scratch = take.at
                self.p = take(4 * S).rearrange("p (g e s) -> p g e s", g=2, e=2)
                self.t = take(4 * S).rearrange("p (g e s) -> p g e s", g=2, e=2) if mode != "plain" else None
                self.pts = chunks(take(4 * S), 4)
                self.on = chunks(take(2 * heads * vwidth), 2)
                self.ot = chunks(take(self.nch * S), self.nch)
                self.sums = take(NI * heads)
                self.rsum = take(2 * heads)
                self.mx = take(4)
                self.nmx = take(4)
                self.rel = take(4 * 4 * S).rearrange("p (r h s) -> p r h s", r=4, h=4) if mode == "rel" else None
                self.size = take.at - start
                self.groups = [(i, h) for i in range(NI) for h in range(0, heads, 2)]
                self.per = heads // 2
                self.slots = []
                self.steps = len(self.groups) + 5
                for n in range(self.steps):
                    if 1 <= n <= len(self.groups):
                        self.slots += [("p", n - 1, 0), ("p", n - 1, 1)]
                    i = self.finishing(n, 3)
                    if i is not None:
                        self.slots.append(("o", i, 0))
                    i = self.finishing(n, 4)
                    if i is not None:
                        self.slots.append(("y", i, 0))
                self.reads = []
                d = s = 0
                for kind, _, e in self.slots:
                    on_act = kind == "p" and e == 1
                    d, s = d + (not on_act), s + on_act
                    self.reads.append((d, s, on_act))

            def keys(self, i):
                return (i + 1) * P if self.causal else S

            def keys_of(self, t):
                return self.k[:, t * self.per_tile:(t + 1) * self.per_tile]

            def finishing(self, n, lag):
                g = n - lag
                if 0 <= g < len(self.groups) and (g + 1) % self.per == 0:
                    return g // self.per
                return None

        def slot_read(at, s):
            d, c, on_act = at.reads[s]
            if on_act:
                nc.tensor.wait_ge(pt_act, c)
            else:
                nc.tensor.wait_ge(pt_dve, d)

        def attention_tensor(at, wo, width_of, bias):
            s = 0
            base = {}
            for n in range(at.steps):
                if n < len(at.groups):
                    i, h = at.groups[n]
                    kw = at.keys(i)
                    if n >= 2:
                        if at.mode == "plain":
                            nc.tensor.wait_ge(exp_ready, 2 * (n - 1))
                        else:
                            nc.tensor.wait_ge(max_ready, n - 1)
                    for e in range(2):
                        o = bank(2 * (n % 2) + e)
                        if at.ktile is not None and i == 0:
                            nc.tensor.wait_ge(keys_ready, h + e + 1)
                        last = nc.tensor.matmul(o[:, 0:kw], at.q[:, (h + e) // at.per_tile, i * P:(i + 1) * P],
                                                at.k[:, h + e, 0:kw], start=True, stop=not at.causal)
                        if at.causal:
                            last = nc.tensor.matmul(o[:, kw - P:kw], identb, upperb, start=False, stop=True)
                    last.then_inc(scores_ready, 1)
                if 1 <= n <= len(at.groups):
                    i, h = at.groups[n - 1]
                    for e in range(2):
                        nc.tensor.wait_ge(exp_ready, 2 * (n - 1) + e + 1)
                        if s >= 2:
                            slot_read(at, s - 2)
                        for kb in range(at.keys(i) // P):
                            last = nc.tensor.transpose(bank(4 + s % 2)[:, kb * P:(kb + 1) * P],
                                                       at.p[:, (n - 1) % 2, e, kb * P:(kb + 1) * P], ident)
                        last.then_inc(pt_ready, 1)
                        base[n - 1, e] = s
                        s += 1
                if 2 <= n <= len(at.groups) + 1:
                    i, h = at.groups[n - 2]
                    if h == 0 and i >= 2:
                        nc.tensor.wait_ge(on_ready, i - 1)
                    for e in range(2):
                        slot_read(at, base[n - 2, e])
                        vs = slice((h + e) * at.vwidth, (h + e + 1) * at.vwidth)
                        nk = at.keys(i) // P
                        for kb in range(nk):
                            last = nc.tensor.matmul(bank(6 + i % 2)[:, vs],
                                                    at.pts[:, (2 * (n - 2) + e) % 4, kb * P:(kb + 1) * P],
                                                    at.v[:, kb, vs], start=kb == 0, stop=kb == nk - 1)
                    if h + 2 == at.heads:
                        last.then_inc(o_ready, 1)
                i = at.finishing(n, 3)
                if i is not None:
                    nc.tensor.wait_ge(on_ready, i + 1)
                    slot_read(at, s - 2)
                    for c in range(at.nch):
                        last = nc.tensor.transpose(bank(4 + s % 2)[:, c * P:(c + 1) * P],
                                                   at.on[:, i % 2, c * P:(c + 1) * P], ident)
                    last.then_inc(pt_ready, 1)
                    base["o", i] = s
                    s += 1
                i = at.finishing(n, 4)
                if i is not None:
                    slot_read(at, base["o", i])
                    if s - 2 != base["o", i]:
                        slot_read(at, s - 2)
                    m = width_of(i)
                    o = bank(4 + s % 2)[:, 0:m]
                    if bias is not None:
                        nc.tensor.matmul(o, ones[:, :], bias[:, 0:m], start=True, stop=False)
                    full = m if m < D else at.nch * P
                    for c in range(-(-full // P)):
                        rows = min(P, full - c * P)
                        last = nc.tensor.matmul(o, at.ot[0:rows, c, i * P:(i + 1) * P], wo[0:rows, c, 0:m],
                                                start=bias is None and c == 0, stop=(c + 1) * P >= full)
                    last.then_inc(pt_ready, 1)
                    s += 1

        def key_scalar(at, h):
            e = h % at.per_tile
            nc.scalar.activation(at.k[:, h], at.ktile[:, h // at.per_tile], ACT.Copy, scale=at.mask[:, e:e + 1]
                                 ).then_inc(keys_ready, 1)

        def keys_scalar(at, tiles, t, last):
            nc.scalar.wait_ge(proj_dve, tiles.through[last][0])
            for h in range(t * at.per_tile, (t + 1) * at.per_tile):
                key_scalar(at, h)

        def attention_vector(at, width_of, add_to, base_of):
            s = 0
            for n in range(at.steps):
                if n < len(at.groups):
                    i, h = at.groups[n]
                    kw = at.keys(i)
                    g = n % 2
                    nc.vector.wait_ge(scores_ready, n + 1)
                    if n >= 2:
                        nc.vector.wait_ge(exp_ready, 2 * (n - 1))
                    if at.mode == "plain":
                        o = bank(2 * g, 2).rearrange("p (e s) -> p e s", e=2)[:, :, 0:kw]
                        nc.vector.tensor_reduce(at.nmx[:, 2 * g:2 * g + 2], o, AX, ALU.min).then_inc(max_ready, 1)
                    elif at.mode == "decay":
                        for e in range(2):
                            last = nc.vector.tensor_tensor_reduce(
                                at.t[:, g, e, 0:kw], bank(2 * g + e)[:, 0:kw], at.decay[:, i, 0:kw], 1.0, -LOWEST,
                                ALU.mult, ALU.max, at.mx[:, 2 * g + e:2 * g + e + 1])
                        v.step(last)
                        v.settle()
                        nc.vector.tensor_scalar(at.nmx[:, 2 * g:2 * g + 2], at.mx[:, 2 * g:2 * g + 2], -1.0, None,
                                                ALU.mult).then_inc(max_ready, 1)
                    else:
                        if h % 4 == 0:
                            r = i * 4 + h // 4
                            nc.vector.wait_ge(rel_loaded[r % 4], 16 * (r // 4 + 1))
                        for e in range(2):
                            last = nc.vector.tensor_tensor_reduce(
                                at.t[:, g, e, 0:kw], bank(2 * g + e)[:, 0:kw],
                                at.rel[:, (i * 4 + h // 4) % 4, h % 4 + e, 0:kw], 1.0, LOWEST,
                                ALU.add, ALU.min, at.nmx[:, 2 * g + e:2 * g + e + 1])
                        last.then_inc(max_ready, 1)
                while s < len(at.slots):
                    kind, j, e = at.slots[s]
                    at_step = j + 1 if kind == "p" else (j + 1) * at.per - 1 + (3 if kind == "o" else 4)
                    if at_step > n:
                        break
                    if kind == "p" and e == 0:
                        kw = at.keys(at.groups[j][0])
                        nc.vector.wait_ge(pt_ready, s + 1)
                        nc.vector.tensor_copy(at.pts[:, (2 * j) % 4, 0:kw], bank(4 + s % 2)[:, 0:kw]).then_inc(pt_dve, 1)
                    elif kind == "o":
                        nc.vector.wait_ge(pt_ready, s + 1)
                        nc.vector.tensor_copy(at.ot[:, :, j * P:(j + 1) * P],
                                              bank(4 + s % 2)[:, 0:at.nch * P].rearrange("p (c q) -> p c q", q=P)
                                              ).then_inc(pt_dve, 1)
                    elif kind == "y":
                        m = width_of(j)
                        nc.vector.wait_ge(pt_ready, s + 1)
                        nc.vector.tensor_tensor(add_to[:, j, 0:m], bank(4 + s % 2)[:, 0:m], base_of[:, j, 0:m],
                                                ALU.add).then_inc(pt_dve, 1)
                    s += 1
                i = at.finishing(n, 2)
                if i is not None:
                    nc.vector.wait_ge(exp_ready, 2 * (i + 1) * at.per)
                    rs = at.rsum[:, (i % 2) * at.heads:(i % 2 + 1) * at.heads]
                    v.step(nc.vector.reciprocal(rs, at.sums[:, i * at.heads:(i + 1) * at.heads]))
                    nc.vector.wait_ge(o_ready, i + 1)
                    v.settle()
                    nc.vector.tensor_tensor(
                        at.on[:, i % 2].rearrange("p (h d) -> p h d", h=at.heads),
                        bank(6 + i % 2)[:, 0:at.heads * at.vwidth].rearrange("p (h d) -> p h d", h=at.heads),
                        rs.rearrange("p (h o) -> p h o", o=1).to_broadcast([P, at.heads, at.vwidth]),
                        ALU.mult).then_inc(on_ready, 1)

        def attention_scalar(at):
            s = 0
            for n in range(at.steps):
                if n < len(at.groups):
                    i, h = at.groups[n]
                    kw = at.keys(i)
                    g = n % 2
                    nc.scalar.wait_ge(max_ready, n + 1)
                    if n >= 2:
                        k = [q for q, (kind, j, e) in enumerate(at.slots) if kind == "p" and j == n - 2][-1]
                        nc.scalar.wait_ge(pt_ready, k + 1)
                    for e in range(2):
                        src = bank(2 * g + e)[:, 0:kw] if at.mode == "plain" else at.t[:, g, e, 0:kw]
                        nc.scalar.activation(at.p[:, g, e, 0:kw], src, ACT.Exp,
                                             bias=at.nmx[:, 2 * g + e:2 * g + e + 1],
                                             scale=1.0 if at.mode == "decay" else -1.0,
                                             accum_out=at.sums[:, i * at.heads + h + e:i * at.heads + h + e + 1]
                                             ).then_inc(exp_ready, 1)
                for q, (kind, j, e) in enumerate(at.slots):
                    if kind == "p" and e == 1 and j == n - 1:
                        kw = at.keys(at.groups[j][0])
                        nc.scalar.wait_ge(pt_ready, q + 1)
                        nc.scalar.activation(at.pts[:, (2 * j + 1) % 4, 0:kw], bank(4 + q % 2)[:, 0:kw],
                                             ACT.Copy).then_inc(pt_act, 1)

        def rank_vector(score, rank, groups, n, tri, work):
            gt, eq = (w[:, 0:groups * n * n].rearrange("p (g e r) -> p g e r", g=groups, e=n) for w in work)
            rival = score.rearrange("p g (o r) -> p g o r", o=1).to_broadcast([P, groups, n, n])
            own = score.rearrange("p g (e o) -> p g e o", o=1).to_broadcast([P, groups, n, n])
            low = tri.rearrange("p (o e r) -> p o e r", o=1, e=n).to_broadcast([P, groups, n, n])
            nc.vector.tensor_tensor(gt, rival, own, ALU.is_gt)
            v.step(nc.vector.tensor_tensor(eq, rival, own, ALU.is_equal))
            v.settle()
            v.step(nc.vector.tensor_tensor(eq, eq, low, ALU.mult))
            v.settle()
            v.step(nc.vector.tensor_tensor(gt, gt, eq, ALU.add))
            v.settle()
            v.step(nc.vector.tensor_reduce(rank, gt, AX, ALU.add))
            v.settle()

        def over(ap, shape):
            return ap.rearrange("p (g o) -> p g o", o=1).to_broadcast(shape)

        def softmax_router_vector(r, experts, keep, weigh, tri):
            e3 = [P, NI, experts]
            lg = bank(7)[:, 0:NI * experts].rearrange("p (i e) -> p i e", i=NI)
            nc.vector.wait_ge(logits_ready, 1)
            v.step(nc.vector.tensor_reduce(r.a4, lg, AX, ALU.max))
            v.settle()
            nc.vector.tensor_tensor(r.e, lg, over(r.a4, e3), ALU.subtract).then_inc(router_in, 1)
            nc.vector.wait_ge(router_exp, 1)
            v.step(nc.vector.tensor_reduce(r.a4, r.e, AX, ALU.add))
            v.settle()
            v.step(nc.vector.reciprocal(r.b4, r.a4))
            v.settle()
            v.step(nc.vector.tensor_tensor(r.e, r.e, over(r.b4, e3), ALU.mult))
            v.settle()
            rank_vector(r.e, r.rank, NI, experts, tri, r.work)
            if weigh:
                v.step(nc.vector.scalar_tensor_tensor(out=r.e, in0=r.rank, scalar=float(keep), in1=r.e,
                                                      op0=ALU.is_lt, op1=ALU.mult))
                v.settle()
                v.step(nc.vector.tensor_reduce(r.a4, r.e, AX, ALU.add))
                v.settle()
                v.step(nc.vector.reciprocal(r.b4, r.a4))
                v.settle()
                nc.vector.tensor_tensor(r.comb, r.e, over(r.b4, e3), ALU.mult).then_inc(comb_ready, 1)
            else:
                nc.vector.tensor_scalar(r.comb, r.rank, float(keep), None, ALU.is_lt).then_inc(comb_ready, 1)

        def combt_vector(r, experts):
            nc.vector.memset(r.parts[0:96], 0.0)
            nc.vector.wait_ge(comb_turned, 1)
            v.step(nc.vector.tensor_copy(r.combt[0:experts], bank(6)[0:experts, 0:S]))
            v.settle()
            split_vector(r.combt[0:experts], experts, r.parts, (0, 32, 64), r.rest[0:experts],
                         r.second[0:experts]).then_inc(combt_ready, 1)

        def router_scalar(r, scale):
            nc.scalar.wait_ge(router_in, 1)
            nc.scalar.activation(r.e, r.e, ACT.Exp, scale=scale).then_inc(router_exp, 1)

        def router_tensor(r, src, gate, bias, experts):
            for i in range(NI):
                o = bank(7)[:, i * experts:(i + 1) * experts]
                if bias is not None:
                    nc.tensor.matmul(o, ones[:, :], bias[:, 0:experts], start=True, stop=False)
                nch = gate.shape[1]
                for c in range(nch):
                    last = nc.tensor.matmul(o, src[:, c, i * P:(i + 1) * P], gate[:, c, 0:experts],
                                            start=bias is None and c == 0, stop=c == nch - 1)
            last.then_inc(logits_ready, 1)

        def comb_tensor(r, experts):
            nc.tensor.wait_ge(comb_ready, 1)
            for i in range(NI):
                last = nc.tensor.transpose(bank(6)[0:experts, i * P:(i + 1) * P], r.comb[:, i], ident)
            last.then_inc(comb_turned, 1)

        class Router:
            def __init__(self, take, experts, keep=None):
                keep = keep or take
                t3 = lambda: chunks(take(NI * experts), NI)
                self.e, self.rank, self.comb, self.f, self.g = t3(), t3(), t3(), t3(), t3()
                self.work = [take(NI * experts * experts) for _ in range(2)]
                self.a4, self.b4 = take(4), take(4)
                self.gs, self.gr = take(16), take(16)
                self.rest, self.second = take(S), take(S // 2).bitcast(BF16)
                self.combt, self.parts = keep(S), keep(S // 2).bitcast(BF16)

        class Experts:
            def __init__(self, take, r, w, routed, shared, experts):
                self.r, self.shared, self.n, self.experts = r, shared, routed + shared, experts
                self.wg, self.wu = (w[k].rearrange("p (t c n) -> p t c n", t=self.n, c=NC) for k in ("e_g", "e_u"))
                self.wd = chunks(w["e_d"], self.n)
                self.select = w["select_b"].rearrange("p (t n) -> p t n", n=P)
                self.s = chunks(take(2 * S), 2)
                self.h = chunks(take(2 * S), 2)
                self.hw = chunks(take(self.n * S), self.n)

        def experts_tensor(x, src, routed_here):
            for j in range(x.n):
                b = 3 * (j % 2)
                if j >= 2:
                    nc.tensor.wait_ge(hidden_ready, j - 1)
                for k, w in enumerate((x.wg, x.wu)):
                    for c in range(NC):
                        last = nc.tensor.matmul(bank(b + k), w[:, j, c], src[:, c], start=c == 0, stop=c == NC - 1)
                if j == x.shared and routed_here:
                    comb_tensor(x.r, x.experts)
                    nc.tensor.wait_ge(combt_ready, 1)
                if j >= x.shared:
                    last = nc.tensor.matmul(bank(b + 2), x.select[0:96, j - x.shared], x.r.parts[0:96],
                                            start=True, stop=True)
                last.then_inc(gate_ready, 1)
            nc.tensor.wait_ge(hidden_ready, x.n)
            for i in range(NI):
                if i >= 2:
                    nc.tensor.wait_ge(down_done, i - 1)
                for j in range(x.n):
                    last = nc.tensor.matmul(bank(6 + i % 2)[:, 0:D], x.hw[:, j, i * P:(i + 1) * P], x.wd[:, j],
                                            start=j == 0, stop=j == x.n - 1)
                last.then_inc(down_ready, 1)

        def experts_scalar(x):
            for j in range(x.n):
                nc.scalar.wait_ge(gate_ready, j + 1)
                if j >= 2:
                    nc.scalar.wait_ge(hidden_ready, j - 1)
                nc.scalar.activation(x.s[:, j % 2], bank(3 * (j % 2)), ACT.Silu).then_inc(silu_ready, 1)

        def experts_vector(x, part=slice(None)):
            for j in range(x.n)[part]:
                b = 3 * (j % 2)
                nc.vector.wait_ge(silu_ready, j + 1)
                if j >= x.shared:
                    v.step(nc.vector.tensor_tensor(x.h[:, j % 2], x.s[:, j % 2], bank(b + 1), ALU.mult))
                    v.settle()
                    last = nc.vector.tensor_tensor(x.hw[:, j], x.h[:, j % 2], bank(b + 2), ALU.mult)
                else:
                    last = nc.vector.tensor_tensor(x.hw[:, j], x.s[:, j % 2], bank(b + 1), ALU.mult)
                last.then_inc(hidden_ready, 1)

        def down_vector(bank_of=lambda i: 6 + i % 2):
            for i in range(NI):
                nc.vector.wait_ge(down_ready, i + 1)
                nc.vector.tensor_tensor(ACC[:, i], bank(bank_of(i))[:, 0:D], ACC[:, i], ALU.add).then_inc(down_done, 1)

        def tokens(dram, b):
            return dram[bass.ds(b * S, S), :].rearrange("(i p) d -> p i d", p=P)

        def load_x(b, src):
            nc.sync.dma_start(X, tokens(src, b)).then_inc(x_loaded, 16)

        def last_x_stored():
            nc.sync.wait_ge(x_loaded, 16)
            nc.sync.wait_ge(x_stored, 16)

        def next_x_and_store(b, src, dst, ready, count):
            load_x(b + 1, src)
            nc.sync.wait_ge(ready, count)
            nc.sync.dma_start(tokens(dst, b), ACC).then_inc(x_stored, 16)

        whole = lambda i: D

        def plan0():
            w, end = views(0)
            A = Place()
            take = Taker(end)
            A.at = Attention(take, 16, 16, 16, False, "decay", chunks(w["decay"], NI))
            kv, lat = chunks(take(2 * S), 2), take(S)
            wq, wk, wv = chunks(w["a_q"], 2), chunks(w["a_k"], 2), chunks(w["a_v"], 2)
            down, upk, upv = chunks(w["a_down"], 2), w["a_upk"], w["a_upv"]
            col = lambda t: slice(t * P, (t + 1) * P)
            tiles = [(feature_tile(wk, XT, col(t)) + feature_tile(wv, XT, col(t)), kv[:, t], {}, None) for t in range(2)]
            tiles += [(feature_tile(wq, XT, col(t)), A.at.q[:, t], {"mul": 1 / 16}, None) for t in range(2)]
            tiles += [(feature_tile(down, kv, slice(0, P)), lat, {}, 1)]
            tiles += [([(upk[:, col(t)], lat)], A.at.keys_of(t), {"spread": A.at.mask}, 4) for t in range(2)]
            tiles += [([(lat[:, col(i)], upv)], A.at.v[:, i], {}, None) for i in range(NI)]
            A.tiles = Tiles([(p, d, y, n if n is None or k - 4 <= n else k - 4) for k, (p, d, y, n) in enumerate(tiles)])
            A.wo = chunks(w["a_o"], 2)

            B = Place()
            keep, work = take, Taker(A.at.scratch)
            take = Taker(end)
            B.at = Attention(take, 16, 64, 32, True, "plain")
            B.r0 = chunks(work(NI * D), NI)
            B.r0t = chunks(keep(NC * S), NC)
            B.r1 = chunks(take(NI * D), NI)
            B.r1t = chunks(take(NC * S), NC)
            B.lkr = take(S)
            B.sin = chunks(take(2 * S), 2)
            B.x2 = chunks(take(NI * D), NI)
            fq, kva, k2, kvb = chunks(w["f_q"], 2), chunks(w["f_kva"], 2), w["f_k2"], w["f_kvb"]
            tiles = [(feature_tile(kva, B.r0t, slice(0, P)), B.lkr, {}, None)]
            tiles += [(feature_tile(fq, B.r0t, col(t)), B.at.q[:, t], {"mul": -1 / 8}, None) for t in range(8)]
            B.first = Tiles(tiles)
            B.rope = [B.lkr] + [B.at.q[:, t] for t in range(8)]
            tiles = [([(k2[:, col(t)], B.lkr)], B.at.keys_of(t), {"spread": B.at.mask}, None) for t in range(8)]
            tiles += [([(B.lkr[:, col(i)], kvb)], B.at.v[:, i], {}, None) for i in range(NI)]
            B.second = Tiles(tiles, B.first)
            B.wo = chunks(w["f_o"], 4)
            take = Taker(end)
            B.router = Router(take, 8)
            B.experts = Experts(take, B.router, w, 8, 1, 8)
            assert take.at <= end + B.at.size
            B.w = w
            return A, B

        def rope_tensor(B):
            for n in range(len(B.rope) + 2):
                if n < len(B.rope):
                    tiles_tensor(B.first, slice(n, n + 1))
                if n >= 2:
                    m = n - 2
                    tiles_there(nc.tensor, B.first, m)
                    if m >= 2:
                        nc.tensor.wait_ge(sin_done, m - 1)
                    nc.tensor.matmul(bank(4 + m % 2), B.w["swap"], B.rope[m], start=True, stop=True
                                     ).then_inc(swapped, 1)

        def rope_gpsimd(B):
            for n, t in enumerate(B.rope):
                nc.gpsimd.wait_ge(swapped, n + 1)
                nc.gpsimd.tensor_tensor(t, t, B.w["cos"], ALU.mult).then_inc(cos_done, 1)

        def rope_vector(B):
            for n in range(len(B.rope) + 4):
                if n < len(B.rope):
                    tiles_vector(B.first, slice(n, n + 1))
                m = n - 3
                if 0 <= m < len(B.rope):
                    nc.vector.wait_ge(swapped, m + 1)
                    if m >= 2:
                        nc.vector.wait_ge(roped, m - 1)
                    nc.vector.tensor_tensor(B.sin[:, m % 2], bank(4 + m % 2), B.w["sin"], ALU.mult
                                            ).then_inc(sin_done, 1)
                if m >= 1:
                    nc.vector.wait_ge(cos_done, m)
                    nc.vector.wait_ge(sin_done, m)
                    t = B.rope[m - 1]
                    nc.vector.tensor_tensor(t, t, B.sin[:, (m - 1) % 2], ALU.add).then_inc(roped, 1)

        def block0(e, b, A, B, src, dst):
            w = B.w
            if e is nc.sync:
                last_x_stored()
                meet(e, 0)
                next_x_and_store(b, src, dst, down_done, NI)
                meet(e, 1)
            if e is nc.gpsimd:
                meet(e, 0)
                rope_gpsimd(B)
                meet(e, 1)
            if e is nc.tensor:
                norm_tensor(0, XN)
                turned_there(e, 0)
                tiles_tensor(A.tiles, slice(0, 5))
                norm_tensor(1, B.r0)
                tiles_tensor(A.tiles, slice(5, None))
                tiles_there(e, A.tiles)
                turned_there(e, 1)
                attention_tensor(A.at, A.wo, whole, None)
                meet(e, 0)
                rope_tensor(B)
                e.wait_ge(roped, 1)
                tiles_tensor(B.second)
                tiles_there(e, B.second)
                e.wait_ge(roped, 9)
                attention_tensor(B.at, B.wo, whole, None)
                norm_tensor(0, B.r1)
                turned_there(e, 0)
                router_tensor(B.router, B.r1t, chunks(w["gate"], 2), w["gate_b"], 8)
                experts_tensor(B.experts, B.r1t, True)
                meet(e, 1)
            if e is nc.scalar:
                norm_scalar(0, XT)
                tiles_scalar(A.tiles, slice(0, 4))
                norm_scalar(1, B.r0t, w["ln1"])
                tiles_scalar(A.tiles, slice(4, None))
                attention_scalar(A.at)
                meet(e, 0)
                tiles_scalar(B.first)
                tiles_scalar(B.second)
                attention_scalar(B.at)
                norm_scalar(0, B.r1t, w["ln2"])
                router_scalar(B.router, 1.0)
                experts_scalar(B.experts)
                meet(e, 1)
            if e is nc.vector:
                e.wait_ge(x_loaded, 16)
                norm_vector(0, X, False, XN, XT)
                tiles_vector(A.tiles, slice(0, 4))
                norm_vector(1, XN, True, B.r0, B.r0t, w["ln1"])
                tiles_vector(A.tiles, slice(4, None))
                e.wait_ge(x_stored, 16)
                attention_vector(A.at, whole, ACC, X)
                meet(e, 0)
                rope_vector(B)
                tiles_vector(B.second)
                attention_vector(B.at, whole, B.x2, XN)
                nc.vector.wait_ge(pt_dve, B.at.reads[-1][0])
                v.step(nc.vector.tensor_tensor(ACC, ACC, B.x2, ALU.add))
                norm_vector(0, B.x2, True, B.r1, B.r1t, w["ln2"])
                softmax_router_vector(B.router, 8, 2, True, w["tri"])
                experts_vector(B.experts, slice(0, B.experts.shared))
                combt_vector(B.router, 8)
                experts_vector(B.experts, slice(B.experts.shared, None))
                down_vector()
                meet(e, 1)

        class Scan:

            def __init__(self, take):
                four = lambda: chunks(take(NT * S), NT)
                ring = lambda n: take(n * NH * S).rearrange("p (g t s) -> p g t s", g=n, t=NH)
                self.h, self.r = chunks(take(NI * D), NI), chunks(take(NI * D), NI)
                self.rt = chunks(take(NC * S), NC)
                self.xi = chunks(take(NT * (S + 4)), NT)
                self.c, self.u, self.z, self.delta, self.du, self.soft = (four() for _ in range(6))
                self.dbc, self.rest, self.second = take(S), take(S), take(S // 2).bitcast(BF16)
                self.bc = take(S // 2).bitcast(BF16)
                self.dbx, self.hs, self.hc = ring(3), ring(3), ring(4)
                self.c_all = chunks(take(4 * S), 4)
                self.ae, self.aneg = take(NT * NS), take(NT * NS)

        def plan_scan(sc, w, i, before):
            L = Place()
            n = f"m{i}_"
            L.cw, L.cb, L.a_log, L.d, L.norm = (w[n + k] for k in ("cw", "cb", "A", "D", "norm"))
            L.out = chunks(w[n + "out"], NT)
            w_in, wx, wdt = chunks(w[n + "in"], NC), chunks(w[n + "x"], NT), w[n + "dt"]
            col = lambda t: slice(t * P, (t + 1) * P)
            tiles = []
            for t in range(NT):
                tap = L.cw[:, (t + 1) * KC - 1:(t + 1) * KC]
                tiles.append((feature_tile(w_in, sc.rt, col(t)), sc.xi[:, t, KC - 1:KC - 1 + S],
                              {"tap": (sc.c[:, t], tap, L.cb[:, t:t + 1])}, None))
            for t in range(NT):
                tiles.append((feature_tile(w_in, sc.rt, col(NT + t)), sc.z[:, t], {"silu": 1}, None))
            L.first = Tiles(tiles, before)
            tiles = [(feature_tile(wx, sc.u, slice(0, P)), sc.dbc, {}, None)]
            tiles += [([(wdt[:, col(t)], sc.dbc)], sc.c[:, t], {"col": w[n + "dtb"][:, t:t + 1]}, 0)
                      for t in range(NT)]
            L.second = Tiles(tiles, L.first)
            return L

        def one_hot(row):
            return three[:, row:row + 1].to_broadcast([96, P])

        def split_vector(x, rows, parts, at_rows, rest, second):
            first = parts[at_rows[0]:at_rows[0] + rows]
            v.step(nc.vector.tensor_copy(first, x))
            v.settle()
            v.step(nc.vector.tensor_tensor(rest, x, first, ALU.subtract))
            v.settle()
            v.step(nc.vector.tensor_copy(second, rest))
            v.settle()
            nc.vector.tensor_copy(parts[at_rows[1]:at_rows[1] + rows], second)
            return nc.vector.tensor_tensor(parts[at_rows[2]:at_rows[2] + rows], rest, second, ALU.subtract)

        def scan_tensor(sc, L, i):
            norm_tensor(i + 1, sc.r)
            turned_there(nc.tensor, i + 1)
            tiles_tensor(L.first)
            nc.tensor.wait_ge(u_ready, NT * (i + 1))
            tiles_tensor(L.second)
            tiles_there(nc.tensor, L.second)
            nc.tensor.wait_ge(split_ready, i + 1)
            at = STEPS * i
            for k in range(STEPS + 4):
                if k < STEPS:
                    if at + k >= 2:
                        nc.tensor.wait_ge(dbx_done, at + k - 1)
                    nc.tensor.matmul(bank(4 + k % 2), one_hot(k % NS), sc.bc[0:96],
                                     start=True, stop=True).then_inc(b_ready, 1)
                    if at + k >= 2:
                        nc.tensor.wait_ge(c_copied, at + k - 1)
                    nc.tensor.matmul(bank(6 + k % 2), one_hot(NS + k % NS), sc.bc[0:96],
                                     start=True, stop=True).then_inc(c_ready, 1)
                if k >= 4:
                    m = k - 4
                    if m == NS:
                        nc.tensor.wait_ge(y_taken, i + 1)
                    nc.tensor.wait_ge(hc_done, at + m + 1)
                    for t in range(NH):
                        last = nc.tensor.matmul(bank(t), ident, sc.hc[:, m % 4, t],
                                                start=m % NS == 0, stop=m % NS == NS - 1)
                    last.then_inc(y_added, 1)
            nc.tensor.wait_ge(y_ready, i + 1)
            for j in range(NI):
                if NI * i + j >= 2:
                    nc.tensor.wait_ge(down_done, NI * i + j - 1)
                for t in range(NT):
                    last = nc.tensor.matmul(bank(4 + j % 2)[:, 0:D], sc.c[:, t, j * P:(j + 1) * P], L.out[:, t],
                                            start=t == 0, stop=t == NT - 1)
                last.then_inc(down_ready, 1)

        def scan_scalar(sc, L, i):
            norm_scalar(i + 1, sc.rt, L.norm)
            tiles_scalar(L.first, slice(0, NT + 1))
            for t in range(NT):
                nc.scalar.wait_ge(conv_ready, NT * i + t + 1)
                nc.scalar.activation(sc.u[:, t], sc.c[:, t], ACT.Silu).then_inc(u_ready, 1)
                if t < NT - 1:
                    tiles_scalar(L.first, slice(NT + 1 + t, NT + 2 + t))
            a.step(nc.scalar.activation(sc.ae, L.a_log, ACT.Exp))
            a.settle()
            a.step(nc.scalar.activation(sc.aneg, sc.ae, ACT.Copy, scale=-1.0))
            for t in range(NT):
                tiles_there(nc.scalar, L.second, t + 1)
                a.step(nc.scalar.activation(sc.soft[:, t], sc.c[:, t], ACT.Abs))
                a.settle()
                a.step(nc.scalar.activation(sc.soft[:, t], sc.soft[:, t], ACT.Exp, scale=-1.0))
            for t in range(NT):
                a.settle()
                nc.scalar.activation(sc.soft[:, t], sc.soft[:, t], ACT.Ln, bias=1.0).then_inc(soft_log, 1)
            at = STEPS * i
            for k in range(STEPS):
                for e in range(NH):
                    t, n = k // NS * NH + e, k % NS
                    if n == 0:
                        nc.scalar.wait_ge(delta_ready, NT * i + t + 1)
                    if k >= 1:
                        nc.scalar.wait_ge(scan_done, NH * (at + k - 1) + e + 1)
                    nc.scalar.activation(bank(2 + e), sc.delta[:, t], ACT.Exp,
                                         scale=sc.aneg[:, t * NS + n:t * NS + n + 1]).then_inc(da_ready, 1)
                nc.scalar.wait_ge(c_ready, at + k + 1)
                if at + k >= 4:
                    nc.scalar.wait_ge(hc_done, at + k - 3)
                nc.scalar.activation(sc.c_all[:, k % 4], bank(6 + k % 2), ACT.Copy).then_inc(c_copied, 1)

        def scan_gpsimd(sc, i):
            at = STEPS * i
            for k in range(STEPS):
                nc.gpsimd.wait_ge(scan_done, NH * (at + k + 1))
                nc.gpsimd.wait_ge(c_copied, at + k + 1)
                if at + k >= 4:
                    nc.gpsimd.wait_ge(y_added, at + k - 3)
                nc.gpsimd.tensor_tensor(sc.hc[:, k % 4], sc.hs[:, k % 3],
                                        sc.c_all[:, k % 4].rearrange("p (o s) -> p o s", o=1).to_broadcast([P, NH, S]),
                                        ALU.mult).then_inc(hc_done, 1)

        def scan_vector(sc, L, i, h_in):
            norm_vector(i + 1, h_in, True, sc.r, sc.rt, L.norm)
            for t0 in range(0, NT, 2):
                for k in range(KC - 1):
                    for t in (t0, t0 + 1):
                        if k == 0:
                            nc.vector.wait_ge(proj_act, L.first.through[t][1])
                        last = nc.vector.scalar_tensor_tensor(
                            out=sc.c[:, t], in0=sc.xi[:, t, k:k + S], scalar=L.cw[:, t * KC + k:t * KC + k + 1],
                            in1=sc.c[:, t], op0=ALU.mult, op1=ALU.add)
                        if k == KC - 2:
                            last.then_inc(conv_ready, 1)
                    if k < KC - 2:
                        v.step(last)
                        v.settle()
            nc.vector.wait_ge(u_ready, NT * (i + 1))
            tiles_vector(L.second)
            nc.vector.wait_ge(proj_dve, L.second.through[0][0])
            if i:
                nc.vector.wait_ge(y_added, STEPS * i)
            bc = slice(DTR, DTR + 2 * NS)
            split_vector(sc.dbc[bc], 2 * NS, sc.bc, (64, 32, 0), sc.rest[bc], sc.second[bc]).then_inc(split_ready, 1)
            for t in range(NT + 1):
                if t < NT:
                    nc.vector.wait_ge(soft_log, NT * i + t + 1)
                    nc.vector.scalar_tensor_tensor(out=sc.delta[:, t], in0=sc.c[:, t], scalar=0.0, in1=sc.soft[:, t],
                                                   op0=ALU.max, op1=ALU.add).then_inc(delta_ready, 1)
                if t >= 1:
                    nc.vector.wait_ge(delta_ready, NT * i + t)
                    v.step(nc.vector.tensor_tensor(sc.du[:, t - 1], sc.delta[:, t - 1], sc.u[:, t - 1], ALU.mult))
            v.settle()
            at = STEPS * i

            def take_y(half):
                for e in range(NH):
                    t = half * NH + e
                    last = nc.vector.scalar_tensor_tensor(out=sc.c[:, t], in0=sc.u[:, t], scalar=L.d[:, t:t + 1],
                                                          in1=bank(e), op0=ALU.mult, op1=ALU.add)
                return last

            for k in range(STEPS + 1):
                if k < STEPS:
                    half = k // NS
                    nc.vector.wait_ge(b_ready, at + k + 1)
                    if at + k >= 3:
                        nc.vector.wait_ge(scan_done, NH * (at + k - 2))
                    nc.vector.tensor_tensor(sc.dbx[:, k % 3], sc.du[:, half * NH:(half + 1) * NH],
                                            bank(4 + k % 2).rearrange("p (o s) -> p o s", o=1).to_broadcast([P, NH, S]),
                                            ALU.mult).then_inc(dbx_done, 1)
                if k == NS + 4:
                    nc.vector.wait_ge(y_added, at + NS)
                    take_y(0).then_inc(y_taken, 1)
                if k >= 1:
                    m = k - 1
                    nc.vector.wait_ge(dbx_done, at + m + 1)
                    if at + m >= 3:
                        nc.vector.wait_ge(hc_done, at + m - 2)
                    for e in range(NH):
                        nc.vector.wait_ge(da_ready, NH * (at + m) + e + 1)
                        nc.vector.tensor_tensor_scan(sc.hs[:, m % 3, e], bank(2 + e), sc.dbx[:, m % 3, e],
                                                     0.0, ALU.mult, ALU.add).then_inc(scan_done, 1)
            nc.vector.wait_ge(y_added, at + STEPS)
            v.step(take_y(1))
            nc.vector.wait_ge(y_taken, i + 1)
            v.settle()
            nc.vector.tensor_tensor(sc.c, sc.c, sc.z, ALU.mult).then_inc(y_ready, 1)
            for j in range(NI):
                nc.vector.wait_ge(down_ready, NI * i + j + 1)
                nc.vector.tensor_tensor(sc.h[:, j], bank(4 + j % 2)[:, 0:D], h_in[:, j], ALU.add).then_inc(down_done, 1)
            nc.vector.wait_ge(down_done, NI * (i + 1))

        def plan1():
            w, end = views(1)
            A = Place()
            A.scan = Scan(Taker(end))
            A.layers = []
            for i in range(NL):
                A.layers.append(plan_scan(A.scan, w, i, A.layers[-1].second if A.layers else None))
            B = Place()
            take = Taker(end)
            B.at = Attention(take, 8, 32, 32, False, "plain", two_steps=True)
            B.l, B.lt = chunks(take(NI * D), NI), chunks(take(NC * S), NC)
            fq, fk, fv = (chunks(w["f_" + n], 2) for n in "qkv")
            def rows(i):
                return [(c, min(P, (D >> i) - c * P)) for c in range(-(-(D >> i) // P))]
            tiles = []
            for wt, dst, bias, mul in ((fk, B.at.ktile, w["f_kb"], 1.0), (fq, B.at.q, w["f_qb"], -1 / 16)):
                for t in range(2):
                    for i in range(NI):
                        blk = slice(i * P, (i + 1) * P)
                        tiles.append(([(wt[0:m, c, t * P:(t + 1) * P], B.lt[0:m, c, blk]) for c, m in rows(i)],
                                      dst[:, t, blk], {"col": bias[:, t:t + 1], "mul": mul}, None))
            for i in range(NI):
                blk = slice(i * P, (i + 1) * P)
                tiles.append((bias_row(w["f_vb"]) + [(B.lt[0:m, c, blk], fv[0:m, c, :]) for c, m in rows(i)],
                              B.at.v[:, i], {}, None))
            B.tiles = Tiles(tiles)
            B.wo = chunks(w["f_o"], 2)
            B.w = w
            return A, B

        def block1(e, b, A, B, src, dst):
            w = B.w
            narrow = lambda i: D >> i
            if e is nc.sync:
                last_x_stored()
                meet(e, 0)
                next_x_and_store(b, src, dst, pt_dve, B.at.reads[-1][0])
                meet(e, 1)
            if e is nc.gpsimd:
                for i in range(NL):
                    scan_gpsimd(A.scan, i)
                meet(e, 0)
                meet(e, 1)
            if e is nc.tensor:
                norm_tensor(0, XN)
                turned_there(e, 0)
                for i in range(NL):
                    scan_tensor(A.scan, A.layers[i], i)
                meet(e, 0)
                norm_tensor(0, B.l)
                turned_there(e, 0)
                tiles_tensor(B.tiles)
                tiles_there(e, B.tiles)
                attention_tensor(B.at, B.wo, narrow, w["f_ob"])
                meet(e, 1)
            if e is nc.scalar:
                norm_scalar(0, XT)
                for i in range(NL):
                    scan_scalar(A.scan, A.layers[i], i)
                meet(e, 0)
                norm_scalar(0, B.lt, w["norm_w"], w["norm_b"])
                for t in range(2):
                    keys_scalar(B.at, B.tiles, t, (t + 1) * NI - 1)
                tiles_scalar(B.tiles)
                attention_scalar(B.at)
                meet(e, 1)
            if e is nc.vector:
                e.wait_ge(x_loaded, 16)
                norm_vector(0, X, False, XN, XT)
                v.step(nc.vector.memset(A.scan.xi[:, :, 0:KC - 1], 0.0))
                v.settle()
                for i in range(NL):
                    scan_vector(A.scan, A.layers[i], i, XN if i == 0 else A.scan.h)
                e.wait_ge(x_stored, 16)
                v.step(nc.vector.tensor_tensor(ACC, X, A.scan.h, ALU.add))
                v.settle()
                v.step(nc.vector.tensor_tensor(ACC, ACC, XN, ALU.add))
                meet(e, 0)
                norm_vector(0, XN, False, B.l, B.lt, w["norm_w"], w["norm_b"])
                tiles_vector(B.tiles)
                attention_vector(B.at, narrow, ACC, ACC)
                meet(e, 1)

        def plan2():
            w, end = views(2)
            A = Place()
            take = Taker(end)
            A.at = Attention(take, 16, 32, 16, True, "plain", two_steps=True)
            wq, wk, wv = chunks(w["a_q"], 2), chunks(w["a_k"], 2), chunks(w["a_v"], 2)
            alibi = chunks(w["alibi"], 4)
            col = lambda t: slice(t * P, (t + 1) * P)
            tiles = []
            for t in range(4):
                tiles.append((feature_tile(wk, XT, col(t)), A.at.ktile[:, t],
                              {"col": w["a_kb"][:, t:t + 1], "plus": alibi[:, t]}, None))
            for t in range(4):
                tiles.append((feature_tile(wq, XT, col(t)), A.at.q[:, t],
                              {"col": w["a_qb"][:, t:t + 1], "mul": -1 / 4}, None))
                tiles.append((bias_row(w["a_vb"]) + token_tile(XT, wv, t, slice(0, D)), A.at.v[:, t], {}, None))
            A.tiles = Tiles(tiles)
            A.wo = chunks(w["a_o"], 2)
            B = Place()
            B.router = Router(Taker(A.at.scratch), 16, take)
            take = Taker(end)
            B.experts = Experts(take, B.router, w, 8, 4, 16)
            assert take.at <= A.at.scratch
            B.w = w
            return A, B

        def group_router_vector(r, w, others):
            """The best 2 of 4 groups by their best two biased scores, then the best 4 experts of them."""
            e3, g3 = [P, NI, 16], [P, 16, 4]
            by_group = lambda ap: ap.rearrange("p i (g e) -> p (i g) e", g=4)
            lg = bank(7)[:, 0:NI * 16].rearrange("p (i e) -> p i e", i=NI)
            nc.vector.wait_ge(logits_ready, 1)
            nc.vector.tensor_copy(r.e, lg).then_inc(router_in, 1)
            nc.vector.wait_ge(router_exp, 1)
            v.step(nc.vector.tensor_scalar(r.e, r.e, 1.0, None, ALU.add))
            v.settle()
            v.step(nc.vector.reciprocal(r.f, r.e))
            v.settle()
            bias = w["bias"].rearrange("p (o e) -> p o e", o=1).to_broadcast(e3)
            v.step(nc.vector.tensor_tensor(r.g, r.f, bias, ALU.add))
            v.settle()
            rank_vector(by_group(r.g), by_group(r.rank), 16, 4, w["tri4"], r.work)
            v.step(nc.vector.scalar_tensor_tensor(out=r.e, in0=r.rank, scalar=2.0, in1=r.g, op0=ALU.is_lt, op1=ALU.mult))
            v.settle()
            v.step(nc.vector.tensor_reduce(r.gs, by_group(r.e), AX, ALU.add))
            v.settle()
            others[0]()
            rank_vector(chunks(r.gs, NI), chunks(r.gr, NI), NI, 4, w["tri4"], r.work)
            v.step(nc.vector.tensor_scalar(r.gr, r.gr, 2.0, None, ALU.is_lt))
            v.settle()
            v.step(nc.vector.tensor_scalar(r.gs, r.gr, -1.0, LOWEST, ALU.add, ALU.mult))
            v.step(nc.vector.tensor_tensor(by_group(r.e), by_group(r.g), over(r.gr, g3), ALU.mult))
            v.settle()
            v.step(nc.vector.tensor_tensor(by_group(r.e), by_group(r.e), over(r.gs, g3), ALU.add))
            v.settle()
            others[1]()
            rank_vector(r.e, r.rank, NI, 16, w["tri16"], r.work)
            v.step(nc.vector.scalar_tensor_tensor(out=r.e, in0=r.rank, scalar=4.0, in1=r.f, op0=ALU.is_lt, op1=ALU.mult))
            v.settle()
            v.step(nc.vector.tensor_reduce(r.a4, r.e, AX, ALU.add))
            v.settle()
            v.step(nc.vector.tensor_scalar(r.a4, r.a4, 1e-20, None, ALU.add))
            v.settle()
            v.step(nc.vector.reciprocal(r.b4, r.a4))
            v.settle()
            nc.vector.tensor_tensor(r.comb, r.e, over(r.b4, e3), ALU.mult).then_inc(comb_ready, 1)

        def block2(e, b, A, B, src, dst):
            w = B.w
            if e is nc.sync:
                last_x_stored()
                meet(e, 0)
                next_x_and_store(b, src, dst, down_done, NI)
                meet(e, 1)
            if e is nc.gpsimd:
                meet(e, 0)
                meet(e, 1)
            if e is nc.tensor:
                norm_tensor(0, XN)
                turned_there(e, 0)
                router_tensor(B.router, XT, chunks(w["gate"], 2), None, 16)
                tiles_tensor(A.tiles, slice(0, 10))
                comb_tensor(B.router, 16)
                tiles_tensor(A.tiles, slice(10, None))
                tiles_there(e, A.tiles)
                attention_tensor(A.at, A.wo, whole, w["a_ob"])
                meet(e, 0)
                experts_tensor(B.experts, XT, False)
                meet(e, 1)
            if e is nc.scalar:
                norm_scalar(0, XT)
                router_scalar(B.router, -1.0)
                for t in range(4):
                    keys_scalar(A.at, A.tiles, t, t)
                    tiles_scalar(A.tiles, slice(4 + 2 * t, 6 + 2 * t))
                attention_scalar(A.at)
                meet(e, 0)
                experts_scalar(B.experts)
                meet(e, 1)
            if e is nc.vector:
                e.wait_ge(x_loaded, 16)
                norm_vector(0, X, False, XN, XT)
                group_router_vector(B.router, w, [lambda: tiles_vector(A.tiles, slice(0, 2)),
                                                  lambda: tiles_vector(A.tiles, slice(2, 4))])
                tiles_vector(A.tiles, slice(4, 10))
                combt_vector(B.router, 16)
                tiles_vector(A.tiles, slice(10, None))
                e.wait_ge(x_stored, 16)
                attention_vector(A.at, whole, ACC, X)
                meet(e, 0)
                experts_vector(B.experts)
                down_vector()
                meet(e, 1)

        def plan3():
            w, end = views(3)
            A = Place()
            take = Taker(end)
            A.at = Attention(take, 16, 16, 16, True, "rel")
            A.stage = take(2 * 4 * (S + 1)).rearrange("p (g h s) -> p g h s", g=2, h=4)
            A.e = chunks(w["a_e"], 16)
            wq, wk, wv = chunks(w["a_q"], 2), chunks(w["a_k"], 2), chunks(w["a_v"], 2)
            col = lambda t: slice(t * P, (t + 1) * P)
            tiles = [(feature_tile(wq, XT, col(t)), A.at.q[:, t], {"mul": -1 / 4}, None) for t in range(2)]
            work, keep = Taker(A.at.scratch), take
            A.at.ktile = chunks(work(2 * S), 2)
            tiles += [(feature_tile(wk, XT, col(t)), A.at.ktile[:, t], {}, None) for t in range(2)]
            tiles += [(token_tile(XT, wv, i, slice(0, D)), A.at.v[:, i], {}, None) for i in range(NI)]
            A.wo = chunks(w["a_o"], 2)
            B = Place()
            B.router = Router(work, 8, keep)
            B.h1 = work(S)
            hidden = (feature_tile(chunks(w["w1"], 2), XT, slice(0, P)), B.h1, {"relu": 1, "col": w["b1"][:, 0:1]}, None)
            A.tiles = Tiles([hidden] + tiles)
            take = Taker(end)
            B.xe = take(8 * NC * S).rearrange("p (e c s) -> p e c s", e=8, c=NC)
            B.select = chunks(w["select_b"], 8)
            B.ew = w["e_w"].rearrange("p (e c n) -> p e c n", e=8, c=NC)
            B.w = w
            return A, B

        def rel_tensor(A):
            at = A.at
            for r in range(16):
                i, h0 = r // 4, 4 * (r % 4)
                kw = at.keys(i)
                if r >= 2:
                    nc.tensor.wait_ge(rel_dve, 2 * (r - 1))
                    nc.tensor.wait_ge(rel_act, 2 * (r - 1))
                for h in range(4):
                    last = nc.tensor.matmul(bank(4 * (r % 2) + h)[:, 0:kw], at.qz[:, (h0 + h) // 8, i * P:(i + 1) * P],
                                            A.e[:, h0 + h, S - kw:S], start=True, stop=True)
                    last.then_inc(rel_ready, 1)

        def rel_vector(A):
            for r in range(16):
                kw = A.at.keys(r // 4)
                if r >= 2:
                    nc.vector.wait_ge(rel_stored[r % 2], 16 * (r // 2))
                for h in (0, 2):
                    nc.vector.wait_ge(rel_ready, 4 * r + h + 1)
                    nc.vector.tensor_copy(A.stage[:, r % 2, h, 1:kw + 1],
                                          bank(4 * (r % 2) + h)[:, 0:kw]).then_inc(rel_dve, 1)

        def rel_scalar(A):
            tiles_there(nc.scalar, A.tiles, 4)
            for r in range(16):
                key_scalar(A.at, r)
                kw = A.at.keys(r // 4)
                if r >= 2:
                    nc.scalar.wait_ge(rel_stored[r % 2], 16 * (r // 2))
                for h in (1, 3):
                    nc.scalar.wait_ge(rel_ready, 4 * r + h + 1)
                    nc.scalar.activation(A.stage[:, r % 2, h, 1:kw + 1],
                                         bank(4 * (r % 2) + h)[:, 0:kw], ACT.Copy).then_inc(rel_act, 1)

        def rel_sync(A):
            def load(r):
                kw = A.at.keys(r // 4)
                skewed = bass.AP(tensor=rel_mid.tensor, offset=r * REL + P + 1,
                                 ap=[[kw, P], [P * (kw + 1), 4], [1, kw]])
                nc.sync.dma_start(A.at.rel[:, r % 4, :, 0:kw], skewed).then_inc(rel_loaded[r % 4], 16)

            for r in range(17):
                if r < 16:
                    kw = A.at.keys(r // 4)
                    nc.sync.wait_ge(rel_dve, 2 * (r + 1))
                    nc.sync.wait_ge(rel_act, 2 * (r + 1))
                    nc.sync.dma_start(rel_mid[r, 0:4 * P * (kw + 1)].rearrange("(h p s) -> p h s", h=4, p=P),
                                      A.stage[:, r % 2, :, 0:kw + 1]).then_inc(rel_stored[r % 2], 16)
                if r >= 1:
                    nc.sync.wait_ge(rel_stored[(r - 1) % 2], 16 * ((r - 1) // 2 + 1))
                    if r <= 4:
                        load(r - 1)
            for r in range(4, 16):
                nc.sync.wait_ge(max_ready, 2 * (r - 4) + 2)
                load(r)
            for k in range(4):
                nc.sync.wait_ge(rel_loaded[k], 64)

        def pick_tensor(B):
            blk = lambda i: slice(i * P, (i + 1) * P)
            for i in range(NI):
                nc.tensor.matmul(bank(i)[:, 0:D], B.router.combt[0:8, blk(i)], B.w["e_b"][0:8, :],
                                 start=True, stop=False)
            for j in range(9):
                if j < 8:
                    if j >= 2:
                        nc.tensor.wait_ge(hidden_ready, j - 1)
                    nc.tensor.matmul(bank(4 + j % 2), B.select[0:96, j], B.router.parts[0:96], start=True, stop=True
                                     ).then_inc(gate_ready, 1)
                if j >= 1:
                    nc.tensor.wait_ge(hidden_ready, j)
                    for i in range(NI):
                        for c in range(NC):
                            last = nc.tensor.matmul(bank(i)[:, 0:D], B.xe[:, j - 1, c, blk(i)], B.ew[:, j - 1, c],
                                                    start=False, stop=j == 8 and c == NC - 1)
                        if j == 8:
                            last.then_inc(down_ready, 1)

        def pick_vector(B):
            for j in range(8):
                nc.vector.wait_ge(gate_ready, j + 1)
                nc.vector.tensor_tensor(B.xe[:, j], XT, bank(4 + j % 2).rearrange("p (o s) -> p o s", o=1)
                                        .to_broadcast([P, NC, S]), ALU.mult).then_inc(hidden_ready, 1)

        def block3(e, b, A, B, src, dst):
            w = B.w
            if e is nc.sync:
                rel_sync(A)
                last_x_stored()
                meet(e, 0)
                next_x_and_store(b, src, dst, down_done, NI)
                meet(e, 1)
            if e is nc.gpsimd:
                meet(e, 0)
                meet(e, 1)
            if e is nc.tensor:
                norm_tensor(0, XN)
                turned_there(e, 0)
                tiles_tensor(A.tiles, slice(0, 3))
                tiles_there(e, A.tiles, 0)
                router_tensor(B.router, chunks(B.h1, 1), chunks(w["w2"], 1), w["b2"], 8)
                tiles_tensor(A.tiles, slice(3, None))
                tiles_there(e, A.tiles)
                e.wait_ge(comb_ready, 1)
                rel_tensor(A)
                e.wait_ge(rel_dve, 32)
                e.wait_ge(rel_act, 32)
                comb_tensor(B.router, 8)
                attention_tensor(A.at, A.wo, whole, w["a_ob"])
                meet(e, 0)
                pick_tensor(B)
                meet(e, 1)
            if e is nc.scalar:
                norm_scalar(0, XT)
                tiles_scalar(A.tiles, slice(0, 4))
                router_scalar(B.router, 1.0)
                tiles_scalar(A.tiles, slice(4, None))
                rel_scalar(A)
                attention_scalar(A.at)
                meet(e, 0)
                meet(e, 1)
            if e is nc.vector:
                e.wait_ge(x_loaded, 16)
                nc.vector.memset(A.at.qz[:, :, 0:1], 0.0)
                nc.vector.memset(A.stage[:, :, :, 0:1], 0.0)
                norm_vector(0, X, False, XN, XT)
                tiles_vector(A.tiles, slice(0, 5))
                softmax_router_vector(B.router, 8, 1, False, w["tri"])
                tiles_vector(A.tiles, slice(5, None))
                rel_vector(A)
                combt_vector(B.router, 8)
                e.wait_ge(combt_ready, 1)
                e.wait_ge(x_stored, 16)
                attention_vector(A.at, whole, ACC, X)
                meet(e, 0)
                pick_vector(B)
                down_vector(lambda i: i)
                meet(e, 1)

        plans = {n: (plan0, plan1, plan2, plan3)[n]() for n in blocks}
        bodies = {0: block0, 1: block1, 2: block2, 3: block3}

        block = ctx.enter_context(nc.Block())

        def run(e):
            selections = 0
            for n, which in enumerate(blocks):
                e.wait_ge(weights_loaded, 32 * (n + 1))
                late.blocks = n + 1
                w = views(which)[0]
                if "select" in w:
                    selections += 1
                    if e is nc.vector:
                        nc.vector.tensor_copy(w["select_b"], w["select"]).then_inc(select_made, 1)
                    elif e is nc.tensor:
                        e.wait_ge(select_made, selections)
                src = x_in if n == 0 else x_mid
                dst = out if n == len(blocks) - 1 else x_mid
                with e.Fori(0, batches) as b:
                    bodies[which](e, b, *plans[which], src, dst)

        @block.sync
        def _(sp):
            sp.dma_start(const[:, :], consts).then_inc(constants_loaded, 16)
            sp.wait_ge(constants_made, 1)
            for i in range(NI):
                end = 4 * P * ((i + 1) * P + 1)
                sp.dma_start(rel_mid[4 * i:4 * i + 4, end:end + 16], zero[0:4, :]).then_inc(zeros_stored, 16)
            sp.wait_ge(zeros_stored, 16 * NI)
            end = batches * S
            sp.dma_start(x_mid[end:end + S, :], x_in[end:end + S, :]).then_inc(x_stored, 16)
            for n, which in enumerate(blocks):
                src = x_in if n == 0 else x_mid
                dst = out if n == len(blocks) - 1 else x_mid
                if n:
                    last_x_stored()
                    sp.sem_clear(range(x_loaded.num, x_loaded.num + 1))
                    sp.drain()
                load_x(0, src)
                total, early = sum(s for _, s in sizes[which]), 0
                for name, size in sizes[which]:
                    if name in LATE:
                        break
                    early += size
                cut = [0, early // 2, early, (early + total) // 2, total]
                for k in range(4):
                    sp.dma_start(arena[:, cut[k]:cut[k + 1]], packs[which][:, cut[k]:cut[k + 1]]
                                 ).then_inc(weights_loaded if k < 2 else late_loaded, 16)
                with sp.Fori(0, batches) as b:
                    bodies[which](sp, b, *plans[which], src, dst)
            last_x_stored()

        @block.tensor
        def _(pe):
            pe.wait_ge(constants_loaded, 16)
            pe.wait_ge(constants_made, 1)
            run(pe)

        @block.vector
        def _(dve):
            dve.wait_ge(constants_loaded, 16)
            nc.vector.memset(ones[:, :], 1.0)
            nc.vector.memset(zero[:, :], 0.0)
            nc.vector.tensor_copy(constb[:, :], const[:, :]).then_inc(constants_made, 1)
            run(dve)

        @block.scalar
        def _(act):
            act.wait_ge(constants_loaded, 16)
            run(act)

        @block.gpsimd
        def _(pool):
            run(pool)


def kernel(**inputs):
    import concourse.bacc as bacc
    from concourse.bass_utils import run_bass_kernel_spmd

    blocks = (0, 1, 2, 3)
    x = np.ascontiguousarray(inputs["L0_attn_x"])
    batches = x.shape[0]
    arrays = {"x_in": np.pad(x.reshape(batches * S, D), ((0, S), (0, 0))), "consts": pack_constants()}
    sizes = {}
    for n in blocks:
        parts = pack_block(n, inputs)
        sizes[n] = [(name, w.shape[1]) for name, w in parts]
        arrays[f"pack{n}"] = np.ascontiguousarray(np.concatenate([w for _, w in parts], 1))
    nc = bacc.Bacc("TRN2", target_bir_lowering=False, num_devices=1)
    aps = {k: nc.dram_tensor(k, list(w.shape), F32, kind="ExternalInput").ap() for k, w in arrays.items()}
    out = nc.dram_tensor("out", [batches * S, D], F32, kind="ExternalOutput").ap()
    build(nc, aps["x_in"], aps["consts"], {n: aps[f"pack{n}"] for n in blocks}, sizes, out, blocks, batches)
    got = run_bass_kernel_spmd(nc, [arrays], core_ids=[0]).results[0]["out"]
    return got.reshape(batches, S, D)
```
